# Optimizing a Trainium2 kernel written in Bass

```python
import numpy as np
import jax
import jax.numpy as jnp

def _softmax(x, axis=-1):
    return jax.nn.softmax(x, axis=axis)

def _gelu(x):
    return jax.nn.gelu(x, approximate=True)

def _silu(x):
    return jax.nn.silu(x)

def _sigmoid(x):
    return jax.nn.sigmoid(x)

def _layernorm(x, axis=-1, eps=1e-05):
    m = jnp.mean(x, axis=axis, keepdims=True)
    v = jnp.var(x, axis=axis, keepdims=True)
    return (x - m) / jnp.sqrt(v + eps)

def _scatter_add(tgt, idx, src, axis=0):
    return tgt.at[idx].add(src)

def _segment_sum(src, seg, n):
    return jax.ops.segment_sum(src, seg, n)
kernel_name = 'mk_decoder_preln_d2_seqx_r8_617a9c'

def setup_inputs(seed: int=0):
    np.random.seed(seed)
    _w = jnp.asarray

    def _rec_inputs():
        import jax
        import jax.numpy as jnp
        _rk = jax.random.key(seed)
        x = 7.22e-05 + 1 * jax.random.normal(jax.random.fold_in(_rk, 1), (8, 256, 128), jnp.float32)
        _lenS = 256 - jax.random.randint(jax.random.fold_in(_rk, 7), (8,), 0, max(1, 256 // 4) + 1, jnp.int32)
        _lenS2 = 256 - jax.random.randint(jax.random.fold_in(_rk, 8), (8,), 0, max(1, 256 // 4) + 1, jnp.int32)
        _ctx_1024P = jax.random.normal(jax.random.fold_in(_rk, 11), (8, 16, 128), jnp.float32)
        _ctx_1024c = jax.random.dirichlet(jax.random.fold_in(_rk, 511), 0.3 * jnp.ones((16,), jnp.float32), (8, 256))
        _ctx_1024t = jnp.einsum('bsk,bkd->bsd', _ctx_1024c, _ctx_1024P)
        _ctx_1024t = _ctx_1024t * jax.lax.rsqrt(jnp.mean(jnp.square(_ctx_1024t)) + 1e-12) * 0.953939
        ctx_1024 = 4.13588e-05 + 0.999923 * (_ctx_1024t + 0.3 * jax.random.normal(jax.random.fold_in(_rk, 611), (8, 256, 128), jnp.float32))
        _validS = jnp.arange(256)[None, :] < _lenS[:, None]
        _validS2 = jnp.arange(256)[None, :] < _lenS2[:, None]
        _causal = jnp.tril(jnp.ones((256, 256), dtype=bool))
        mask_SxS2_ik0 = jnp.where(jnp.broadcast_to(_validS2[0:1, :], (256, 256)), 0, 1).astype(jnp.int32)
        return (x, ctx_1024, mask_SxS2_ik0)
    x, ctx_1024, mask_SxS2_ik0 = _rec_inputs()

    def _L0_attn_setup():
        import jax, jax.numpy as jnp
        import numpy as np
        DT = 0.01
        DAMP_MIN = 0.0005
        BATCH, SEQ, D_IN, N_STATE = (16, 256, 128, 128)
        key = jax.random.key(seed)
        k1, k2, k3, k4, k5 = jax.random.split(key, 5)
        u = jax.random.normal(k1, (BATCH, SEQ, D_IN), jnp.float32)
        A_real = jnp.minimum(jax.random.normal(k2, (N_STATE,), jnp.float32) * 0.1 - DAMP_MIN, -DAMP_MIN)
        A_imag = jax.random.normal(k3, (N_STATE,), jnp.float32)
        B = jax.random.normal(k4, (N_STATE, D_IN), jnp.float32) * 0.02
        C = jax.random.normal(k5, (D_IN, N_STATE), jnp.float32) * 0.02
        return {'u': u, 'A_real': A_real, 'A_imag': A_imag, 'B': B, 'C': C}
    _L0_attn_all = _L0_attn_setup()
    _L0_attn_in = {k: v for k, v in _L0_attn_all.items() if k in ('A_real', 'A_imag', 'B', 'C')}
    del _L0_attn_all

    def _L0_xattn_setup():
        import jax, jax.numpy as jnp
        import numpy as np
        D_MODEL = 128
        NUM_HEADS = 16
        HEAD_DIM = D_MODEL // NUM_HEADS
        B, S = (4, 256)
        key = jax.random.key(seed)
        ks = jax.random.split(key, 11)
        scale = 1.0 / np.sqrt(D_MODEL)
        return {'query': jax.random.normal(ks[0], (B, S, D_MODEL), jnp.float32), 'key': jax.random.normal(ks[1], (B, S, D_MODEL), jnp.float32), 'value': jax.random.normal(ks[2], (B, S, D_MODEL), jnp.float32), 'Wq': jax.random.normal(ks[3], (D_MODEL, D_MODEL), jnp.float32) * scale, 'bq': jnp.zeros((D_MODEL,), jnp.float32), 'Wk': jax.random.normal(ks[4], (D_MODEL, D_MODEL), jnp.float32) * scale, 'bk': jnp.zeros((D_MODEL,), jnp.float32), 'Wv': jax.random.normal(ks[5], (D_MODEL, D_MODEL), jnp.float32) * scale, 'bv': jnp.zeros((D_MODEL,), jnp.float32), 'Wo': jax.random.normal(ks[6], (D_MODEL, D_MODEL), jnp.float32) * scale, 'bo': jnp.zeros((D_MODEL,), jnp.float32)}
    _L0_xattn_all = _L0_xattn_setup()
    _L0_xattn_in = {k: v for k, v in _L0_xattn_all.items() if k in ('Wq', 'bq', 'Wk', 'bk', 'Wv', 'bv', 'Wo', 'bo')}
    del _L0_xattn_all

    def _L0_ffn_setup():
        import jax, jax.numpy as jnp
        import numpy as np
        B, S, D, E = (4, 512, 128, 8)
        key = jax.random.key(seed)
        k1, k2, k3, k4, k5 = jax.random.split(key, 5)
        scale = 1.0 / np.sqrt(D)
        return {'x': jax.random.normal(k1, (B, S, D), dtype=jnp.float32), 'Wg': jax.random.normal(k2, (D, D), dtype=jnp.float32) * scale, 'bg': jnp.zeros((D,), dtype=jnp.float32), 'We': jax.random.normal(k3, (E, D, D), dtype=jnp.float32) * scale, 'be': jnp.zeros((E, D), dtype=jnp.float32)}
    _L0_ffn_all = _L0_ffn_setup()
    _L0_ffn_in = {k: v for k, v in _L0_ffn_all.items() if k in ('Wg', 'bg', 'We', 'be')}
    del _L0_ffn_all

    def _L1_attn_setup():
        import jax, jax.numpy as jnp
        import numpy as np
        B, T, D = (4, 256, 128)

        def ste_sign(x):
            return jax.lax.stop_gradient(jnp.sign(x) - x) + x
        key = jax.random.key(seed)
        kx, kq, kk, kv = jax.random.split(key, 4)
        return {'x': jax.random.normal(kx, (B, T, D), dtype=jnp.float32), 'bv_q': jax.random.normal(kq, (D,), dtype=jnp.float32) * 0.02, 'bv_k': jax.random.normal(kk, (D,), dtype=jnp.float32) * 0.02, 'bv_v': jax.random.normal(kv, (D,), dtype=jnp.float32) * 0.02}
    _L1_attn_all = _L1_attn_setup()
    _L1_attn_in = {k: v for k, v in _L1_attn_all.items() if k in ('bv_q', 'bv_k', 'bv_v')}
    del _L1_attn_all

    def _L1_xattn_setup():
        import jax, jax.numpy as jnp
        import numpy as np
        MODEL_DIM = 128
        NUM_HEADS = 16
        HEAD_DIM = MODEL_DIM // NUM_HEADS

        def _split_heads(x):
            B, S, D = x.shape
            return x.reshape(B, S, NUM_HEADS, HEAD_DIM).transpose(0, 2, 1, 3)
        key = jax.random.key(seed)
        ks = jax.random.split(key, 11)
        B, S, D = (2, 256, MODEL_DIM)
        scale = 1.0 / np.sqrt(D)
        inp = {'Q': jax.random.normal(ks[0], (B, S, D), jnp.float32), 'K': jax.random.normal(ks[1], (B, S, D), jnp.float32), 'V': jax.random.normal(ks[2], (B, S, D), jnp.float32), 'mask': jnp.tril(jnp.ones((S, S), jnp.int32)), 'Wq': jax.random.normal(ks[3], (D, D), jnp.float32) * scale, 'bq': jax.random.normal(ks[4], (D,), jnp.float32) * 0.01, 'Wk': jax.random.normal(ks[5], (D, D), jnp.float32) * scale, 'bk': jax.random.normal(ks[6], (D,), jnp.float32) * 0.01, 'Wv': jax.random.normal(ks[7], (D, D), jnp.float32) * scale, 'bv': jax.random.normal(ks[8], (D,), jnp.float32) * 0.01, 'Wo': jax.random.normal(ks[9], (D, D), jnp.float32) * scale, 'bo': jax.random.normal(ks[10], (D,), jnp.float32) * 0.01}
        return inp
    _L1_xattn_all = _L1_xattn_setup()
    _L1_xattn_in = {k: v for k, v in _L1_xattn_all.items() if k in ('Wq', 'bq', 'Wk', 'bk', 'Wv', 'bv', 'Wo', 'bo')}
    del _L1_xattn_all

    def _L1_ffn_setup():
        import jax, jax.numpy as jnp
        import numpy as np
        B, T, C, H, E = (4, 256, 128, 256, 8)
        CAPACITY_FACTOR = 1.0
        key = jax.random.key(seed)
        ks = jax.random.split(key, 5)
        scale = 0.02
        return {'x': jax.random.normal(ks[0], (B, T, C), dtype=jnp.float32), 'Wg': jax.random.normal(ks[1], (E, C), dtype=jnp.float32) * scale, 'W1': jax.random.normal(ks[2], (E, H, C), dtype=jnp.float32) * scale, 'W2': jax.random.normal(ks[3], (E, C, H), dtype=jnp.float32) * scale, 'W3': jax.random.normal(ks[4], (E, H, C), dtype=jnp.float32) * scale}
    _L1_ffn_all = _L1_ffn_setup()
    _L1_ffn_in = {k: v for k, v in _L1_ffn_all.items() if k in ('Wg', 'W1', 'W2', 'W3')}
    del _L1_ffn_all
    return {'x': x, 'ctx_1024': ctx_1024, 'mask_SxS2_ik0': mask_SxS2_ik0, 'L0_attn_A_real': _L0_attn_in['A_real'], 'L0_attn_A_imag': _L0_attn_in['A_imag'], 'L0_attn_B': _L0_attn_in['B'], 'L0_attn_C': _L0_attn_in['C'], 'L0_xattn_Wq': _L0_xattn_in['Wq'], 'L0_xattn_bq': _L0_xattn_in['bq'], 'L0_xattn_Wk': _L0_xattn_in['Wk'], 'L0_xattn_bk': _L0_xattn_in['bk'], 'L0_xattn_Wv': _L0_xattn_in['Wv'], 'L0_xattn_bv': _L0_xattn_in['bv'], 'L0_xattn_Wo': _L0_xattn_in['Wo'], 'L0_xattn_bo': _L0_xattn_in['bo'], 'L0_ffn_Wg': _L0_ffn_in['Wg'], 'L0_ffn_bg': _L0_ffn_in['bg'], 'L0_ffn_We': _L0_ffn_in['We'], 'L0_ffn_be': _L0_ffn_in['be'], 'L1_attn_bv_q': _L1_attn_in['bv_q'], 'L1_attn_bv_k': _L1_attn_in['bv_k'], 'L1_attn_bv_v': _L1_attn_in['bv_v'], 'L1_xattn_Wq': _L1_xattn_in['Wq'], 'L1_xattn_bq': _L1_xattn_in['bq'], 'L1_xattn_Wk': _L1_xattn_in['Wk'], 'L1_xattn_bk': _L1_xattn_in['bk'], 'L1_xattn_Wv': _L1_xattn_in['Wv'], 'L1_xattn_bv': _L1_xattn_in['bv'], 'L1_xattn_Wo': _L1_xattn_in['Wo'], 'L1_xattn_bo': _L1_xattn_in['bo'], 'L1_ffn_Wg': _L1_ffn_in['Wg'], 'L1_ffn_W1': _L1_ffn_in['W1'], 'L1_ffn_W2': _L1_ffn_in['W2'], 'L1_ffn_W3': _L1_ffn_in['W3']}

def reference(x, ctx_1024, mask_SxS2_ik0, L0_attn_A_real, L0_attn_A_imag, L0_attn_B, L0_attn_C, L0_xattn_Wq, L0_xattn_bq, L0_xattn_Wk, L0_xattn_bk, L0_xattn_Wv, L0_xattn_bv, L0_xattn_Wo, L0_xattn_bo, L0_ffn_Wg, L0_ffn_bg, L0_ffn_We, L0_ffn_be, L1_attn_bv_q, L1_attn_bv_k, L1_attn_bv_v, L1_xattn_Wq, L1_xattn_bq, L1_xattn_Wk, L1_xattn_bk, L1_xattn_Wv, L1_xattn_bv, L1_xattn_Wo, L1_xattn_bo, L1_ffn_Wg, L1_ffn_W1, L1_ffn_W2, L1_ffn_W3):
    import jax
    import jax.numpy as jnp

    def _L0_attn_ref(u, A_real, A_imag, B, C):
        import jax, jax.numpy as jnp
        import numpy as np
        DT = 0.01
        DAMP_MIN = 0.0005
        BATCH, SEQ, D_IN, N_STATE = (16, 256, 128, 128)
        'Real-input path of StableResonantSSM.\n\n            Bilinear discretization of diagonal complex A:\n              a_disc = (1 + dt/2 * a) / (1 - dt/2 * a)          (elementwise, A diagonal)\n              B_disc = sqrt(dt) * B / (1 - dt/2 * a)            (row-wise scaling)\n            Recurrence: h_t = a_disc * h_{t-1} + B_disc @ u_t;  y_t = Re(C @ h_t).\n            '
        dt = jnp.float32(DT)
        a = (A_real + 1j * A_imag).astype(jnp.complex64)
        denom = 1.0 - dt / 2 * a
        a_disc = (1.0 + dt / 2 * a) / denom
        B_disc = jnp.sqrt(dt) * B.astype(jnp.complex64) / denom[:, None]
        Bu = jnp.einsum('btd,nd->tbn', u, B_disc)

        def step(h, bu_t):
            h = a_disc * h + bu_t
            return (h, h)
        h0 = jnp.zeros((u.shape[0], a.shape[0]), jnp.complex64)
        _, hs = jax.lax.scan(step, h0, Bu)
        y = jnp.einsum('tbn,dn->btd', hs.real, C)
        return y

    def _L0_xattn_ref(query, key, value, Wq, bq, Wk, bk, Wv, bv, Wo, bo):
        import jax, jax.numpy as jnp
        import numpy as np
        D_MODEL = 128
        NUM_HEADS = 16
        HEAD_DIM = D_MODEL // NUM_HEADS
        B, S = (4, 256)
        b = query.shape[0]

        def split_heads(x):
            return x.reshape(b, -1, NUM_HEADS, HEAD_DIM).transpose(0, 2, 1, 3)
        q = split_heads(query @ Wq.T + bq)
        k = split_heads(key @ Wk.T + bk)
        v = split_heads(value @ Wv.T + bv)
        scores = jnp.einsum('bhqd,bhkd->bhqk', q, k) / np.sqrt(HEAD_DIM)
        weights = jax.nn.softmax(scores, axis=-1)
        out = jnp.einsum('bhqk,bhkd->bhqd', weights, v)
        out = out.transpose(0, 2, 1, 3).reshape(b, -1, D_MODEL)
        return out @ Wo.T + bo

    def _L0_ffn_ref(x, Wg, bg, We, be):
        import jax, jax.numpy as jnp
        import numpy as np
        B, S, D, E = (4, 512, 128, 8)
        probs = jax.nn.softmax(x @ Wg + bg, axis=-1)
        idx = jnp.argmax(probs, axis=-1)
        p = jnp.take_along_axis(probs, idx[..., None], axis=-1)[..., 0]
        e_idx = idx % We.shape[0]
        h = jax.nn.relu(jnp.einsum('bsd,edf->besf', x, We) + be[None, :, None, :])
        onehot = jax.nn.one_hot(e_idx, We.shape[0], dtype=x.dtype)
        out = jnp.einsum('besf,bse->bsf', h, onehot) * p[..., None]
        return out

    def _L1_attn_ref(x, bv_q, bv_k, bv_v):
        import jax, jax.numpy as jnp
        import numpy as np
        B, T, D = (4, 256, 128)

        def ste_sign(x):
            return jax.lax.stop_gradient(jnp.sign(x) - x) + x
        d = x.shape[-1]
        scale = d ** (-0.5)
        bq = ste_sign(bv_q)
        bk = ste_sign(bv_k)
        bv = ste_sign(bv_v)
        Q = ste_sign(x * bq)
        K = ste_sign(x * bk)
        V = x * bv
        scores = jnp.einsum('btd,bsd->bts', Q, K) * scale
        t = x.shape[1]
        causal = jnp.tril(jnp.ones((t, t), dtype=bool))
        scores = jnp.where(causal, scores, -jnp.inf)
        attn = jax.nn.sigmoid(scores * 4.0)
        attn = jnp.where(causal, attn, 0.0)
        return jnp.einsum('bts,bsd->btd', attn, V)

    def _L1_xattn_ref(Q, K, V, mask, Wq, bq, Wk, bk, Wv, bv, Wo, bo):
        import jax, jax.numpy as jnp
        import numpy as np
        MODEL_DIM = 128
        NUM_HEADS = 16
        HEAD_DIM = MODEL_DIM // NUM_HEADS

        def _split_heads(x):
            B, S, D = x.shape
            return x.reshape(B, S, NUM_HEADS, HEAD_DIM).transpose(0, 2, 1, 3)
        q = _split_heads(Q @ Wq.T + bq)
        k = _split_heads(K @ Wk.T + bk)
        v = _split_heads(V @ Wv.T + bv)
        scores = jnp.einsum('bhqd,bhkd->bhqk', q, k) / jnp.sqrt(jnp.float32(HEAD_DIM))
        scores = jnp.where(mask == 0, jnp.float32(-1e-09), scores)
        probs = jax.nn.softmax(scores, axis=-1)
        attn = jnp.einsum('bhqk,bhkd->bhqd', probs, v)
        B, H, S, hd = attn.shape
        out = attn.transpose(0, 2, 1, 3).reshape(B, S, MODEL_DIM)
        return out @ Wo.T + bo

    def _L1_ffn_ref(x, Wg, W1, W2, W3):
        import jax, jax.numpy as jnp
        import numpy as np
        B, T, C, H, E = (4, 256, 128, 256, 8)
        CAPACITY_FACTOR = 1.0
        b, t, c = x.shape
        e = Wg.shape[0]
        n = b * t
        capacity = max(1, int(CAPACITY_FACTOR * n / e))
        x_flat = x.reshape(n, c)
        scores = (x_flat @ Wg.T).T
        top_vals, token_idx = jax.lax.top_k(scores, capacity)
        token_w = jax.nn.softmax(top_vals, axis=-1)
        xg = x_flat[token_idx]
        h = jax.nn.silu(jnp.einsum('eic,ehc->eih', xg, W1)) * jnp.einsum('eic,ehc->eih', xg, W3)
        y = jnp.einsum('eih,ech->eic', h, W2) * token_w[..., None]
        out = jnp.zeros_like(x_flat).at[token_idx.reshape(-1)].add(y.reshape(-1, c))
        return out.reshape(b, t, c)
    x = x + _L0_attn_ref(_layernorm(x, axis=-1), L0_attn_A_real, L0_attn_A_imag, L0_attn_B, L0_attn_C)
    x = x + _L0_xattn_ref(_layernorm(x, axis=-1), ctx_1024, ctx_1024, L0_xattn_Wq, L0_xattn_bq, L0_xattn_Wk, L0_xattn_bk, L0_xattn_Wv, L0_xattn_bv, L0_xattn_Wo, L0_xattn_bo)
    x = x + _L0_ffn_ref(_layernorm(x, axis=-1), L0_ffn_Wg, L0_ffn_bg, L0_ffn_We, L0_ffn_be)
    x = x + _L1_attn_ref(_layernorm(x, axis=-1), L1_attn_bv_q, L1_attn_bv_k, L1_attn_bv_v)
    x = x + _L1_xattn_ref(_layernorm(x, axis=-1), ctx_1024, ctx_1024, mask_SxS2_ik0, L1_xattn_Wq, L1_xattn_bq, L1_xattn_Wk, L1_xattn_bk, L1_xattn_Wv, L1_xattn_bv, L1_xattn_Wo, L1_xattn_bo)
    x = x + _L1_ffn_ref(_layernorm(x, axis=-1), L1_ffn_Wg, L1_ffn_W1, L1_ffn_W2, L1_ffn_W3)
    return x

_drawn_inputs = setup_inputs


def setup_inputs(seed=0):
    import zlib

    import numpy as np

    out = dict(_drawn_inputs(seed))
    spreads = {'L0_xattn_bq': (0.0, 0.1),
     'L0_xattn_bk': (0.0, 2.0),
     'L0_xattn_bv': (0.0, 0.1),
     'L0_xattn_bo': (0.0, 0.1),
     'L0_ffn_bg': (0.0, 0.1),
     'L0_ffn_be': (0.0, 0.397)}
    factors = {'L0_attn_A_real': 3.759,
     'L1_xattn_Wq': 8.0,
     'L1_xattn_bq': 25.472,
     'L1_xattn_Wk': 8.0,
     'L1_xattn_bk': 200.0,
     'L1_xattn_Wv': 4.325,
     'L1_xattn_bv': 49.102,
     'L1_xattn_Wo': 4.285,
     'L1_xattn_bo': 64.0,
     'L1_ffn_Wg': 64.0,
     'L1_ffn_W1': 64.0,
     'L1_ffn_W2': 64.0,
     'L1_ffn_W3': 64.0}
    for name, (base, spread) in spreads.items():
        noise = np.random.default_rng([zlib.crc32(name.encode()), seed]).standard_normal(out[name].shape)
        drawn = base * np.exp(spread * noise) if base else spread * noise
        out[name] = jnp.asarray(drawn.astype(out[name].dtype))
    for name, factor in factors.items():
        out[name] = (out[name] * factor).astype(out[name].dtype)
    return out
```

```python
from contextlib import ExitStack

import concourse.bass as bass
from concourse import mybir

ALU = mybir.AluOpType
ACT = mybir.ActivationFunctionType
AX = mybir.AxisListType
F32 = mybir.dt.float32
BF16 = mybir.dt.bfloat16
I32 = mybir.dt.int32
U32 = mybir.dt.uint32

P = 128
B, S, D = 8, 256, 128
NT = B * S // P
H, HD = 16, 8
E = 8
HID = 256
CAP = B * S // E
LANES = 2
ROUNDS = B // LANES
NLN = 6
SCALE = 1.0 / float(HD) ** 0.5
BIG = -1.0e30
DT = 0.01
SPLITS = 6
MROW = SPLITS * HD
KROWS = MROW + 3
NTILE = 16
NQUAD = 4


def decoder(nc, a, out):
    ctx = ExitStack()
    with ctx:
        def sb(name, shape, dt=F32):
            return ctx.enter_context(nc.sbuf_tensor(name, shape, dt))

        def sem(name):
            return ctx.enter_context(nc.semaphore(name))

        def lanes(name, shape, dt=F32):
            return [sb(f"{name}{p}", shape, dt) for p in range(LANES)]

        def bank(name):
            return ctx.enter_context(nc.psum_tensor(name, [P, 512], F32))

        score_ps = [bank(f"score_ps{i}") for i in range(2)]
        st_ps = [bank(f"st_ps{i}") for i in range(2)]
        lane_ps = [bank(f"lane_ps{p}") for p in range(LANES)]
        o_ps, t_ps = bank("o_ps"), bank("t_ps")
        quad_ps = [o_ps, t_ps]
        banks = score_ps + st_ps + lane_ps + [o_ps, t_ps]

        ident = sb("ident", [P, P])
        identb = sb("identb", [P, P], BF16)
        ones = sb("ones", [P, P])
        iota_rev = sb("iota_rev", [P, P])
        iota_slot = sb("iota_slot", [P, CAP], BF16)
        tokid = sb("tokid", [P, NT, 2], BF16)
        halfmask = sb("halfmask", [P, 384])
        selb = sb("selb", [E, E, P], BF16)
        blockb = sb("blockb", [P, P], BF16)
        below = sb("below", [P, P])
        emask = sb("emask", [P, E])
        wT = sb("wT", [P, 10, P])
        WQ, WK, WV, WO, SB, SC = 0, 2, 4, 6, 8, 9
        w_hash = sb("w_hash", [P, P])
        w_exp = sb("w_exp", [P, E, P])
        b_exp = sb("b_exp", [E, P])
        rows = sb("rows", [1, 5, P])
        cols = sb("cols", [P, 12])
        CQ, CK, CAR, CAI, CSQ, CSK = 0, 2, 4, 5, 6, 7
        sgn = sb("sgn", [P, 4])
        svrow = sb("svrow", [1, P])
        svs = sb("svs", [1, P])
        svb = sb("svb", [P, P])
        wg_nat = sb("wg_nat", [E, P])
        wg_pad = sb("wg_pad", [P, 248])
        w1n = sb("w1n", [P, 2 * E, P])
        w3n = sb("w3n", [P, 2 * E, P])
        w2n = sb("w2n", [P, E, HID])
        w1T = sb("w1T", [P, 2 * E, P])
        w3T = sb("w3T", [P, 2 * E, P])
        w2T = sb("w2T", [P, 2 * E, P])
        mask = sb("mask", [P, 2, S])
        mbar = sb("mbar", [P, 2, S])
        mbias = sb("mbias", [P, 2, S], BF16)
        blockf = sb("blockf", [P, P])
        er, ei = sb("er", [P, S]), sb("ei", [P, S])
        esin = sb("esin", [P, S])
        t1, t2 = sb("t1", [P, S]), sb("t2", [P, S])
        rdec = sb("rdec", [P, S])
        sv = sb("sv", [P, 32])

        x_all = sb("x_all", [P, NT, D])
        z6 = sb("z6", [P, NT, D])
        nat = z6[:, 0:10, :]
        ctx_in = lanes("ctx_in", [P, 2, D])
        ctxT = lanes("ctxT", [P, S])
        stat = lanes("stat", [P, 2, 6])
        mv = lanes("mv", [P, 2, 2])
        rstd = lanes("rstd", [P, 6])
        z = lanes("z", [P, 2, D])
        zT = lanes("zT", [P, S])
        zm = sb("zm", [P, E, S])
        wa = [zm[:, 4 * p:4 * p + 2, :] for p in range(LANES)]
        ga = [zm[:, 4 * p + 2:4 * p + 4, :] for p in range(LANES)]
        ha = wa
        ytmp = lanes("ytmp", [P, S])
        parts = lanes("parts", [P, 3, S], BF16)
        rest = lanes("rest", [P, S])
        kst = [lanes(f"kst{l}_", [P, 8, S], BF16) for l in range(2)]
        qst = lanes("qst", [P, 8, S], BF16)
        vx = [lanes(f"vx{l}_", [P, 2, H, 32]) for l in range(2)]
        mvx = lanes("mvx", [P, 2, H, 9])
        mx = lanes("mx", [P, 2, H])
        emx = lanes("emx", [P, 2, H])
        mparts = lanes("mparts", [H, 3, S], BF16)
        mrest = lanes("mrest", [H, S])
        probs = [sb(f"probs{i}", [P, 2, S]) for i in range(8)]
        maski = probs[0][:, :, :].bitcast(I32)
        stmp = probs[1][:, 0, :]
        oT = [sb(f"oT{i}", [P, S]) for i in range(2)]
        onums = [sb(f"onum{i}", [P, 2, 4, 9]) for i in range(2)]
        orecs = [sb(f"orec{i}", [P, 2, 4]) for i in range(2)]
        att = lanes("att", [P, 2, D])
        attT = lanes("attT", [P, S])
        lmax = lanes("lmax", [P, 8])
        lexp = lanes("lexp", [P, 2, P])
        hot = lanes("hot", [P, 2, E])
        hotT = lanes("hotT", [E, S])
        hotTb = lanes("hotTb", [E, S], BF16)
        kb = lanes("kb", [P, S], BF16)
        qb = lanes("qb", [P, S], BF16)
        th = lanes("th", [P, 384])
        aw = th
        junk = sb("junk", [P, 2, 2, S], BF16)

        zT6, xgT = w1n, w3n
        xg = w2n[:, :, :].rearrange("p e (i c) -> p (e i) c", i=2)
        sc, ex, eq, cum = er[:, 0:P], er[:, P:S], ei[:, 0:P], ei[:, P:S]
        sel, pos, posT = t1[:, 0:P], t1[:, P:S], t2[:, 0:P]
        g = sb("g", [P, 64])
        uthr = sb("uthr", [P, 4], I32)
        U, M, F, DB = (uthr[:, i:i + 1] for i in range(4))
        cntb = sb("cntb", [P, 2], BF16)
        m8 = sb("m8", [1, 2 * P])
        onehot = [probs[i][:, 0, 0:CAP // 2].bitcast(BF16) for i in range(8)]
        ids = sb("ids", [P, 2 * E], I32)
        wslot = sb("wslot", [P, 2 * E])
        nm8 = sb("nm8", [P, E])
        rs8 = sb("rs8", [P, E])
        act1 = [zm[:, 2 * i:2 * i + 2, :] for i in range(2)]
        hT = [zm[:, 4 + 2 * i:6 + 2 * i, :] for i in range(2)]
        ysc = [oT[i][:, :].rearrange("p (i c) -> p i c", i=2) for i in range(2)]

        def dram(name, shape, dt):
            return nc.dram_tensor(name, shape, dt, kind="Internal").ap()

        kscr = [[dram(f"kscr{l}{p}", (3, P, S), BF16) for p in range(LANES)] for l in range(2)]
        qscr = [dram(f"qscr{p}", (3, P, S), BF16) for p in range(LANES)]
        mscr = [dram(f"mscr{p}", (H, 3, S), BF16) for p in range(LANES)]
        zrows = dram("zrows", (B * S, D), F32)

        ld_small, ld_x, ld_moe = sem("ld_small"), sem("ld_x"), sem("ld_moe")
        pool_const, pool_step = sem("pool_const"), sem("pool_step")
        act_setup, dve_setup = sem("act_setup"), sem("dve_setup")
        setup_ps, setup_act, setup_dve = sem("setup_ps"), sem("setup_act"), sem("setup_dve")
        dve_chain = sem("dve_chain")
        tab_sq, tab_pow = sem("tab_sq"), sem("tab_pow")
        ctx_ld = [sem(f"ctx_ld{p}") for p in range(LANES)]
        ctxT_psum, ctxT_ready = sem("ctxT_psum"), sem("ctxT_ready")
        k_psum, k_split = sem("k_psum"), sem("k_split")
        v_psum, v_ready = sem("v_psum"), sem("v_ready")
        mv_psum, mv_ready = sem("mv_psum"), sem("mv_ready")
        k_stored = [sem(f"k_stored{p}") for p in range(LANES)]
        k_stacked = [sem(f"k_stacked{p}") for p in range(LANES)]
        ln_stats, ln_rstd, z_ready = sem("ln_stats"), sem("ln_rstd"), sem("z_ready")
        zT_psum, zT_ready = sem("zT_psum"), sem("zT_ready")
        w_psum, scan_done, h_ready = sem("w_psum"), sem("scan_done"), sem("h_ready")
        y_psum, resid = sem("y_psum"), sem("resid")
        q_psum, q_split = sem("q_psum"), sem("q_split")
        q_stored = [sem(f"q_stored{p}") for p in range(LANES)]
        q_stacked = [sem(f"q_stacked{p}") for p in range(LANES)]
        s_psum, s_maxed = sem("s_psum"), sem("s_maxed")
        mT_psum, m_split = sem("mT_psum"), sem("m_split")
        m_neg, emx_ready = sem("m_neg"), sem("emx_ready")
        m_stored = [sem(f"m_stored{p}") for p in range(LANES)]
        m_stacked = [sem(f"m_stacked{p}") for p in range(LANES)]
        st_psum, exp_done = sem("st_psum"), sem("exp_done")
        pv_done, o_evac = sem("pv_done"), sem("o_evac")
        t_psum, norm_done = sem("t_psum"), sem("norm_done")
        attT_psum, attT_ready = sem("attT_psum"), sem("attT_ready")
        lg_psum, lg_copied, lg_max, lg_exp = sem("lg_psum"), sem("lg_copied"), sem("lg_max"), sem("lg_exp")
        hot_ready, hotT_psum, hotT_ready = sem("hot_ready"), sem("hotT_psum"), sem("hotT_ready")
        bc_psum, zm_ready = sem("bc_psum"), sem("zm_ready")
        sign_ready, qb_ready, sg_psum = sem("sign_ready"), sem("qb_ready"), sem("sg_psum")
        tanh_done, aw_ready = sem("tanh_done"), sem("aw_ready")
        rows_out = sem("rows_out")
        zT6_psum, zT6_ready, gate_psum = sem("zT6_psum"), sem("zT6_ready"), sem("gate_psum")
        cmax_ready, cmaxT_psum, m8_ready, mbc_psum = sem("cmax_ready"), sem("cmaxT_psum"), sem("m8_ready"), sem("mbc_psum")
        nm_ready, gate_exp = sem("nm_ready"), sem("gate_exp")
        cnt_ready, tot_psum = sem("cnt_ready"), sem("tot_psum")
        ties_ready, ties_psum = sem("ties_ready"), sem("ties_psum")
        sel_ready, sel_psum = sem("sel_ready"), sem("sel_psum")
        pos_ready, pos_psum = sem("pos_ready"), sem("pos_psum")
        onehot_ready, onehot_used, ids_ready = sem("onehot_ready"), sem("onehot_used"), sem("ids_ready")
        gathered = [sem(f"gathered{i}") for i in range(2 * E)]
        xgT_psum, xgT_ready, ws_psum, wslot_ready = sem("xgT_psum"), sem("xgT_ready"), sem("ws_psum"), sem("wslot_ready")
        up_psum, silu_done, hT_ready = sem("up_psum"), sem("silu_done"), sem("hT_ready")
        down_psum, y_ready = sem("down_psum"), sem("y_ready")
        scattered = [sem(f"scattered{i}") for i in range(2)]

        block = ctx.enter_context(nc.Block())

        def nth(r, p, n=1, k=None):
            return (LANES * r + p) * n + (n if k is None else k)

        def nth_ln(r, i, p):
            return r * NLN * LANES + i * LANES + p + 1

        def nth_zp(r, i, p):
            return r * (NLN - 1) * LANES + i * LANES + p + 1

        def tile_no(r, l, p, u):
            return ((r * 2 + l) * LANES + p) * NTILE + u

        def wait(eng, s, v):
            if isinstance(v, int) and v <= 0:
                return
            eng.wait_ge(s, v)

        def head_at(h):
            return 64 * (h // 8), h % 8

        def xs(r, p):
            return x_all[:, bass.ds(2 * (LANES * r + p), 2), :] if not isinstance(r, int) else \
                x_all[:, 2 * (LANES * r + p):2 * (LANES * r + p) + 2, :]

        def z6s(r, p):
            t = 2 * (LANES * r + p)
            return z6[:, bass.ds(t, 2), :] if not isinstance(r, int) else z6[:, t:t + 2, :]

        def rounds(eng, body):
            body(0)
            for r in range(1, ROUNDS):
                body(r)

        turn = [([nat[:, i, :] for i in range(4 * j, 4 * j + 4)], wT[:, 4 * j:4 * j + 4, :]) for j in range(2)]
        turn.append(([nat[:, 8, :], nat[:, 9, :]], wT[:, 8:10, :]))
        for src, dst in ((w1n, w1T), (w3n, w3T)):
            turn += [([src[:, i, :] for i in range(4 * j, 4 * j + 4)], dst[:, 4 * j:4 * j + 4, :]) for j in range(4)]
        turn += [([w2n[:, 2 * j + i // 2, P * (i % 2):P * (i % 2) + P] for i in range(4)],
                  w2T[:, 4 * j:4 * j + 4, :]) for j in range(4)]
        NSMALL = 3
        N_SMALL = 15 + 6 + 8
        POOL_SETUP = 49
        NTURN = len(turn)

        @block.sync
        def _(sp):
            small = [
                (nat[:, WQ, :], a["L0_xattn_Wq"]), (nat[:, WQ + 1, :], a["L1_xattn_Wq"]),
                (nat[:, WK, :], a["L0_xattn_Wk"]), (nat[:, WK + 1, :], a["L1_xattn_Wk"]),
                (nat[:, WV, :], a["L0_xattn_Wv"]), (nat[:, WV + 1, :], a["L1_xattn_Wv"]),
                (nat[:, WO, :], a["L0_xattn_Wo"]), (nat[:, WO + 1, :], a["L1_xattn_Wo"]),
                (nat[:, SB, :], a["L0_attn_B"]), (nat[:, SC, :], a["L0_attn_C"]),
                (w_hash[:, :], a["L0_ffn_Wg"]), (w_exp[:, :, :], a["L0_ffn_We"].rearrange("e d f -> d e f")),
                (b_exp[:, :], a["L0_ffn_be"]), (wg_nat[:, :], a["L1_ffn_Wg"]),
                (maski[:, :, :], a["mask_SxS2_ik0"].rearrange("(t p) k -> p t k", p=P)),
            ]
            for i, n in enumerate(("L0_xattn_bv", "L1_xattn_bv", "L0_xattn_bo", "L1_xattn_bo", "L0_ffn_bg")):
                small.append((rows[0:1, i, :], a[n].rearrange("(o n) -> o n", o=1)))
            small.append((svrow[:, :], a["L1_attn_bv_v"].rearrange("(o n) -> o n", o=1)))
            for c, n in ((CQ, "L0_xattn_bq"), (CQ + 1, "L1_xattn_bq"), (CK, "L0_xattn_bk"), (CK + 1, "L1_xattn_bk"),
                         (CAR, "L0_attn_A_real"), (CAI, "L0_attn_A_imag"), (CSQ, "L1_attn_bv_q"), (CSK, "L1_attn_bv_k")):
                small.append((cols[:, c:c + 1], a[n].rearrange("(n o) -> n o", o=1)))
            assert len(small) == N_SMALL
            for dst, src in small:
                sp.dma_start(dst, src).then_inc(ld_small, 16)
            sp.dma_start(x_all[:, :, :], a["x"].rearrange("b (t p) d -> p (b t) d", p=P)).then_inc(ld_x, 16)
            sp.dma_start(w1n[:, :, :], a["L1_ffn_W1"].rearrange("e (t p) c -> p (e t) c", p=P)).then_inc(ld_moe, 16)
            sp.dma_start(w3n[:, :, :], a["L1_ffn_W3"].rearrange("e (t p) c -> p (e t) c", p=P)).then_inc(ld_moe, 16)
            sp.dma_start(w2n[:, :, :], a["L1_ffn_W2"].rearrange("e c h -> c e h")).then_inc(ld_moe, 16)

            def stack_rows(dst, scr, plan, s):
                for e in range(2):
                    for j, srcs in plan:
                        for i, part in enumerate(srcs):
                            r0 = 64 * e + HD * (j + i)
                            sp.dma_start(dst[r0:r0 + HD, :, :],
                                         scr[part, 64 * e:64 * e + 64, :].rearrange("(t d) n -> d t n", d=HD)
                                         ).then_inc(s, 16)

            def body(r):
                for p in range(LANES):
                    wait(sp, ctxT_psum, nth(r - 1, p))
                    sp.dma_start(ctx_in[p][:, :, :],
                                 a["ctx_1024"][LANES * r + p].rearrange("(t p) d -> p t d", p=P)).then_inc(ctx_ld[p], 16)
                for l in range(2):
                    for p in range(LANES):
                        sp.wait_ge(k_split, nth(r, p) + l * LANES + r * LANES)
                        sp.dma_start(kscr[l][p].rearrange("s p n -> p s n"), parts[p][:, :, :]).then_inc(k_stored[p], 16)
                    for p in range(LANES):
                        sp.wait_ge(k_stored[p], 16 * (2 * r + l + 1))
                        stack_rows(kst[l][p], kscr[l][p], [(0, (0, 0, 0, 1, 1, 2))], k_stacked[p])
                for l in range(2):
                    for p in range(LANES):
                        sp.wait_ge(q_split, nth(r, p) + l * LANES + r * LANES)
                        sp.dma_start(qscr[p].rearrange("s p n -> p s n"), parts[p][:, :, :]).then_inc(q_stored[p], 16)
                    for p in range(LANES):
                        sp.wait_ge(q_stored[p], 16 * (2 * r + l + 1))
                        stack_rows(qst[p], qscr[p], [(0, (0, 1, 2, 0, 1, 0))], q_stacked[p])
                    for p in range(LANES):
                        sp.wait_ge(m_split, nth(r, p) + l * LANES + r * LANES)
                        sp.dma_start(mscr[p], mparts[p][:, :, :]).then_inc(m_stored[p], 16)
                        sp.wait_ge(m_stored[p], 16 * (2 * r + l + 1))
                        for e in range(2):
                            sp.dma_start(qst[p][64 * e + MROW:64 * e + KROWS, :, :],
                                         mscr[p][8 * e:8 * e + 8].rearrange("t j n -> j t n")).then_inc(m_stacked[p], 16)

            rounds(sp, body)
            sp.wait_ge(z_ready, NLN * B)
            sp.dma_start(zrows.rearrange("(t p) d -> p t d", p=P), z6[:, :, :]).then_inc(rows_out, 16)
            sp.dma_start(out.rearrange("b (t p) d -> p (b t) d", p=P), x_all[:, :, :]).then_inc(rows_out, 16)
            sp.wait_ge(rows_out, 32)
            for i in range(2):
                sp.wait_ge(scattered[i], 16 * E)


        @block.gpsimd
        def _(pool):
            n = [0]

            def step(ins):
                n[0] += 1
                ins.then_inc(pool_step, 1)
                pool.wait_ge(pool_step, n[0])

            step(pool.memset(ident[:, :], 0.0))
            step(pool.affine_select(out=ident[:, :], in_=ident[:, :], compare_op=ALU.not_equal, fill=1.0,
                                    base=0, pattern=[[-1, P]], channel_multiplier=1))
            pool.memset(ones[:, :], 1.0).then_inc(pool_const, 1)
            step(pool.tensor_copy(identb[:, :], ident[:, :]))
            step(pool.iota(iota_rev[:, :], pattern=[[-1, P]], base=P, channel_multiplier=0,
                           allow_small_or_imprecise_dtypes=True))
            step(pool.iota(iota_slot[:, :], pattern=[[1, CAP]], base=0, channel_multiplier=0,
                           allow_small_or_imprecise_dtypes=True))
            step(pool.iota(tokid[:, :, 0], pattern=[[0, NT]], base=0, channel_multiplier=1,
                           allow_small_or_imprecise_dtypes=True))
            step(pool.iota(tokid[:, :, 1], pattern=[[1, NT]], base=0, channel_multiplier=0,
                           allow_small_or_imprecise_dtypes=True))
            step(pool.memset(halfmask[:, :], 0.5))
            for c in (0, 256):
                step(pool.affine_select(out=halfmask[:, c:c + P], in_=halfmask[:, c:c + P], compare_op=ALU.is_ge,
                                        fill=0.0, base=0, pattern=[[1, P]], channel_multiplier=-1))
            step(pool.memset(selb[:, :, :], 0.0))
            step(pool.affine_select(out=selb[:, :, :], in_=selb[:, :, :], compare_op=ALU.not_equal, fill=1.0,
                                    base=0, pattern=[[-1, E], [0, P]], channel_multiplier=1))
            step(pool.memset(emask[:, :], 0.0))
            for i in range(NT):
                step(pool.affine_select(out=emask[:, :], in_=emask[:, :], compare_op=ALU.not_equal, fill=1.0,
                                        base=-E * i, pattern=[[-1, E]], channel_multiplier=1))
            step(pool.tensor_copy(below[:, :].rearrange("p (c e) -> p c e", e=E),
                                  emask[:, :].unsqueeze(1).to_broadcast([P, NT, E])))
            step(pool.tensor_copy(blockf[:, :], below[:, :]))
            step(pool.tensor_copy(blockb[:, :], below[:, :]))
            step(pool.affine_select(out=below[:, :].rearrange("p (c e) -> p c e", e=E),
                                    in_=below[:, :].rearrange("p (c e) -> p c e", e=E), compare_op=ALU.is_gt,
                                    fill=0.0, base=0, pattern=[[E, NT], [0, E]], channel_multiplier=-1))
            step(pool.memset(wg_pad[:, :], 0.0))
            for p in range(LANES):
                for l in range(2):
                    for e in range(2):
                        step(pool.memset(kst[l][p][64 * e + 32:64 * e + 64, :, :], 1.0))
                    step(pool.memset(vx[l][p][:, :, :, :], 1.0))
                step(pool.memset(rstd[p][:, 4:6], -0.5))
            step(pool.memset(rdec[:, :], 1.0))
            pool.memset(junk[:, 0, 0, :], 0.0).then_inc(pool_const, 1)

            pool.wait_ge(tab_sq, 1)
            pool.tensor_tensor(sv[:, 12:13], sv[:, 10:11], sv[:, 11:12], ALU.pow).then_inc(tab_pow, 1)

            def norm(r, i, p):
                pool.wait_ge(ln_stats, nth_ln(r, i, p))
                step(pool.tensor_scalar(rstd[p][:, 0:2], mv[p][:, :, 1], 1e-5, None, ALU.add))
                pool.tensor_tensor(rstd[p][:, 2:4], rstd[p][:, 0:2], rstd[p][:, 4:6], ALU.pow).then_inc(ln_rstd, 1)

            def body(r):
                for i in range(NLN):
                    for p in range(LANES):
                        norm(r, i, p)
                    if i == 0:
                        for p in range(LANES):
                            pool.wait_ge(scan_done, nth(r, p))
                            pool.tensor_tensor(ha[p][:, 0, :], ga[p][:, 0, :], t1[:, :], ALU.mult)
                            pool.tensor_tensor(ha[p][:, 1, :], ga[p][:, 1, :], t2[:, :], ALU.mult).then_inc(h_ready, 1)

            rounds(pool, body)

            pool.wait_ge(rows_out, 32)
            for k in range(2 * E):
                pool.wait_ge(ids_ready, k // 2 + 1)
                pool.indirect_dma_start(out=xg[:, k, :], out_offset=None, in_=zrows[:, :],
                                        in_offset=bass.IndirectOffsetOnAxis(ap=ids[:, k:k + 1], axis=0)
                                        ).then_inc(gathered[k], 16)
            for e in range(E):
                pool.wait_ge(y_ready, e + 1)
                for i in range(2):
                    if e > 0:
                        pool.wait_ge(scattered[0], 16 * e)
                        pool.wait_ge(scattered[1], 16 * e)
                for i in range(2):
                    k = 2 * e + i
                    pool.indirect_dma_start(out=out.rearrange("b s d -> (b s) d"),
                                            out_offset=bass.IndirectOffsetOnAxis(ap=ids[:, k:k + 1], axis=0),
                                            in_=ysc[e % 2][:, i, :], in_offset=None, compute_op=ALU.add,
                                            ).then_inc(scattered[i], 16)

        @block.scalar
        def _(act):
            def copy(o, i):
                return act.activation(o, i, ACT.Copy)

            act.wait_ge(ld_small, 16 * N_SMALL)
            act.activation(sgn[:, 0:2], cols[:, CSQ:CSQ + 2], ACT.Sign)
            act.activation(svs[:, :], svrow[:, :], ACT.Sign).then_inc(act_setup, 1)
            for i in range(0, NTURN, 2):
                act.wait_ge(setup_ps, i + 1)
                n = len(turn[i][0]) * P
                copy(turn[i][1], banks[i % 6][:, 0:n]).then_inc(setup_act, 1)

            def zt(r, i, p):
                act.wait_ge(zT_psum, nth_zp(r, i, p))
                copy(zT[p][:, :], lane_ps[p][:, 0:S]).then_inc(zT_ready, 1)

            def exps(r, l, p, v):
                n = tile_no(r, l, p, v)
                act.wait_ge(st_psum, n + 1)
                wait(act, pv_done, (n // 4 if isinstance(n, int) else quad_no(r, l, p, v // 4)) - 1)
                act.activation(probs[v % 8][:, :, :], st_ps[v % 2][:, :], ACT.Exp, scale=SCALE).then_inc(exp_done, 1)

            def quad_no(r, l, p, q):
                return ((r * 2 + l) * LANES + p) * NQUAD + q

            def evac(r, l, p, q):
                n = quad_no(r, l, p, q)
                act.wait_ge(pv_done, n + 1)
                wait(act, t_psum, n - 1)
                copy(oT[q % 2][:, :], quad_ps[q % 2][:, 0:S]).then_inc(o_evac, 1)

            def body(r):
                for p in range(LANES):
                    act.wait_ge(ctxT_psum, nth(r, p))
                    copy(ctxT[p][:, :], lane_ps[p][:, 0:S]).then_inc(ctxT_ready, 1)
                for l in range(2):
                    for p in range(LANES):
                        act.wait_ge(v_psum, r * 2 * LANES + l * LANES + p + 1)
                        copy(vx[l][p][:, :, :, 0:HD],
                             st_ps[p][:, 0:S].rearrange("p (t h d) -> p t h d", h=H, d=HD)).then_inc(v_ready, 1)
                for p in range(LANES):
                    act.wait_ge(mv_psum, nth(r, p))
                    copy(mvx[p][:, :, :, :], st_ps[p][:, 0:2 * H * 9]).then_inc(mv_ready, 1)
                for p in range(LANES):
                    zt(r, 0, p)
                for l in range(2):
                    if l == 1:
                        for p in range(LANES):
                            zt(r, 2, p)
                        for p in range(LANES):
                            act.wait_ge(lg_psum, nth(r, p))
                            copy(lexp[p][:, :, :], lane_ps[p][:, S:2 * S]).then_inc(lg_copied, 1)
                        for p in range(LANES):
                            act.wait_ge(lg_max, nth(r, p))
                            for t in range(2):
                                ins = act.activation(th[p][:, P * t:P * t + P], lexp[p][:, t, :], ACT.Exp,
                                                     bias=lmax[p][:, 2 + t:3 + t], accum_out=lmax[p][:, 4 + t:5 + t])
                            ins.then_inc(lg_exp, 1)
                        for p in range(LANES):
                            act.wait_ge(hotT_psum, nth(r, p))
                            copy(hotT[p][:, :], lane_ps[p][0:E, 0:S])
                            copy(hotTb[p][:, :], lane_ps[p][0:E, 0:S]).then_inc(hotT_ready, 1)
                        for p in range(LANES):
                            act.wait_ge(zT_psum, nth_zp(r, 3, p))
                            act.activation(kb[p][:, :], lane_ps[p][:, 0:S], ACT.Sign).then_inc(sign_ready, 1)
                        for p in range(LANES):
                            act.wait_ge(sg_psum, nth(r, p))
                            act.activation(th[p][:, :], lane_ps[p][:, 0:384], ACT.Tanh,
                                           scale=2.0 / float(D) ** 0.5).then_inc(tanh_done, 1)
                    for p in range(LANES):
                        zt(r, 1 + 3 * l, p)
                    for p in range(LANES):
                        if l == 1:
                            act.wait_ge(m_neg, nth(r, p))
                            act.activation(emx[p][:, :, :], emx[p][:, :, :], ACT.Exp).then_inc(emx_ready, 1)
                        for q in range(NQUAD):
                            for i in range(4):
                                exps(r, l, p, 4 * q + i)
                            if q >= 1:
                                evac(r, l, p, q - 1)
                        evac(r, l, p, NQUAD - 1)
                        act.wait_ge(attT_psum, r * 2 * LANES + l * LANES + p + 1)
                        copy(attT[p][:, :], lane_ps[p][:, 0:S]).then_inc(attT_ready, 1)

            rounds(act, body)

            for j in range(4):
                act.wait_ge(zT6_psum, j + 1)
                copy(zT6[:, 4 * j:4 * j + 4, :], banks[j][:, :]).then_inc(zT6_ready, 1)
            act.wait_ge(nm_ready, 1)
            act.activation(ex[:, :], sc[:, :], ACT.Exp, bias=g[:, 2:3]).then_inc(gate_exp, 1)
            for e in range(E):
                act.wait_ge(xgT_psum, e + 1)
                copy(xgT[:, 2 * e:2 * e + 2, :], lane_ps[e % 2][:, 0:S]).then_inc(xgT_ready, 1)
                act.wait_ge(ws_psum, e + 1)
                act.activation(wslot[:, 2 * e:2 * e + 2], lane_ps[e % 2][:, S:S + 2], ACT.Exp,
                               bias=nm8[:, e:e + 1]).then_inc(wslot_ready, 1)
            for e in range(E):
                act.wait_ge(up_psum, e + 1)
                if e >= 2:
                    act.wait_ge(hT_ready, e - 1)
                act.activation(act1[e % 2], score_ps[e % 2][:, :], ACT.Silu).then_inc(silu_done, 1)

        @block.tensor
        def _(pe):
            mm = nc.tensor.matmul
            tr = nc.tensor.transpose
            pe.wait_ge(pool_const, 2)
            pe.wait_ge(pool_step, 5)
            pe.wait_ge(ld_small, 16 * N_SMALL)
            for i, (srcs, _) in enumerate(turn):
                if i == NSMALL:
                    pe.wait_ge(ld_moe, 48)
                if i >= 6:
                    j = i - 6
                    pe.wait_ge(setup_act if j % 2 == 0 else setup_dve, j // 2 + 1)
                for k, s in enumerate(srcs):
                    ins = tr(banks[i % 6][:, P * k:P * k + P], s, ident[:, :])
                ins.then_inc(setup_ps, 1)
            tr(o_ps[:, 0:E], wg_nat[:, :], ident[0:E, 0:E])
            pe.wait_ge(act_setup, 1)
            mm(o_ps[:, 256:384], ones[0:1, :], svs[:, :], start=True, stop=True).then_inc(setup_ps, 1)
            pe.wait_ge(dve_setup, 1)
            for kt in range(2):
                for qt in range(2):
                    ins = tr(t_ps[:, S * kt + P * qt:S * kt + P * qt + P], mask[:, qt, P * kt:P * kt + P], ident[:, :])
            ins.then_inc(setup_ps, 1)
            pe.wait_ge(setup_act, (NTURN + 1) // 2)
            pe.wait_ge(setup_dve, NTURN // 2)
            pe.wait_ge(dve_setup, 2)

            def quad_no(r, l, p, q):
                return ((r * 2 + l) * LANES + p) * NQUAD + q

            def zt(r, i, p):
                pe.wait_ge(z_ready, nth_ln(r, i, p))
                for t in range(2):
                    ins = tr(lane_ps[p][:, P * t:P * t + P], z[p][:, t, :], ident[:, :])
                ins.then_inc(zT_psum, 1)

            def score_tile(r, l, p, u):
                n = tile_no(r, l, p, u)
                if u == 0:
                    pe.wait_ge(q_stacked[p], 16 * 12 * (2 * r + l + 1))
                    if l == 0:
                        pe.wait_ge(k_stacked[p], 16 * 24 * (r + 1))
                wait(pe, s_maxed, n - 1)
                qt, pair = u // 8, u % 8
                for i in range(2):
                    r0, t = head_at(2 * pair + i)
                    ins = mm(score_ps[u % 2][:, S * i:S * i + S], qst[p][r0:r0 + MROW, t, P * qt:P * qt + P],
                             kst[l][p][r0:r0 + MROW, t, :], start=True, stop=True)
                ins.then_inc(s_psum, 1)

            def st_tile(r, l, p, v):
                n = tile_no(r, l, p, v)
                if v == 0:
                    pe.wait_ge(m_stacked[p], 16 * 2 * (2 * r + l + 1))
                wait(pe, exp_done, n - 1)
                pair, kt = v // 2, v % 2
                if l == 1:
                    mm(st_ps[v % 2][:, :], identb[:, :], mbias[:, kt, :].unsqueeze(1).to_broadcast([P, 2, S]),
                       start=True, stop=False)
                for i in range(2):
                    r0, t = head_at(2 * pair + i)
                    ins = mm(st_ps[v % 2][:, S * i:S * i + S], kst[l][p][r0:r0 + KROWS, t, P * kt:P * kt + P],
                             qst[p][r0:r0 + KROWS, t, :], start=(l == 0), stop=(l == 0 or i == 1))
                ins.then_inc(st_psum, 1)

            def values(r, l, p, q):
                n = quad_no(r, l, p, q)
                pe.wait_ge(exp_done, 4 * n + 4)
                wait(pe, norm_done, n - 1)
                for kt in range(2):
                    for j in range(4):
                        h = 4 * q + j
                        ins = mm(quad_ps[q % 2][32 * j:32 * j + 32, 0:S], vx[l][p][:, kt, h, :],
                                 probs[(4 * q + 2 * (j // 2) + kt) % 8][:, j % 2, :], start=(kt == 0), stop=(kt == 1),
                                 skip_group_check=True)
                ins.then_inc(pv_done, 1)

            def turn_out(r, l, p, q):
                n = quad_no(r, l, p, q)
                pe.wait_ge(o_evac, n + 1)
                for t in range(2):
                    ins = tr(quad_ps[q % 2][:, S + P * t:S + P * t + P], oT[q % 2][:, P * t:P * t + P], ident[:, :])
                ins.then_inc(t_psum, 1)

            def project(r, p, lhs, w, brow, done):
                for t in range(2):
                    y = lane_ps[p][:, S + P * t:S + P * t + P]
                    mm(y, ones[0:1, :], rows[0:1, brow, :], start=True, stop=False)
                    ins = mm(y, lhs[:, P * t:P * t + P], w, start=False, stop=True)
                ins.then_inc(done, 1)

            def body(r):
                for p in range(LANES):
                    wait(pe, z_ready, nth_ln(r - 1, NLN - 1, p) if not isinstance(r, int) or r > 0 else 0)
                    pe.wait_ge(ctx_ld[p], 16 * (r + 1))
                    for t in range(2):
                        ins = tr(lane_ps[p][:, P * t:P * t + P], ctx_in[p][:, t, :], ident[:, :])
                    ins.then_inc(ctxT_psum, 1)
                for l in range(2):
                    for p in range(LANES):
                        if l == 0:
                            pe.wait_ge(ctxT_ready, nth(r, p))
                        else:
                            pe.wait_ge(k_split, r * 2 * LANES + p + 1)
                            pe.wait_ge(v_ready, r * 2 * LANES + p + 1)
                        mm(lane_ps[p][:, S:2 * S], wT[:, WK + l, :], ctxT[p][:, :], start=True, stop=True).then_inc(k_psum, 1)
                        for t in range(2):
                            v = st_ps[p][:, P * t:P * t + P]
                            mm(v, ones[0:1, :], rows[0:1, l, :], start=True, stop=False)
                            ins = mm(v, ctxT[p][:, P * t:P * t + P], wT[:, WV + l, :], start=False, stop=True)
                        ins.then_inc(v_psum, 1)
                for p in range(LANES):
                    pe.wait_ge(v_ready, r * 2 * LANES + LANES + p + 1)
                    pe.wait_ge(k_split, r * 2 * LANES + LANES + p + 1)
                    for qt in range(2):
                        for kt in range(2):
                            ins = mm(st_ps[p][:, 144 * qt:144 * qt + 144].rearrange("p (h d) -> p h d", d=9),
                                     mbar[:, kt, P * qt:P * qt + P], vx[1][p][:, kt, :, 0:9], start=(kt == 0), stop=(kt == 1))
                    ins.then_inc(mv_psum, 1)
                for p in range(LANES):
                    pe.wait_ge(mv_ready, nth(r, p))
                    zt(r, 0, p)
                for p in range(LANES):
                    pe.wait_ge(zT_ready, nth_zt(r, 0, p))
                    mm(lane_ps[p][:, S:2 * S], wT[:, SB, :], zT[p][:, :], start=True, stop=True).then_inc(w_psum, 1)
                for p in range(LANES):
                    pe.wait_ge(h_ready, nth(r, p))
                    for t in range(2):
                        for i in range(2):
                            ins = mm(lane_ps[p][:, S + P * t:S + P * t + P], ha[p][:, i, P * t:P * t + P], wT[:, SC, :],
                                     start=(i == 0), stop=(i == 1))
                    ins.then_inc(y_psum, 1)
                for l in range(2):
                    if l == 1:
                        ffn(r)
                        sign_attention(r)
                    for p in range(LANES):
                        zt(r, 1 + 3 * l, p)
                    for p in range(LANES):
                        pe.wait_ge(zT_ready, nth_zt(r, 1 + 3 * l, p))
                        mm(lane_ps[p][:, S:2 * S], wT[:, WQ + l, :], zT[p][:, :], start=True, stop=True).then_inc(q_psum, 1)
                    for u in range(NTILE):
                        score_tile(r, l, 0, u)
                    maxima(r, l, 0)
                    attend(r, l, 0)
                    attend(r, l, 1)

            def nth_zt(r, i, p):
                return r * (NLN - 2) * LANES + (i - (1 if i > 3 else 0)) * LANES + p + 1

            def maxima(r, l, p):
                pe.wait_ge(s_maxed, tile_no(r, l, p, NTILE - 1) + 1)
                for t in range(2):
                    ins = tr(lane_ps[p][0:H, P * t:P * t + P], mx[p][:, t, :], ident[:, :])
                ins.then_inc(mT_psum, 1)

            def attend(r, l, p):
                for q in range(NQUAD):
                    for i in range(4):
                        st_tile(r, l, p, 4 * q + i)
                        if p == 0:
                            score_tile(r, l, 1, 4 * q + i)
                    if q >= 1:
                        values(r, l, p, q - 1)
                    if q >= 2:
                        turn_out(r, l, p, q - 2)
                if p == 0:
                    maxima(r, l, 1)
                values(r, l, p, NQUAD - 1)
                turn_out(r, l, p, NQUAD - 2)
                turn_out(r, l, p, NQUAD - 1)
                pe.wait_ge(norm_done, quad_no(r, l, p, NQUAD - 1) + 1)
                for t in range(2):
                    ins = tr(lane_ps[p][:, P * t:P * t + P], att[p][:, t, :], ident[:, :])
                ins.then_inc(attT_psum, 1)
                pe.wait_ge(attT_ready, r * 2 * LANES + l * LANES + p + 1)
                project(r, p, attT[p], wT[:, WO + l, :], 2 + l, y_psum)

            def ffn(r):
                for p in range(LANES):
                    zt(r, 2, p)
                for p in range(LANES):
                    pe.wait_ge(zT_ready, nth_zt(r, 2, p))
                    project(r, p, zT[p], w_hash[:, :], 4, lg_psum)
                for p in range(LANES):
                    pe.wait_ge(hot_ready, nth(r, p))
                    for t in range(2):
                        ins = tr(lane_ps[p][0:E, P * t:P * t + P], hot[p][:, t, :], ident[:, :])
                    ins.then_inc(hotT_psum, 1)
                for p in range(LANES):
                    pe.wait_ge(hotT_ready, nth(r, p))
                    pe.wait_ge(lg_exp, nth(r, p))
                    for e in range(E):
                        ins = mm(banks[e // 2][:, S * (e % 2):S * (e % 2) + S], selb[:, e, :], hotTb[p][:, :],
                                 start=True, stop=True)
                        if e % 2 == 1:
                            ins.then_inc(bc_psum, 1)
                    pe.wait_ge(zm_ready, nth(r, p, E // 2))
                    for t in range(2):
                        y = lane_ps[p][:, S + P * t:S + P * t + P]
                        mm(y, hotT[p][:, P * t:P * t + P], b_exp[:, :], start=True, stop=False)
                        for e in range(E):
                            ins = mm(y, zm[:, e, P * t:P * t + P], w_exp[:, e, :], start=False, stop=(e == E - 1))
                    ins.then_inc(y_psum, 1)

            def sign_attention(r):
                for p in range(LANES):
                    zt(r, 3, p)
                for p in range(LANES):
                    pe.wait_ge(qb_ready, nth(r, p))
                    mm(lane_ps[p][:, 0:S], kb[p][:, 0:P], qb[p][:, :], start=True, stop=True)
                    mm(lane_ps[p][:, S:S + P], kb[p][:, P:S], qb[p][:, P:S], start=True, stop=True).then_inc(sg_psum, 1)
                for p in range(LANES):
                    pe.wait_ge(aw_ready, nth(r, p))
                    mm(lane_ps[p][:, S:S + P], aw[p][:, 0:P], z[p][:, 0, :], start=True, stop=True)
                    mm(lane_ps[p][:, S + P:2 * S], aw[p][:, P:S], z[p][:, 0, :], start=True, stop=False)
                    mm(lane_ps[p][:, S + P:2 * S], aw[p][:, S:384], z[p][:, 1, :], start=False, stop=True).then_inc(y_psum, 1)

            rounds(pe, body)

            pe.wait_ge(z_ready, NLN * B)
            for j in range(4):
                for k in range(4):
                    ins = tr(banks[j][:, P * k:P * k + P], z6[:, 4 * j + k, :], ident[:, :])
                ins.then_inc(zT6_psum, 1)
            for c in range(NT):
                if c % 4 == 0:
                    pe.wait_ge(zT6_ready, c // 4 + 1)
                ins = mm(o_ps[:, 0:P], wg_pad[:, 120 - E * c:248 - E * c], zT6[:, c, :], start=(c == 0), stop=(c == NT - 1))
            ins.then_inc(gate_psum, 1)
            pe.wait_ge(cmax_ready, 1)
            tr(t_ps[0:1, 0:P], g[:, 0:1], ident[:, :]).then_inc(cmaxT_psum, 1)
            pe.wait_ge(m8_ready, 1)
            mm(t_ps[:, 128:129], m8[0:1, P:2 * P], ones[0:1, 0:1], start=True, stop=True)
            mm(t_ps[:, 136:136 + E], ones[0:1, :], m8[0:1, P:P + E], start=True, stop=True).then_inc(mbc_psum, 1)
            for b in range(32):
                pe.wait_ge(cnt_ready, b + 1)
                mm(o_ps[:, 256:257], blockb[:, :], cntb[:, 0:1], start=True, stop=True).then_inc(tot_psum, 1)
            pe.wait_ge(ties_ready, 1)
            mm(t_ps[:, 144:145], blockf[:, :], g[:, 20:21], start=True, stop=True)
            mm(t_ps[:, 148:149], below[:, :], cum[:, P - 1:P], start=True, stop=True).then_inc(ties_psum, 1)
            pe.wait_ge(sel_ready, 1)
            mm(t_ps[:, 152:153], below[:, :], cum[:, P - 1:P], start=True, stop=True)
            mm(t_ps[:, 160:160 + E], ones[:, :], g[:, 24:24 + E], start=True, stop=True).then_inc(sel_psum, 1)
            pe.wait_ge(pos_ready, 1)
            tr(t_ps[:, 256:384], pos[:, :], ident[:, :]).then_inc(pos_psum, 1)
            for n in range(E * NT):
                e, c = n // NT, n % NT
                pe.wait_ge(onehot_ready, n + 1)
                for i in range(2):
                    ins = mm(st_ps[i][:, 2 * e:2 * e + 2], onehot[n % 8][:, P * i:P * i + P], tokid[:, c, :],
                             start=(c == 0), stop=(c == NT - 1))
                ins.then_inc(onehot_used, 1)

            def down(e):
                pe.wait_ge(hT_ready, e + 1)
                if e >= 2:
                    pe.wait_ge(y_ready, e - 1)
                for i in range(2):
                    for t in range(2):
                        ins = mm(quad_ps[e % 2][:, P * i:P * i + P], hT[e % 2][:, t, P * i:P * i + P],
                                 w2T[:, 2 * e + t, :], start=(t == 0), stop=(t == 1))
                ins.then_inc(down_psum, 1)

            pe.wait_ge(ids_ready, E)
            for e in range(E):
                for i in range(2):
                    pe.wait_ge(gathered[2 * e + i], 16)
                if e >= 2:
                    pe.wait_ge(wslot_ready, e - 1)
                for i in range(2):
                    ins = tr(lane_ps[e % 2][:, P * i:P * i + P], xg[:, 2 * e + i, :], ident[:, :])
                ins.then_inc(xgT_psum, 1)
                pe.wait_ge(xgT_ready, e + 1)
                for i in range(2):
                    ins = mm(lane_ps[e % 2][:, S + i:S + i + 1], xgT[:, 2 * e + i, :], wg_pad[:, 120 + e:121 + e],
                             start=True, stop=True)
                ins.then_inc(ws_psum, 1)
            for e in range(E):
                if e >= 2:
                    pe.wait_ge(hT_ready, e - 1)
                for t in range(2):
                    mm(score_ps[e % 2][:, S * t:S * t + S], w1T[:, 2 * e + t, :], xgT[:, 2 * e:2 * e + 2, :],
                       start=True, stop=True)
                    ins = mm(st_ps[e % 2][:, S * t:S * t + S], w3T[:, 2 * e + t, :], xgT[:, 2 * e:2 * e + 2, :],
                             start=True, stop=True)
                ins.then_inc(up_psum, 1)
                if e >= 1:
                    down(e - 1)
            down(E - 1)

        @block.vector
        def _(dve):
            n = [0]

            def link(ins):
                n[0] += 1
                ins.then_inc(dve_chain, 1)
                dve.wait_ge(dve_chain, n[0])

            ts, tt, stt = dve.tensor_scalar, dve.tensor_tensor, dve.scalar_tensor_tensor

            dve.wait_ge(ld_small, 16 * N_SMALL)
            ts(mask[:, :, :], maski[:, :, :], 0.0, None, ALU.not_equal).then_inc(dve_setup, 1)
            hdt = DT / 2
            v = [sv[:, i:i + 1] for i in range(32)]
            DR, NI, D2, T0, INV, AR, AI, CR, CI, Z0, M2, MH, RS, T1_, T2_, UR, UI, R = range(18)
            dve.memset(v[MH], -0.5)
            ts(v[NI], cols[:, CAI:CAI + 1], hdt, None, ALU.mult)
            link(ts(v[DR], cols[:, CAR:CAR + 1], -hdt, 1.0, ALU.mult, ALU.add))
            link(tt(v[T0], v[NI], v[NI], ALU.mult))
            link(stt(v[D2], v[DR], v[DR], v[T0], ALU.mult, ALU.add))
            link(dve.reciprocal(v[INV], v[D2]))
            link(ts(v[T1_], cols[:, CAR:CAR + 1], hdt, 1.0, ALU.mult, ALU.add))
            link(stt(v[T2_], v[T1_], v[DR], v[T0], ALU.mult, ALU.subtract))
            link(tt(v[AR], v[T2_], v[INV], ALU.mult))
            link(stt(v[AI], v[NI], 2.0, v[INV], ALU.mult, ALU.mult))
            rdt = DT ** 0.5
            link(stt(v[CR], v[DR], rdt, v[INV], ALU.mult, ALU.mult))
            link(stt(v[CI], v[NI], rdt, v[INV], ALU.mult, ALU.mult))
            link(tt(v[T0], v[AI], v[AI], ALU.mult))
            link(stt(v[T1_], v[AR], v[AR], v[T0], ALU.mult, ALU.add))
            link(ts(v[Z0], v[T1_], 0.0, None, ALU.is_equal))
            tt(v[M2], v[T1_], v[Z0], ALU.add).then_inc(tab_sq, 1)
            dve.wait_ge(tab_pow, 1)
            link(tt(v[T0], v[RS], v[RS], ALU.mult))
            link(tt(v[T0], v[T0], v[M2], ALU.mult))
            link(ts(v[T0], v[T0], -0.5, 1.5, ALU.mult, ALU.add))
            link(tt(v[RS], v[RS], v[T0], ALU.mult))
            link(stt(v[UR], v[AR], v[RS], v[Z0], ALU.mult, ALU.add))
            link(tt(v[UI], v[AI], v[RS], ALU.mult))
            link(tt(v[T0], v[AI], v[UI], ALU.mult))
            link(stt(v[R], v[AR], v[UR], v[T0], ALU.mult, ALU.add))
            dve.wait_ge(pool_const, 2)
            link(ts(rdec[:, :], rdec[:, :], v[R], None, ALU.mult))
            dve.memset(er[:, 0:1], 1.0)
            link(dve.memset(ei[:, 0:1], 0.0))
            w = 1
            while w < S:
                ts(stmp[:, 0:w], ei[:, 0:w], v[UI], None, ALU.mult)
                link(ts(stmp[:, P:P + w], er[:, 0:w], v[UI], None, ALU.mult))
                stt(er[:, w:2 * w], er[:, 0:w], v[UR], stmp[:, 0:w], ALU.mult, ALU.subtract)
                link(stt(ei[:, w:2 * w], ei[:, 0:w], v[UR], stmp[:, P:P + w], ALU.mult, ALU.add))
                tt(v[T0], v[UI], v[UI], ALU.mult)
                link(stt(v[T1_], v[UR], 2.0, v[UI], ALU.mult, ALU.mult))
                link(stt(v[UR], v[UR], v[UR], v[T0], ALU.mult, ALU.subtract))
                link(dve.tensor_copy(v[UI], v[T1_]))
                w *= 2
            link(ts(esin[:, :], ei[:, :], -1.0, None, ALU.mult))
            link(ts(stmp[:, :], ei[:, :], v[CI], None, ALU.mult))
            link(stt(t1[:, :], er[:, :], v[CR], stmp[:, :], ALU.mult, ALU.subtract))
            link(ts(stmp[:, :], er[:, :], v[CI], None, ALU.mult))
            link(stt(t2[:, :], ei[:, :], v[CR], stmp[:, :], ALU.mult, ALU.add))
            link(ts(t2[:, :], t2[:, :], -1.0, None, ALU.mult))
            for i in range(1, NTURN, 2):
                dve.wait_ge(setup_ps, i + 1)
                dve.tensor_copy(turn[i][1], banks[i % 6][:, :].rearrange("p (i c) -> p i c", c=P)).then_inc(setup_dve, 1)
            dve.wait_ge(setup_ps, NTURN + 2)
            dve.wait_ge(pool_step, POOL_SETUP)
            dve.tensor_copy(wg_pad[:, 120:128], o_ps[:, 0:E])
            dve.tensor_copy(svb[:, :], o_ps[:, 256:384])
            ts(mbar[:, :, :], t_ps[:, :].rearrange("p (t q) -> p t q", t=2), -1.0, 1.0, ALU.mult, ALU.add)
            ts(mbias[:, :, :], t_ps[:, :].rearrange("p (t q) -> p t q", t=2), -1.0, -BIG, ALU.add, ALU.mult)
            dve.wait_ge(act_setup, 1)
            tt(sgn[:, 2:3], sgn[:, 0:1], sgn[:, 1:2], ALU.mult).then_inc(dve_setup, 1)
            dve.wait_ge(dve_setup, 2)
            dve.wait_ge(ld_x, 16)

            def quad_no(r, l, p, q):
                return ((r * 2 + l) * LANES + p) * NQUAD + q

            def norm(r, i):
                for p in range(LANES):
                    x = xs(r, p)
                    dve.bn_stats(stat[p][:, 0, :], x[:, 0, :])
                    link(dve.bn_stats(stat[p][:, 1, :], x[:, 1, :]))
                    dve.bn_aggr(mv[p][:, 0, :], stat[p][:, 0, :])
                    dve.bn_aggr(mv[p][:, 1, :], stat[p][:, 1, :]).then_inc(ln_stats, 1)
                for p in range(LANES):
                    x = xs(r, p)
                    o = z6s(r, p) if i == NLN - 1 else z[p]
                    dve.wait_ge(ln_rstd, nth_ln(r, i, p))
                    for t in range(2):
                        ins = ts(o[:, t, :], x[:, t, :], mv[p][:, t, 0:1], rstd[p][:, 2 + t:3 + t], ALU.subtract, ALU.mult)
                    ins.then_inc(z_ready, 1)

            def y_no(r, i, p):
                return (r * 5 + i) * LANES + p + 1

            def residual(r, i, p):
                dve.wait_ge(y_psum, y_no(r, i, p))
                link(tt(xs(r, p), xs(r, p), lane_ps[p][:, S:2 * S].rearrange("p (t d) -> p t d", t=2), ALU.add))

            def split(p, src, bias, done):
                link(ts(parts[p][:, 0, :], src, bias, None, ALU.add))
                link(stt(rest[p][:, :], src, bias, parts[p][:, 0, :], ALU.add, ALU.subtract))
                link(dve.tensor_copy(parts[p][:, 1, :], rest[p][:, :]))
                tt(parts[p][:, 2, :], rest[p][:, :], parts[p][:, 1, :], ALU.subtract).then_inc(done, 1)

            def maximum(r, l, p, u):
                k = tile_no(r, l, p, u)
                qt, pair = u // 8, u % 8
                dve.wait_ge(s_psum, k + 1)
                s2 = score_ps[u % 2][:, :].rearrange("p (i k) -> p i k", i=2)
                if l == 0:
                    dve.tensor_reduce(mx[p][:, qt, 2 * pair:2 * pair + 2], s2, AX.X, ALU.max).then_inc(s_maxed, 1)
                else:
                    for i in range(2):
                        h = 2 * pair + i
                        ins = dve.tensor_tensor_reduce(junk[:, u % 2, i, :], s2[:, i, :], mask[:, qt, :], 1.0, -3.0e38,
                                                       ALU.mult, ALU.max, mx[p][:, qt, h:h + 1])
                    ins.then_inc(s_maxed, 1)

            def split_max(r, l, p):
                if l == 1:
                    dve.wait_ge(s_maxed, tile_no(r, l, p, NTILE - 1) + 1)
                    ts(emx[p][:, :, :], mx[p][:, :, :], -SCALE, -1.0e-9, ALU.mult, ALU.min).then_inc(m_neg, 1)
                dve.wait_ge(mT_psum, r * 2 * LANES + l * LANES + p + 1)
                src = lane_ps[p][0:H, 0:S]
                link(ts(mparts[p][:, 0, :], src, -1.0, None, ALU.mult))
                link(stt(mrest[p][:, :], src, -1.0, mparts[p][:, 0, :], ALU.mult, ALU.subtract))
                link(dve.tensor_copy(mparts[p][:, 1, :], mrest[p][:, :]))
                tt(mparts[p][:, 2, :], mrest[p][:, :], mparts[p][:, 1, :], ALU.subtract).then_inc(m_split, 1)

            def normalise(r, l, p, q):
                k = quad_no(r, l, p, q)
                dve.wait_ge(t_psum, k + 1)
                wait(dve, norm_done, k - 1)
                onum, orec = onums[q % 2], orecs[q % 2]
                t4 = quad_ps[q % 2][:, S:2 * S].rearrange("p (t j c) -> p t j c", t=2, j=4)
                num, den = t4[:, :, :, 0:HD], t4[:, :, :, HD]
                if l == 1:
                    dve.wait_ge(emx_ready, nth(r, p))
                    link(tt(onum[:, :, :, :], mvx[p][:, :, 4 * q:4 * q + 4, :],
                            emx[p][:, :, 4 * q:4 * q + 4].unsqueeze(3).to_broadcast([P, 2, 4, 9]), ALU.mult))
                    link(tt(onum[:, :, :, :], t4[:, :, :, 0:9], onum[:, :, :, :], ALU.add))
                    num, den = onum[:, :, :, 0:HD], onum[:, :, :, HD]
                link(dve.reciprocal(orec[:, :, :], den))
                tt(att[p][:, :, 32 * q:32 * q + 32].rearrange("p t (j d) -> p t j d", d=HD), num,
                   orec[:, :, :].unsqueeze(3).to_broadcast([P, 2, 4, HD]), ALU.mult).then_inc(norm_done, 1)

            def attention(r, l):
                for p in range(LANES):
                    if l == 0:
                        dve.wait_ge(k_stored[p], 16 * (2 * r + 2))
                    else:
                        dve.wait_ge(q_stored[p], 16 * (2 * r + 1))
                    dve.wait_ge(q_psum, r * 2 * LANES + l * LANES + p + 1)
                    split(p, lane_ps[p][:, S:2 * S], cols[:, CQ + l:CQ + l + 1], q_split)
                for u in range(NTILE):
                    maximum(r, l, 0, u)
                split_max(r, l, 0)
                for q in range(NQUAD):
                    for i in range(4):
                        maximum(r, l, 1, 4 * q + i)
                    if q >= 2:
                        normalise(r, l, 0, q - 2)
                split_max(r, l, 1)
                for q in range(2, NQUAD):
                    normalise(r, l, 0, q)
                residual(r, 1 + 3 * l, 0)
                for q in range(NQUAD):
                    normalise(r, l, 1, q)
                residual(r, 1 + 3 * l, 1)

            def hashed_ffn(r):
                norm(r, 2)
                for p in range(LANES):
                    lg = lexp[p]
                    dve.wait_ge(lg_copied, nth(r, p))
                    link(dve.tensor_reduce(lmax[p][:, 0:2], lg[:, :, :], AX.X, ALU.max))
                    ts(lmax[p][:, 2:4], lmax[p][:, 0:2], -1.0, None, ALU.mult).then_inc(lg_max, 1)
                    for t in range(2):
                        ins = stt(rest[p][:, P * t:P * t + P], lg[:, t, :], lmax[p][:, t:t + 1], iota_rev[:, :],
                                  ALU.is_ge, ALU.mult)
                    link(ins)
                    link(dve.tensor_reduce(stat[p][:, 0, 0:2], rest[p][:, :].rearrange("p (t d) -> p t d", t=2),
                                           AX.X, ALU.max))
                    for t in range(2):
                        ins = ts(ytmp[p][:, P * t:P * t + P], iota_rev[:, :], stat[p][:, 0, t:t + 1], None, ALU.is_equal)
                    link(ins)
                    dve.tensor_reduce(hot[p][:, :, :], ytmp[p][:, :].rearrange("p (t g e) -> p t e g", t=2, e=E),
                                      AX.X, ALU.max).then_inc(hot_ready, 1)
                for p in range(LANES):
                    dve.wait_ge(lg_exp, nth(r, p))
                    link(dve.reciprocal(lmax[p][:, 6:8], lmax[p][:, 4:6]))
                    for j in range(E // 2):
                        dve.wait_ge(bc_psum, nth(r, p, E // 2, j + 1))
                        if j == 0:
                            wait(dve, y_psum, y_no(r, 2, 0) if p == 1 else 0)
                        tt(zm[:, 2 * j:2 * j + 2, :], zT[p][:, :].unsqueeze(1).to_broadcast([P, 2, S]),
                           banks[j][:, :].rearrange("p (i k) -> p i k", i=2), ALU.mult).then_inc(zm_ready, 1)
                    dve.wait_ge(y_psum, y_no(r, 2, p))
                    for t in range(2):
                        ins = ts(ytmp[p][:, P * t:P * t + P], lane_ps[p][:, S + P * t:S + P * t + P], 0.0,
                                 lmax[p][:, 6 + t:7 + t], ALU.max, ALU.mult)
                    link(ins)
                    link(tt(xs(r, p), xs(r, p), ytmp[p][:, :].rearrange("p (t d) -> p t d", t=2), ALU.add))

            def sign_attention(r):
                norm(r, 3)
                for p in range(LANES):
                    dve.wait_ge(sign_ready, nth(r, p))
                    ts(qb[p][:, :], kb[p][:, :], sgn[:, 2:3], None, ALU.mult).then_inc(qb_ready, 1)
                for p in range(LANES):
                    dve.wait_ge(tanh_done, nth(r, p))
                    stt(aw[p][:, :], th[p][:, :], 1.0, halfmask[:, :], ALU.add, ALU.mult).then_inc(aw_ready, 1)
                for p in range(LANES):
                    dve.wait_ge(y_psum, y_no(r, 3, p))
                    link(tt(ytmp[p][:, :].rearrange("p (t d) -> p t d", t=2),
                            lane_ps[p][:, S:2 * S].rearrange("p (t d) -> p t d", t=2),
                            svb[:, :].unsqueeze(1).to_broadcast([P, 2, P]), ALU.mult))
                    link(tt(xs(r, p), xs(r, p), ytmp[p][:, :].rearrange("p (t d) -> p t d", t=2), ALU.add))

            def body(r):
                for l in range(2):
                    for p in range(LANES):
                        dve.wait_ge(k_psum, r * 2 * LANES + l * LANES + p + 1)
                        if l == 0:
                            wait(dve, q_stored[p], 16 * 2 * r)
                        else:
                            dve.wait_ge(k_stored[p], 16 * (2 * r + 1))
                        split(p, lane_ps[p][:, S:2 * S], cols[:, CK + l:CK + l + 1], k_split)
                norm(r, 0)
                for p in range(LANES):
                    dve.wait_ge(w_psum, nth(r, p))
                    tt(wa[p][:, 0, :], lane_ps[p][:, S:2 * S], er[:, :], ALU.mult)
                    link(tt(wa[p][:, 1, :], lane_ps[p][:, S:2 * S], esin[:, :], ALU.mult))
                    for i in range(2):
                        ins = dve.tensor_tensor_scan(ga[p][:, i, :], rdec[:, :], wa[p][:, i, :], 0.0, ALU.mult, ALU.add)
                    ins.then_inc(scan_done, 1)
                for p in range(LANES):
                    residual(r, 0, p)
                for l in range(2):
                    if l == 1:
                        hashed_ffn(r)
                        sign_attention(r)
                    norm(r, 1 + 3 * l)
                    attention(r, l)
                norm(r, NLN - 1)

            rounds(dve, body)

            dve.wait_ge(gate_psum, 1)
            link(dve.tensor_copy(sc[:, :], o_ps[:, 0:P]))
            dve.tensor_reduce(g[:, 0:1], sc[:, :], AX.X, ALU.max).then_inc(cmax_ready, 1)
            dve.wait_ge(cmaxT_psum, 1)
            link(dve.tensor_reduce(m8[0:1, 0:E], t_ps[0:1, 0:P].rearrange("p (c e) -> p e c", e=E), AX.X, ALU.max))
            ts(m8[0:1, P:2 * P].rearrange("p (c e) -> p c e", e=E), m8[0:1, 0:E].unsqueeze(1).to_broadcast([1, NT, E]),
               -1.0, None, ALU.mult).then_inc(m8_ready, 1)
            dve.wait_ge(mbc_psum, 1)
            dve.tensor_copy(nm8[:, :], t_ps[:, 136:136 + E])
            dve.tensor_copy(g[:, 2:3], t_ps[:, 128:129]).then_inc(nm_ready, 1)
            room = float(CAP) - 0.5

            def count(b, thr):
                ts(eq[:, :], sc[:, :], thr, None, ALU.is_ge, ALU.add, accum_out=cntb[:, 0:1]).then_inc(cnt_ready, 1)
                dve.wait_ge(tot_psum, 32 - b)

            count(31, 0.0)
            link(ts(U, o_ps[:, 256:257], room, -float(2 ** 31), ALU.is_ge, ALU.mult))
            link(ts(M, U, 31, -1, ALU.arith_shift_right, ALU.bitwise_xor))
            link(ts(M, M, -2 ** 31, None, ALU.bitwise_or))
            for b in range(30, -1, -1):
                link(ts(F, U, 2 ** b, None, ALU.bitwise_or))
                link(tt(F, F, M, ALU.bitwise_xor))
                count(b, F.bitcast(F32))
                link(ts(DB, o_ps[:, 256:257], room, float(2 ** b), ALU.is_ge, ALU.mult))
                link(tt(U, U, DB, ALU.bitwise_or))
            link(tt(F, U, M, ALU.bitwise_xor))
            thr = F.bitcast(F32)
            ts(sel[:, :], sc[:, :], thr, None, ALU.is_gt, ALU.add, accum_out=g[:, 20:21])
            link(ts(eq[:, :], sc[:, :], thr, None, ALU.is_equal))
            dve.tensor_tensor_scan(cum[:, :], ones[:, :], eq[:, :], 0.0, ALU.mult, ALU.add).then_inc(ties_ready, 1)
            dve.wait_ge(ties_psum, 1)
            ts(g[:, 4:5], t_ps[:, 144:145], -1.0, float(CAP), ALU.mult, ALU.add)
            link(dve.tensor_copy(g[:, 5:6], t_ps[:, 148:149]))
            link(ts(cum[:, :], cum[:, :], g[:, 5:6], g[:, 4:5], ALU.add, ALU.is_le))
            link(tt(eq[:, :], eq[:, :], cum[:, :], ALU.mult))
            link(tt(sel[:, :], sel[:, :], eq[:, :], ALU.add))
            dve.wait_ge(gate_exp, 1)
            dve.tensor_tensor_scan(cum[:, :], ones[:, :], sel[:, :], 0.0, ALU.mult, ALU.add)
            link(dve.tensor_tensor_reduce(eq[:, :], ex[:, :], sel[:, :], 1.0, 0.0, ALU.mult, ALU.add, g[:, 22:23]))
            ts(g[:, 24:24 + E], emask[:, :], g[:, 22:23], None, ALU.mult).then_inc(sel_ready, 1)
            dve.wait_ge(sel_psum, 1)
            dve.reciprocal(rs8[:, :], t_ps[:, 160:160 + E])
            link(dve.tensor_copy(g[:, 6:7], t_ps[:, 152:153]))
            link(stt(pos[:, :], cum[:, :], g[:, 6:7], sel[:, :], ALU.add, ALU.mult))
            ts(pos[:, :], pos[:, :], -1.0, None, ALU.add).then_inc(pos_ready, 1)
            dve.wait_ge(pos_psum, 1)
            link(dve.tensor_copy(posT[:, :], t_ps[:, 256:384]))
            for n_ in range(E * NT):
                e, c = n_ // NT, n_ % NT
                if n_ >= 8:
                    dve.wait_ge(onehot_used, n_ - 7)
                ts(onehot[n_ % 8], iota_slot[:, :], posT[:, E * c + e:E * c + e + 1], None, ALU.is_equal).then_inc(onehot_ready, 1)
                if c == NT - 1:
                    dve.wait_ge(onehot_used, n_ + 1)
                    for i in range(2):
                        ins = dve.tensor_copy(g[:, 40 + 2 * i:42 + 2 * i], st_ps[i][:, 2 * e:2 * e + 2])
                    link(ins)
                    for i in range(2):
                        ins = stt(ids[:, 2 * e + i:2 * e + i + 1], g[:, 41 + 2 * i:42 + 2 * i], float(P),
                                  g[:, 40 + 2 * i:41 + 2 * i], ALU.mult, ALU.add)
                    ins.then_inc(ids_ready, 1)

            def weigh(e):
                dve.wait_ge(down_psum, e + 1)
                dve.wait_ge(wslot_ready, e + 1)
                if e >= 2:
                    dve.wait_ge(scattered[0], 16 * (e - 1))
                    dve.wait_ge(scattered[1], 16 * (e - 1))
                for i in range(2):
                    ins = ts(ysc[e % 2][:, i, :], quad_ps[e % 2][:, P * i:P * i + P],
                             wslot[:, 2 * e + i:2 * e + i + 1], rs8[:, e:e + 1], ALU.mult, ALU.mult)
                ins.then_inc(y_ready, 1)

            for e in range(E):
                dve.wait_ge(silu_done, e + 1)
                if e >= 2:
                    dve.wait_ge(down_psum, e - 1)
                tt(hT[e % 2], act1[e % 2], st_ps[e % 2][:, :].rearrange("p (t c) -> p t c", t=2), ALU.mult).then_inc(hT_ready, 1)
                if e >= 1:
                    weigh(e - 1)
            weigh(E - 1)


_INS = ["x", "ctx_1024", "mask_SxS2_ik0", "L0_attn_A_real", "L0_attn_A_imag", "L0_attn_B", "L0_attn_C",
        "L0_xattn_Wq", "L0_xattn_bq", "L0_xattn_Wk", "L0_xattn_bk", "L0_xattn_Wv", "L0_xattn_bv", "L0_xattn_Wo",
        "L0_xattn_bo", "L0_ffn_Wg", "L0_ffn_bg", "L0_ffn_We", "L0_ffn_be", "L1_attn_bv_q", "L1_attn_bv_k",
        "L1_attn_bv_v", "L1_xattn_Wq", "L1_xattn_bq", "L1_xattn_Wk", "L1_xattn_bk", "L1_xattn_Wv", "L1_xattn_bv",
        "L1_xattn_Wo", "L1_xattn_bo", "L1_ffn_Wg", "L1_ffn_W1", "L1_ffn_W2", "L1_ffn_W3"]


def kernel(**inputs):
    import numpy as _np
    import concourse.bacc as _bacc
    from concourse import mybir as _mybir
    from concourse.bass_utils import run_bass_kernel_spmd as _run

    nc = _bacc.Bacc("TRN2", target_bir_lowering=False, num_devices=1)
    arrays, aps = {}, {}
    for name in _INS:
        arr = _np.ascontiguousarray(inputs[name])
        arrays[f"in_{name}"] = arr
        aps[name] = nc.dram_tensor(f"in_{name}", arr.shape, _mybir.dt.from_np(arr.dtype), kind="ExternalInput").ap()
    out = nc.dram_tensor("out", (B, S, D), F32, kind="ExternalOutput").ap()
    decoder(nc, aps, out)
    r = _run(nc, [arrays], core_ids=[0])
    return r.results[0]["out"]
```

```python
from contextlib import ExitStack

import concourse.bass as bass
from concourse import mybir

ALU = mybir.AluOpType
ACT = mybir.ActivationFunctionType
AX = mybir.AxisListType
F32 = mybir.dt.float32
BF16 = mybir.dt.bfloat16
I32 = mybir.dt.int32
U32 = mybir.dt.uint32

P = 128
B, S, D = 8, 256, 128
NT = B * S // P
H, HD = 16, 8
E = 8
HID = 256
CAP = B * S // E
LANES = 4
ROUNDS = B // LANES
NLN = 6
SCALE = 1.0 / float(HD) ** 0.5
BIG = -1.0e30
DT = 0.01
SPLITS = 6
MROW = SPLITS * HD
KROWS = MROW + 3
NTILE = 16
NQUAD = 4


def decoder(nc, a, out):
    ctx = ExitStack()
    with ctx:
        def sb(name, shape, dt=F32):
            return ctx.enter_context(nc.sbuf_tensor(name, shape, dt))

        def sem(name):
            return ctx.enter_context(nc.semaphore(name))

        def lanes(name, shape, dt=F32):
            return [sb(f"{name}{p}", shape, dt) for p in range(LANES)]

        def bank(name):
            return ctx.enter_context(nc.psum_tensor(name, [P, 512], F32))

        score_ps = [bank(f"score_ps{i}") for i in range(2)]
        st_ps = [bank(f"st_ps{i}") for i in range(2)]
        lane_ps = [bank(f"lane_ps{i}") for i in range(2)]
        o_ps, t_ps = bank("o_ps"), bank("t_ps")
        quad_ps = [o_ps, t_ps]
        banks = score_ps + st_ps + lane_ps + [o_ps, t_ps]
        work_ps = lane_ps + quad_ps
        value_ps = st_ps + score_ps

        def out_ps(p):
            return lane_ps[p % 2] if p < LANES - 1 else score_ps[0]


        ident = sb("ident", [P, P])
        identb = sb("identb", [P, P], BF16)
        ones = sb("ones", [P, P])
        iota_rev = sb("iota_rev", [P, P])
        iota_slot = sb("iota_slot", [P, CAP], BF16)
        tokid = sb("tokid", [P, NT, 2], BF16)
        halfmask = sb("halfmask", [P, 384])
        selb = sb("selb", [E, E, P], BF16)
        blockb = sb("blockb", [P, P], BF16)
        below = sb("below", [P, P])
        emask = sb("emask", [P, E])
        wT = sb("wT", [P, 10, P])
        WQ, WK, WV, WO, SB, SC = 0, 2, 4, 6, 8, 9
        w_hash = sb("w_hash", [P, P])
        w_exp = sb("w_exp", [P, E, P])
        b_exp = sb("b_exp", [E, P])
        rows = sb("rows", [1, 5, P])
        cols = sb("cols", [P, 12])
        CQ, CK, CAR, CAI, CSQ, CSK = 0, 2, 4, 5, 6, 7
        sgn = sb("sgn", [P, 4])
        svb = sb("svb", [P, P])
        wg_pad = sb("wg_pad", [P, 248])
        w1T = sb("w1T", [P, 2 * E, P])
        w3T = sb("w3T", [P, 2 * E, P])
        w2T = sb("w2T", [P, 2 * E, P])
        mask = sb("mask", [P, 2, S])
        mbar = sb("mbar", [P, 2, S])
        mbias = sb("mbias", [P, 2, S], BF16)
        blockf = sb("blockf", [P, P])
        er, ei = sb("er", [P, S]), sb("ei", [P, S])
        esin = ei
        t1, t2 = sb("t1", [P, S]), sb("t2", [P, S])
        rdec = sb("rdec", [P, S])
        sv = sb("sv", [P, 32])

        x_all = sb("x_all", [P, NT, D])
        z6 = sb("z6", [P, NT, D])
        nat = z6[:, 0:10, :]
        stat = lanes("stat", [P, 2, 6])
        mv = lanes("mv", [P, 2, 2])
        rstd = lanes("rstd", [P, 6])
        z = lanes("z", [P, 2, D])
        zT = lanes("zT", [P, S])
        probs_all = sb("probs_all", [P, 16, S])
        probs = [probs_all[:, 2 * i:2 * i + 2, :] for i in range(8)]
        zm = [probs_all[:, 0:E, :], probs_all[:, E:2 * E, :]]
        wa = [probs_all[:, 4 * p:4 * p + 2, :] for p in range(LANES)]
        ga = [probs_all[:, 4 * p + 2:4 * p + 4, :] for p in range(LANES)]
        ha = wa
        ytmp = lanes("ytmp", [P, S])
        parts = lanes("parts", [P, 3, S], BF16)
        rest = lanes("rest", [P, S])
        kst_all = sb("kst_all", [P, 2 * LANES * 8, S], BF16)
        kst = [[kst_all[:, 8 * (LANES * l + p):8 * (LANES * l + p) + 8, :] for p in range(LANES)] for l in range(2)]
        qst_all = sb("qst_all", [P, LANES * 8, S], BF16)
        qst = [qst_all[:, 8 * p:8 * p + 8, :] for p in range(LANES)]
        vx = [lanes(f"vx{l}_", [P, 2, H, 9]) for l in range(2)]
        mvx = lanes("mvx", [P, 2, H, 9])
        mx = lanes("mx", [P, 2, H])
        emx = lanes("emx", [P, 2, H])
        mparts = lanes("mparts", [H, 3, S], BF16)
        mrest = lanes("mrest", [H, S])
        maski = probs[0].bitcast(I32)
        stmp = probs_all[:, 2, :]
        wg_nat = probs_all[0:E, 3, 0:P]
        svrow, svs = probs_all[0:1, 4, 0:P], probs_all[0:1, 4, P:S]
        qk_perm = probs_all[0:1, 7:9, :].rearrange("p a (b n) -> p (a b) n", b=2)
        qk_rows = probs_all[0:1, 5:7, :].rearrange("p a (b n) -> p (a b) n", b=2)
        oT = [sb(f"oT{i}", [P, S]) for i in range(2)]
        onums = [sb(f"onum{i}", [P, 2, 4, 9]) for i in range(2)]
        orecs = [sb(f"orec{i}", [P, 2, 4]) for i in range(2)]
        turned = sb("turned", [P, 2 * LANES, S])
        ctxT = [turned[:, p, :] for p in range(LANES)]
        att = [t.rearrange("p (t d) -> p t d", t=2) for t in ctxT]
        attT = [turned[:, LANES + p, :] for p in range(LANES)]
        lexp = [t.rearrange("p (t d) -> p t d", t=2) for t in attT]
        lmax = lanes("lmax", [P, 8])
        hot = lanes("hot", [P, 2, E])
        hotT = [mrest[p][0:E, :] for p in range(LANES)]
        hotTb = [mparts[p][0:E, 0, :] for p in range(LANES)]
        kb = [parts[p][:, 0, :] for p in range(LANES)]
        qb = [parts[p][:, 1, :] for p in range(LANES)]
        th = lanes("th", [P, 384])
        ctx_in = [th[p][:, 0:S].rearrange("p (t d) -> p t d", t=2) for p in range(LANES)]
        aw = th
        junk = [[t[p][:, :].bitcast(BF16).rearrange("p (i k) -> p i k", i=2) for t in (ytmp, rest)] for p in range(LANES)]
        qst_f = qst_all[:, :, :].rearrange("p a n -> p (a n)").bitcast(F32)
        w1n = qst_f[:, 0:2 * E * P].rearrange("p (a n) -> p a n", n=P)
        w3n = qst_f[:, 2 * E * P:4 * E * P].rearrange("p (a n) -> p a n", n=P)
        w2n = turned

        kst_f = kst_all[:, :, :].rearrange("p a n -> p (a n)").bitcast(F32)
        zT6, xgT, xg = (kst_f[:, 2 * E * P * i:2 * E * P * (i + 1)].rearrange("p (a n) -> p a n", n=P) for i in range(3))
        sc, ex, eq, cum = er[:, 0:P], er[:, P:S], ei[:, 0:P], ei[:, P:S]
        sel, pos, posT = t1[:, 0:P], t1[:, P:S], t2[:, 0:P]
        g = sb("g", [P, 64])
        uthr = sb("uthr", [P, 4], I32)
        U, M, F, DB = (uthr[:, i:i + 1] for i in range(4))
        cntb = sb("cntb", [P, 2], BF16)
        m8 = ytmp[0][0:1, :]
        onehot = [probs_all[:, i, 0:CAP // 2].bitcast(BF16) for i in range(8)]
        ids = sb("ids", [P, 2 * E], I32)
        wslot = sb("wslot", [P, 2 * E])
        nm8 = sb("nm8", [P, E])
        rs8 = sb("rs8", [P, E])
        act1 = [probs_all[:, 8 + 2 * i:10 + 2 * i, :] for i in range(2)]
        hT = [probs_all[:, 12 + 2 * i:14 + 2 * i, :] for i in range(2)]
        ysc = [oT[i][:, :].rearrange("p (i c) -> p i c", i=2) for i in range(2)]

        def dram(name, shape, dt):
            return nc.dram_tensor(name, shape, dt, kind="Internal").ap()

        kscr = [[dram(f"kscr{l}{p}", (SPLITS, P, S), BF16) for p in range(LANES)] for l in range(2)]
        qscr = [dram(f"qscr{p}", (SPLITS, P, S), BF16) for p in range(LANES)]
        mscr = [dram(f"mscr{p}", (H, 3, S), BF16) for p in range(LANES)]
        zrows = dram("zrows", (B * S, D), F32)

        ld_small, ld_x, ld_moe = sem("ld_small"), sem("ld_x"), sem("ld_moe")
        pool_const, pool_step = sem("pool_const"), sem("pool_step")
        act_setup, dve_setup = sem("act_setup"), sem("dve_setup")
        setup_ps, setup_act, setup_dve = sem("setup_ps"), sem("setup_act"), sem("setup_dve")
        dve_chain = sem("dve_chain")
        tab_sq, tab_pow = sem("tab_sq"), sem("tab_pow")
        ctx_ld = [sem(f"ctx_ld{p}") for p in range(LANES)]
        ctxT_psum, ctxT_ready = sem("ctxT_psum"), sem("ctxT_ready")
        k_psum, k_split = sem("k_psum"), sem("k_split")
        v_psum, v_ready = sem("v_psum"), sem("v_ready")
        mv_psum, mv_ready = sem("mv_psum"), sem("mv_ready")
        k_stored = [sem(f"k_stored{p}") for p in range(LANES)]
        k_stacked = [sem(f"k_stacked{p}") for p in range(LANES)]
        ln_stats, ln_rstd, z_ready = sem("ln_stats"), sem("ln_rstd"), sem("z_ready")
        zT_psum, zT_ready = sem("zT_psum"), sem("zT_ready")
        w_psum, scan_done, h_ready = sem("w_psum"), sem("scan_done"), sem("h_ready")
        y_psum, resid = sem("y_psum"), sem("resid")
        q_psum, q_split = sem("q_psum"), sem("q_split")
        q_stored = [sem(f"q_stored{p}") for p in range(LANES)]
        q_stacked = [sem(f"q_stacked{p}") for p in range(LANES)]
        s_psum, s_maxed = sem("s_psum"), sem("s_maxed")
        mT_psum, m_split = sem("mT_psum"), sem("m_split")
        m_neg, emx_ready = sem("m_neg"), sem("emx_ready")
        m_stored = [sem(f"m_stored{p}") for p in range(LANES)]
        m_stacked = [sem(f"m_stacked{p}") for p in range(LANES)]
        st_psum, exp_done = sem("st_psum"), sem("exp_done")
        pv_done, o_evac = sem("pv_done"), sem("o_evac")
        t_psum, norm_done = sem("t_psum"), sem("norm_done")
        attT_psum, attT_ready = sem("attT_psum"), sem("attT_ready")
        lg_psum, lg_copied, lg_max, lg_exp = sem("lg_psum"), sem("lg_copied"), sem("lg_max"), sem("lg_exp")
        hot_ready, hotT_psum, hotT_ready = sem("hot_ready"), sem("hotT_psum"), sem("hotT_ready")
        bc_psum, zm_ready = sem("bc_psum"), sem("zm_ready")
        sign_ready, qb_ready, sg_psum = sem("sign_ready"), sem("qb_ready"), sem("sg_psum")
        tanh_done, aw_ready = sem("tanh_done"), sem("aw_ready")
        rows_out = sem("rows_out")
        zT6_psum, zT6_ready, gate_psum = sem("zT6_psum"), sem("zT6_ready"), sem("gate_psum")
        cmax_ready, cmaxT_psum, m8_ready, mbc_psum = sem("cmax_ready"), sem("cmaxT_psum"), sem("m8_ready"), sem("mbc_psum")
        nm_ready, gate_exp = sem("nm_ready"), sem("gate_exp")
        cnt_ready, tot_psum = sem("cnt_ready"), sem("tot_psum")
        ties_ready, ties_psum = sem("ties_ready"), sem("ties_psum")
        sel_ready, sel_psum = sem("sel_ready"), sem("sel_psum")
        pos_ready, pos_psum = sem("pos_ready"), sem("pos_psum")
        onehot_ready, onehot_used, ids_ready = sem("onehot_ready"), sem("onehot_used"), sem("ids_ready")
        gathered = [sem(f"gathered{i}") for i in range(2 * E)]
        xgT_psum, xgT_ready, ws_psum, wslot_ready = sem("xgT_psum"), sem("xgT_ready"), sem("ws_psum"), sem("wslot_ready")
        up_psum, silu_done, hT_ready = sem("up_psum"), sem("silu_done"), sem("hT_ready")
        down_psum, y_ready = sem("down_psum"), sem("y_ready")
        scattered = [sem(f"scattered{i}") for i in range(2)]

        block = ctx.enter_context(nc.Block())

        def nth(r, p, n=1, k=None):
            return (LANES * r + p) * n + (n if k is None else k)

        def nth_ln(r, i, p):
            return r * NLN * LANES + i * LANES + p + 1

        def nth_zp(r, i, p):
            return r * (NLN - 1) * LANES + i * LANES + p + 1

        def y_no(r, i, p):
            return (r * 5 + i) * LANES + p + 1

        def tile_no(r, l, p, u):
            return ((r * 2 + l) * LANES + p) * NTILE + u

        def wait(eng, s, v):
            if isinstance(v, int) and v <= 0:
                return
            eng.wait_ge(s, v)

        def head_at(h):
            return 64 * (h // 8), h % 8

        def xs(r, p):
            return x_all[:, bass.ds(2 * (LANES * r + p), 2), :] if not isinstance(r, int) else \
                x_all[:, 2 * (LANES * r + p):2 * (LANES * r + p) + 2, :]

        def z6s(r, p):
            t = 2 * (LANES * r + p)
            return z6[:, bass.ds(t, 2), :] if not isinstance(r, int) else z6[:, t:t + 2, :]

        def rounds(eng, body):
            body(0)
            for r in range(1, ROUNDS):
                body(r)

        turn = [([nat[:, i, :] for i in range(4 * j, 4 * j + 4)], wT[:, 4 * j:4 * j + 4, :]) for j in range(2)]
        turn.append(([nat[:, 8, :], nat[:, 9, :]], wT[:, 8:10, :]))
        for src, dst in ((w1n, w1T), (w3n, w3T)):
            turn += [([src[:, i, :] for i in range(4 * j, 4 * j + 4)], dst[:, 4 * j:4 * j + 4, :]) for j in range(4)]
        turn += [([w2n[:, 2 * j + i // 2, P * (i % 2):P * (i % 2) + P] for i in range(4)],
                  w2T[:, 4 * j:4 * j + 4, :]) for j in range(4)]
        NSMALL = 3
        N_SMALL = 15 + 4 + 6 + 4
        POOL_SETUP = 34 + 7 * LANES
        NTURN = len(turn)

        @block.sync
        def _(sp):
            small = [
                (nat[:, WQ, :], a["L0_xattn_Wq"]), (nat[:, WQ + 1, :], a["L1_xattn_Wq"]),
                (nat[:, WK, :], a["L0_xattn_Wk"]), (nat[:, WK + 1, :], a["L1_xattn_Wk"]),
                (nat[:, WV, :], a["L0_xattn_Wv"]), (nat[:, WV + 1, :], a["L1_xattn_Wv"]),
                (nat[:, WO, :], a["L0_xattn_Wo"]), (nat[:, WO + 1, :], a["L1_xattn_Wo"]),
                (nat[:, SB, :], a["L0_attn_B"]), (nat[:, SC, :], a["L0_attn_C"]),
                (w_hash[:, :], a["L0_ffn_Wg"]), (w_exp[:, :, :], a["L0_ffn_We"].rearrange("e d f -> d e f")),
                (b_exp[:, :], a["L0_ffn_be"]), (wg_nat, a["L1_ffn_Wg"]),
                (maski, a["mask_SxS2_ik0"].rearrange("(t p) k -> p t k", p=P)),
            ]
            for i, n in enumerate(("L0_xattn_bq", "L1_xattn_bq", "L0_xattn_bk", "L1_xattn_bk")):
                small.append((qk_rows[:, i, :], a[n].rearrange("(o n) -> o n", o=1)))
            for i, n in enumerate(("L0_xattn_bv", "L1_xattn_bv", "L0_xattn_bo", "L1_xattn_bo", "L0_ffn_bg")):
                small.append((rows[0:1, i, :], a[n].rearrange("(o n) -> o n", o=1)))
            small.append((svrow, a["L1_attn_bv_v"].rearrange("(o n) -> o n", o=1)))
            for c, n in ((CAR, "L0_attn_A_real"), (CAI, "L0_attn_A_imag"), (CSQ, "L1_attn_bv_q"), (CSK, "L1_attn_bv_k")):
                small.append((cols[:, c:c + 1], a[n].rearrange("(n o) -> n o", o=1)))
            assert len(small) == N_SMALL
            for dst, src in small:
                sp.dma_start(dst, src).then_inc(ld_small, 16)
            sp.dma_start(x_all[:, :, :], a["x"].rearrange("b (t p) d -> p (b t) d", p=P)).then_inc(ld_x, 16)
            sp.dma_start(w1n[:, :, :], a["L1_ffn_W1"].rearrange("e (t p) c -> p (e t) c", p=P)).then_inc(ld_moe, 16)
            sp.dma_start(w3n[:, :, :], a["L1_ffn_W3"].rearrange("e (t p) c -> p (e t) c", p=P)).then_inc(ld_moe, 16)
            sp.dma_start(w2n[:, :, :], a["L1_ffn_W2"].rearrange("e c h -> c e h")).then_inc(ld_moe, 16)

            K_PARTS, Q_PARTS = ((0, 0, 0), (1, 1), (2,)), ((0, 1, 2), (0, 1), (0,))

            def store_parts(p, scr, plan, s):
                slot = 0
                for run in plan:
                    n = len(run)
                    src = parts[p][:, run[0]:run[0] + 1, :].to_broadcast([P, n, S]) if run[0] == run[-1] else \
                        parts[p][:, 0:n, :]
                    sp.dma_start(scr[slot:slot + n].rearrange("s p n -> p s n"), src).then_inc(s, 16)
                    slot += n

            def load_stack(dst, scr, s):
                rows_ = scr.rearrange("s (d e t) n -> e (s d) t n", d=HD, e=2)
                for e in range(2):
                    sp.dma_start(dst[64 * e:64 * e + MROW, :, :], rows_[e]).then_inc(s, 16)

            def stack_q(r, l, p):
                sp.wait_ge(q_stored[p], 16 * 3 * (2 * r + l + 1))
                load_stack(qst[p], qscr[p], q_stacked[p])

            def body(r):
                for p in range(LANES):
                    if r > 0:
                        sp.wait_ge(y_psum, y_no(r - 1, 3, p))
                    sp.dma_start(ctx_in[p][:, :, :],
                                 a["ctx_1024"][LANES * r + p].rearrange("(t p) d -> p t d", p=P)).then_inc(ctx_ld[p], 16)
                for l in range(2):
                    for p in range(LANES):
                        sp.wait_ge(k_split, nth(r, p) + l * LANES + r * LANES)
                        store_parts(p, kscr[l][p], K_PARTS, k_stored[p])
                    for p in range(LANES):
                        sp.wait_ge(k_stored[p], 16 * 3 * (2 * r + l + 1))
                        load_stack(kst[l][p], kscr[l][p], k_stacked[p])
                for l in range(2):
                    for p in range(LANES):
                        sp.wait_ge(q_split, nth(r, p) + l * LANES + r * LANES)
                        store_parts(p, qscr[p], Q_PARTS, q_stored[p])
                        if p > 0:
                            stack_q(r, l, p - 1)
                    stack_q(r, l, LANES - 1)
                    for p in range(LANES):
                        sp.wait_ge(m_split, nth(r, p) + l * LANES + r * LANES)
                        sp.dma_start(mscr[p], mparts[p][:, :, :]).then_inc(m_stored[p], 16)
                        sp.wait_ge(m_stored[p], 16 * (2 * r + l + 1))
                        for e in range(2):
                            sp.dma_start(qst[p][64 * e + MROW:64 * e + KROWS, :, :],
                                         mscr[p][8 * e:8 * e + 8].rearrange("t j n -> j t n")).then_inc(m_stacked[p], 16)

            rounds(sp, body)
            sp.wait_ge(z_ready, NLN * B)
            sp.dma_start(zrows.rearrange("(t p) d -> p t d", p=P), z6[:, :, :]).then_inc(rows_out, 16)
            sp.dma_start(out.rearrange("b (t p) d -> p (b t) d", p=P), x_all[:, :, :]).then_inc(rows_out, 16)
            sp.wait_ge(rows_out, 32)
            for i in range(2):
                sp.wait_ge(scattered[i], 16 * E)


        @block.gpsimd
        def _(pool):
            n = [0]

            def step(ins):
                n[0] += 1
                ins.then_inc(pool_step, 1)
                pool.wait_ge(pool_step, n[0])

            step(pool.memset(ident[:, :], 0.0))
            step(pool.affine_select(out=ident[:, :], in_=ident[:, :], compare_op=ALU.not_equal, fill=1.0,
                                    base=0, pattern=[[-1, P]], channel_multiplier=1))
            pool.memset(ones[:, :], 1.0).then_inc(pool_const, 1)
            step(pool.tensor_copy(identb[:, :], ident[:, :]))
            step(pool.iota(iota_rev[:, :], pattern=[[-1, P]], base=P, channel_multiplier=0,
                           allow_small_or_imprecise_dtypes=True))
            step(pool.iota(iota_slot[:, :], pattern=[[1, CAP]], base=0, channel_multiplier=0,
                           allow_small_or_imprecise_dtypes=True))
            step(pool.iota(tokid[:, :, 0], pattern=[[0, NT]], base=0, channel_multiplier=1,
                           allow_small_or_imprecise_dtypes=True))
            step(pool.iota(tokid[:, :, 1], pattern=[[1, NT]], base=0, channel_multiplier=0,
                           allow_small_or_imprecise_dtypes=True))
            step(pool.memset(halfmask[:, :], 0.5))
            for c in (0, 256):
                step(pool.affine_select(out=halfmask[:, c:c + P], in_=halfmask[:, c:c + P], compare_op=ALU.is_ge,
                                        fill=0.0, base=0, pattern=[[1, P]], channel_multiplier=-1))
            step(pool.memset(selb[:, :, :], 0.0))
            step(pool.affine_select(out=selb[:, :, :], in_=selb[:, :, :], compare_op=ALU.not_equal, fill=1.0,
                                    base=0, pattern=[[-1, E], [0, P]], channel_multiplier=1))
            step(pool.memset(emask[:, :], 0.0))
            for i in range(NT):
                step(pool.affine_select(out=emask[:, :], in_=emask[:, :], compare_op=ALU.not_equal, fill=1.0,
                                        base=-E * i, pattern=[[-1, E]], channel_multiplier=1))
            step(pool.tensor_copy(below[:, :].rearrange("p (c e) -> p c e", e=E),
                                  emask[:, :].unsqueeze(1).to_broadcast([P, NT, E])))
            step(pool.tensor_copy(blockf[:, :], below[:, :]))
            step(pool.tensor_copy(blockb[:, :], below[:, :]))
            step(pool.affine_select(out=below[:, :].rearrange("p (c e) -> p c e", e=E),
                                    in_=below[:, :].rearrange("p (c e) -> p c e", e=E), compare_op=ALU.is_gt,
                                    fill=0.0, base=0, pattern=[[E, NT], [0, E]], channel_multiplier=-1))
            step(pool.memset(wg_pad[:, :], 0.0))
            for p in range(LANES):
                for l in range(2):
                    for e in range(2):
                        at = 8 * S // 2 * (LANES * l + p)
                        step(pool.memset(kst_f[64 * e + 32:64 * e + 64, at:at + 8 * S // 2], 1.0 + 0x3F80 / float(2 ** 23)))
                    step(pool.memset(vx[l][p][:, :, :, :], 1.0))
                step(pool.memset(rstd[p][:, 4:6], -0.5))
            pool.memset(rdec[:, :], 1.0).then_inc(pool_const, 1)

            pool.wait_ge(tab_sq, 1)
            pool.tensor_tensor(sv[:, 12:13], sv[:, 10:11], sv[:, 11:12], ALU.pow).then_inc(tab_pow, 1)

            def norm(r, i, p):
                pool.wait_ge(ln_stats, nth_ln(r, i, p))
                step(pool.tensor_scalar(rstd[p][:, 0:2], mv[p][:, :, 1], 1e-5, None, ALU.add))
                pool.tensor_tensor(rstd[p][:, 2:4], rstd[p][:, 0:2], rstd[p][:, 4:6], ALU.pow).then_inc(ln_rstd, 1)

            def body(r):
                for i in range(NLN):
                    for p in range(LANES):
                        norm(r, i, p)
                    if i == 0:
                        for p in range(LANES):
                            pool.wait_ge(scan_done, nth(r, p))
                            pool.tensor_tensor(ha[p][:, 0, :], ga[p][:, 0, :], t1[:, :], ALU.mult)
                            pool.tensor_tensor(ha[p][:, 1, :], ga[p][:, 1, :], t2[:, :], ALU.mult).then_inc(h_ready, 1)

            rounds(pool, body)

            pool.wait_ge(rows_out, 32)
            for k in range(2 * E):
                pool.wait_ge(ids_ready, k // 2 + 1)
                pool.indirect_dma_start(out=xg[:, k, :], out_offset=None, in_=zrows[:, :],
                                        in_offset=bass.IndirectOffsetOnAxis(ap=ids[:, k:k + 1], axis=0)
                                        ).then_inc(gathered[k], 16)
            for e in range(E):
                pool.wait_ge(y_ready, e + 1)
                for i in range(2):
                    if e > 0:
                        pool.wait_ge(scattered[0], 16 * e)
                        pool.wait_ge(scattered[1], 16 * e)
                for i in range(2):
                    k = 2 * e + i
                    pool.indirect_dma_start(out=out.rearrange("b s d -> (b s) d"),
                                            out_offset=bass.IndirectOffsetOnAxis(ap=ids[:, k:k + 1], axis=0),
                                            in_=ysc[e % 2][:, i, :], in_offset=None, compute_op=ALU.add,
                                            ).then_inc(scattered[i], 16)

        @block.scalar
        def _(act):
            def copy(o, i):
                return act.activation(o, i, ACT.Copy)

            act.wait_ge(ld_small, 16 * N_SMALL)
            act.activation(sgn[:, 0:2], cols[:, CSQ:CSQ + 2], ACT.Sign)
            copy(qk_perm.rearrange("p k (d h) -> p k h d", d=HD), qk_rows.rearrange("p k (h d) -> p k h d", d=HD))
            act.activation(svs, svrow, ACT.Sign).then_inc(act_setup, 1)
            for i in range(0, NTURN, 2):
                act.wait_ge(setup_ps, i + 1)
                n = len(turn[i][0]) * P
                src, dst = banks[i % 6][:, 0:n].rearrange("p (k n) -> p k n", n=P), turn[i][1]
                if i == 0:
                    src = src.rearrange("p k (h d) -> p k h d", d=HD)
                    dst = dst.rearrange("p k (d h) -> p k h d", d=HD)
                copy(dst, src).then_inc(setup_act, 1)

            def zt(r, i, p):
                act.wait_ge(zT_psum, nth_zp(r, i, p))
                copy(zT[p][:, :], work_ps[p][:, 0:S]).then_inc(zT_ready, 1)

            def exps(r, l, p, v):
                n = tile_no(r, l, p, v)
                act.wait_ge(st_psum, n + 1)
                wait(act, pv_done, (n // 4 if isinstance(n, int) else quad_no(r, l, p, v // 4)) - 1)
                act.activation(probs[v % 8][:, :, :], st_ps[v % 2][:, :], ACT.Exp, scale=SCALE).then_inc(exp_done, 1)

            def quad_no(r, l, p, q):
                return ((r * 2 + l) * LANES + p) * NQUAD + q

            def evac(r, l, p, q):
                n = quad_no(r, l, p, q)
                act.wait_ge(pv_done, n + 1)
                wait(act, t_psum, n - 1)
                copy(oT[q % 2][:, :], quad_ps[q % 2][:, 0:S]).then_inc(o_evac, 1)

            def turned_out(r, l, p):
                act.wait_ge(attT_psum, r * 2 * LANES + l * LANES + p + 1)
                copy(attT[p], out_ps(p)[:, 0:S]).then_inc(attT_ready, 1)

            def body(r):
                for p in range(LANES):
                    act.wait_ge(ctxT_psum, nth(r, p))
                    copy(ctxT[p][:, :], work_ps[p][:, 0:S]).then_inc(ctxT_ready, 1)
                for l in range(2):
                    for p in range(LANES):
                        act.wait_ge(v_psum, r * 2 * LANES + l * LANES + p + 1)
                        copy(vx[l][p][:, :, :, 0:HD],
                             value_ps[p][:, 0:S].rearrange("p (t h d) -> p t h d", h=H, d=HD)).then_inc(v_ready, 1)
                for p in range(LANES):
                    act.wait_ge(mv_psum, nth(r, p))
                    copy(mvx[p][:, :, :, :], value_ps[p][:, 0:2 * H * 9]).then_inc(mv_ready, 1)
                for p in range(LANES):
                    zt(r, 0, p)
                for l in range(2):
                    if l == 1:
                        for p in range(LANES):
                            zt(r, 2, p)
                        for p in range(LANES):
                            act.wait_ge(lg_psum, nth(r, p))
                            copy(lexp[p][:, :, :], work_ps[p][:, S:2 * S]).then_inc(lg_copied, 1)
                        for p in range(LANES):
                            act.wait_ge(lg_max, nth(r, p))
                            for t in range(2):
                                ins = act.activation(th[p][:, P * t:P * t + P], lexp[p][:, t, :], ACT.Exp,
                                                     bias=lmax[p][:, 2 + t:3 + t], accum_out=lmax[p][:, 4 + t:5 + t])
                            ins.then_inc(lg_exp, 1)
                        for p in range(LANES):
                            act.wait_ge(hotT_psum, nth(r, p))
                            copy(hotT[p][:, :], work_ps[p][0:E, 0:S])
                            copy(hotTb[p][:, :], work_ps[p][0:E, 0:S]).then_inc(hotT_ready, 1)
                        for p in range(LANES):
                            act.wait_ge(zT_psum, nth_zp(r, 3, p))
                            act.activation(kb[p][:, :], work_ps[p][:, 0:S], ACT.Sign).then_inc(sign_ready, 1)
                        for p in range(LANES):
                            act.wait_ge(sg_psum, nth(r, p))
                            act.activation(th[p][:, :], work_ps[p][:, 0:384], ACT.Tanh,
                                           scale=2.0 / float(D) ** 0.5).then_inc(tanh_done, 1)
                    for p in range(LANES):
                        zt(r, 1 + 3 * l, p)
                    for p in range(LANES):
                        if l == 1:
                            act.wait_ge(m_neg, nth(r, p))
                            act.activation(emx[p][:, :, :], emx[p][:, :, :], ACT.Exp).then_inc(emx_ready, 1)
                        for q in range(NQUAD):
                            for i in range(4):
                                exps(r, l, p, 4 * q + i)
                            if q == 0 and p > 0:
                                turned_out(r, l, p - 1)
                            if q >= 1:
                                evac(r, l, p, q - 1)
                        evac(r, l, p, NQUAD - 1)
                    turned_out(r, l, LANES - 1)

            rounds(act, body)

            for j in range(4):
                act.wait_ge(zT6_psum, j + 1)
                copy(zT6[:, 4 * j:4 * j + 4, :], banks[j][:, :]).then_inc(zT6_ready, 1)
            act.wait_ge(nm_ready, 1)
            act.activation(ex[:, :], sc[:, :], ACT.Exp, bias=g[:, 2:3]).then_inc(gate_exp, 1)
            for e in range(E):
                act.wait_ge(xgT_psum, e + 1)
                copy(xgT[:, 2 * e:2 * e + 2, :], lane_ps[e % 2][:, 0:S]).then_inc(xgT_ready, 1)
                act.wait_ge(ws_psum, e + 1)
                act.activation(wslot[:, 2 * e:2 * e + 2], lane_ps[e % 2][:, S:S + 2], ACT.Exp,
                               bias=nm8[:, e:e + 1]).then_inc(wslot_ready, 1)
            for e in range(E):
                act.wait_ge(up_psum, e + 1)
                if e >= 2:
                    act.wait_ge(hT_ready, e - 1)
                act.activation(act1[e % 2], score_ps[e % 2][:, :], ACT.Silu).then_inc(silu_done, 1)

        @block.tensor
        def _(pe):
            mm = nc.tensor.matmul
            tr = nc.tensor.transpose
            pe.wait_ge(pool_const, 2)
            pe.wait_ge(pool_step, 5)
            pe.wait_ge(ld_small, 16 * N_SMALL)
            for i, (srcs, _) in enumerate(turn):
                if i == NSMALL:
                    pe.wait_ge(ld_moe, 48)
                if i >= 6:
                    j = i - 6
                    pe.wait_ge(setup_act if j % 2 == 0 else setup_dve, j // 2 + 1)
                for k, s in enumerate(srcs):
                    ins = tr(banks[i % 6][:, P * k:P * k + P], s, ident[:, :])
                ins.then_inc(setup_ps, 1)
            tr(o_ps[:, 0:E], wg_nat, ident[0:E, 0:E])
            pe.wait_ge(act_setup, 1)
            for i in range(4):
                mm(o_ps[:, E + i:E + i + 1], qk_perm[:, i, :], ones[0:1, 0:1], start=True, stop=True)
            mm(o_ps[:, 256:384], ones[0:1, :], svs, start=True, stop=True).then_inc(setup_ps, 1)
            pe.wait_ge(dve_setup, 1)
            for kt in range(2):
                for qt in range(2):
                    ins = tr(t_ps[:, S * kt + P * qt:S * kt + P * qt + P], mask[:, qt, P * kt:P * kt + P], ident[:, :])
            ins.then_inc(setup_ps, 1)
            pe.wait_ge(setup_act, (NTURN + 1) // 2)
            pe.wait_ge(setup_dve, NTURN // 2)
            pe.wait_ge(dve_setup, 2)

            def quad_no(r, l, p, q):
                return ((r * 2 + l) * LANES + p) * NQUAD + q

            def zt(r, i, p):
                pe.wait_ge(z_ready, nth_ln(r, i, p))
                for t in range(2):
                    ins = tr(work_ps[p][:, P * t:P * t + P], z[p][:, t, :], ident[:, :])
                ins.then_inc(zT_psum, 1)

            def score_tile(r, l, p, u):
                n = tile_no(r, l, p, u)
                if u == 0:
                    pe.wait_ge(q_stacked[p], 16 * 2 * (2 * r + l + 1))
                    if l == 0:
                        pe.wait_ge(k_stacked[p], 16 * 4 * (r + 1))
                wait(pe, s_maxed, n - 1)
                qt, pair = u // 8, u % 8
                for i in range(2):
                    r0, t = head_at(2 * pair + i)
                    ins = mm(score_ps[u % 2][:, S * i:S * i + S], qst[p][r0:r0 + MROW, t, P * qt:P * qt + P],
                             kst[l][p][r0:r0 + MROW, t, :], start=True, stop=True)
                ins.then_inc(s_psum, 1)

            def st_tile(r, l, p, v):
                n = tile_no(r, l, p, v)
                if v == 0:
                    pe.wait_ge(m_stacked[p], 16 * 2 * (2 * r + l + 1))
                wait(pe, exp_done, n - 1)
                pair, kt = v // 2, v % 2
                if l == 1:
                    mm(st_ps[v % 2][:, :], identb[:, :], mbias[:, kt, :].unsqueeze(1).to_broadcast([P, 2, S]),
                       start=True, stop=False)
                for i in range(2):
                    r0, t = head_at(2 * pair + i)
                    ins = mm(st_ps[v % 2][:, S * i:S * i + S], kst[l][p][r0:r0 + KROWS, t, P * kt:P * kt + P],
                             qst[p][r0:r0 + KROWS, t, :], start=(l == 0), stop=(l == 0 or i == 1))
                ins.then_inc(st_psum, 1)

            def values(r, l, p, q):
                n = quad_no(r, l, p, q)
                pe.wait_ge(exp_done, 4 * n + 4)
                if p == 0 and q == 0:
                    pe.wait_ge(q_split, (2 * r + l) * LANES + LANES)
                wait(pe, norm_done, n - 1)
                for kt in range(2):
                    for j in range(4):
                        h = 4 * q + j
                        ins = mm(quad_ps[q % 2][32 * j:32 * j + 9, 0:S], vx[l][p][:, kt, h, :],
                                 probs[(4 * q + 2 * (j // 2) + kt) % 8][:, j % 2, :], start=(kt == 0), stop=(kt == 1),
                                 skip_group_check=True)
                ins.then_inc(pv_done, 1)

            def turn_out(r, l, p, q):
                n = quad_no(r, l, p, q)
                pe.wait_ge(o_evac, n + 1)
                for t in range(2):
                    ins = tr(quad_ps[q % 2][:, S + P * t:S + P * t + P], oT[q % 2][:, P * t:P * t + P], ident[:, :])
                ins.then_inc(t_psum, 1)

            def project(ps, lhs, w, brow, done):
                for t in range(2):
                    y = ps[:, S + P * t:S + P * t + P]
                    mm(y, ones[0:1, :], rows[0:1, brow, :], start=True, stop=False)
                    ins = mm(y, lhs[:, P * t:P * t + P], w, start=False, stop=True)
                ins.then_inc(done, 1)

            def body(r):
                for p in range(LANES):
                    wait(pe, z_ready, nth_ln(r - 1, NLN - 1, p) if not isinstance(r, int) or r > 0 else 0)
                    pe.wait_ge(ctx_ld[p], 16 * (r + 1))
                    for t in range(2):
                        ins = tr(work_ps[p][:, P * t:P * t + P], ctx_in[p][:, t, :], ident[:, :])
                    ins.then_inc(ctxT_psum, 1)
                for l in range(2):
                    for p in range(LANES):
                        if l == 0:
                            pe.wait_ge(ctxT_ready, nth(r, p))
                        else:
                            pe.wait_ge(k_split, r * 2 * LANES + p + 1)
                            pe.wait_ge(v_ready, r * 2 * LANES + p + 1)
                        mm(work_ps[p][:, S:2 * S], wT[:, WK + l, :], ctxT[p], start=True, stop=True).then_inc(k_psum, 1)
                        for t in range(2):
                            v = value_ps[p][:, P * t:P * t + P]
                            mm(v, ones[0:1, :], rows[0:1, l, :], start=True, stop=False)
                            ins = mm(v, ctxT[p][:, P * t:P * t + P], wT[:, WV + l, :], start=False, stop=True)
                        ins.then_inc(v_psum, 1)
                for p in range(LANES):
                    pe.wait_ge(v_ready, r * 2 * LANES + LANES + p + 1)
                    pe.wait_ge(k_split, r * 2 * LANES + LANES + p + 1)
                    for qt in range(2):
                        for kt in range(2):
                            ins = mm(value_ps[p][:, 144 * qt:144 * qt + 144].rearrange("p (h d) -> p h d", d=9),
                                     mbar[:, kt, P * qt:P * qt + P], vx[1][p][:, kt, :, 0:9], start=(kt == 0), stop=(kt == 1))
                    ins.then_inc(mv_psum, 1)
                for p in range(LANES):
                    pe.wait_ge(mv_ready, nth(r, p))
                    zt(r, 0, p)
                for p in range(LANES):
                    pe.wait_ge(zT_ready, nth_zt(r, 0, p))
                    mm(work_ps[p][:, S:2 * S], wT[:, SB, :], zT[p][:, :], start=True, stop=True).then_inc(w_psum, 1)
                for p in range(LANES):
                    pe.wait_ge(h_ready, nth(r, p))
                    for t in range(2):
                        for i in range(2):
                            ins = mm(work_ps[p][:, S + P * t:S + P * t + P], ha[p][:, i, P * t:P * t + P], wT[:, SC, :],
                                     start=(i == 0), stop=(i == 1))
                    ins.then_inc(y_psum, 1)
                for l in range(2):
                    if l == 1:
                        ffn(r)
                        sign_attention(r)
                    for p in range(LANES):
                        zt(r, 1 + 3 * l, p)
                    for p in range(LANES):
                        pe.wait_ge(zT_ready, nth_zt(r, 1 + 3 * l, p))
                        mm(work_ps[p][:, S:2 * S], wT[:, WQ + l, :], zT[p][:, :], start=True, stop=True).then_inc(q_psum, 1)
                    for u in range(NTILE):
                        score_tile(r, l, 0, u)
                    maxima(r, l, 0)
                    for p in range(LANES):
                        attend(r, l, p)

            def nth_zt(r, i, p):
                return r * (NLN - 2) * LANES + (i - (1 if i > 3 else 0)) * LANES + p + 1

            def maxima(r, l, p):
                pe.wait_ge(s_maxed, tile_no(r, l, p, NTILE - 1) + 1)
                for t in range(2):
                    ins = tr(lane_ps[p % 2][0:H, P * t:P * t + P], mx[p][:, t, :], ident[:, :])
                ins.then_inc(mT_psum, 1)

            def turn_attention(r, l, p):
                pe.wait_ge(norm_done, quad_no(r, l, p, NQUAD - 1) + 1)
                for t in range(2):
                    ins = tr(out_ps(p)[:, P * t:P * t + P], att[p][:, t, :], ident[:, :])
                ins.then_inc(attT_psum, 1)

            def project_attention(r, l, p):
                pe.wait_ge(attT_ready, r * 2 * LANES + l * LANES + p + 1)
                project(out_ps(p), attT[p], wT[:, WO + l, :], 2 + l, y_psum)

            def attend(r, l, p):
                for q in range(NQUAD):
                    for i in range(4):
                        st_tile(r, l, p, 4 * q + i)
                        if p + 1 < LANES:
                            score_tile(r, l, p + 1, 4 * q + i)
                    if q == 0 and p > 0:
                        turn_attention(r, l, p - 1)
                    if q >= 1:
                        values(r, l, p, q - 1)
                    if q == 1 and p > 0:
                        project_attention(r, l, p - 1)
                    if q >= 2:
                        turn_out(r, l, p, q - 2)
                if p + 1 < LANES:
                    maxima(r, l, p + 1)
                values(r, l, p, NQUAD - 1)
                turn_out(r, l, p, NQUAD - 2)
                turn_out(r, l, p, NQUAD - 1)
                if p == LANES - 1:
                    turn_attention(r, l, p)
                    project_attention(r, l, p)

            def ffn(r):
                for p in range(LANES):
                    zt(r, 2, p)
                for p in range(LANES):
                    pe.wait_ge(zT_ready, nth_zt(r, 2, p))
                    project(work_ps[p], zT[p], w_hash[:, :], 4, lg_psum)
                for p in range(LANES):
                    pe.wait_ge(hot_ready, nth(r, p))
                    for t in range(2):
                        ins = tr(work_ps[p][0:E, P * t:P * t + P], hot[p][:, t, :], ident[:, :])
                    ins.then_inc(hotT_psum, 1)
                for p in range(LANES):
                    if p == 0:
                        spread(r, 0)
                    if p + 1 < LANES:
                        spread(r, p + 1)
                    pe.wait_ge(zm_ready, nth(r, p, E // 2))
                    for t in range(2):
                        y = work_ps[p][:, S + P * t:S + P * t + P]
                        mm(y, hotT[p][:, P * t:P * t + P], b_exp[:, :], start=True, stop=False)
                        for e in range(E):
                            ins = mm(y, zm[p % 2][:, e, P * t:P * t + P], w_exp[:, e, :], start=False, stop=(e == E - 1))
                    ins.then_inc(y_psum, 1)

            def spread(r, p):
                pe.wait_ge(hotT_ready, nth(r, p))
                for e in range(E):
                    if p > 0 and e % 2 == 0:
                        pe.wait_ge(zm_ready, nth(r, p - 1, E // 2, e // 2 + 1))
                    ins = mm(banks[e // 2][:, S * (e % 2):S * (e % 2) + S], selb[:, e, :], hotTb[p],
                             start=True, stop=True)
                    if e % 2 == 1:
                        ins.then_inc(bc_psum, 1)

            def sign_attention(r):
                for p in range(LANES):
                    zt(r, 3, p)
                for p in range(LANES):
                    pe.wait_ge(qb_ready, nth(r, p))
                    mm(work_ps[p][:, 0:S], kb[p][:, 0:P], qb[p][:, :], start=True, stop=True)
                    mm(work_ps[p][:, S:S + P], kb[p][:, P:S], qb[p][:, P:S], start=True, stop=True).then_inc(sg_psum, 1)
                for p in range(LANES):
                    pe.wait_ge(aw_ready, nth(r, p))
                    mm(work_ps[p][:, S:S + P], aw[p][:, 0:P], z[p][:, 0, :], start=True, stop=True)
                    mm(work_ps[p][:, S + P:2 * S], aw[p][:, P:S], z[p][:, 0, :], start=True, stop=False)
                    mm(work_ps[p][:, S + P:2 * S], aw[p][:, S:384], z[p][:, 1, :], start=False, stop=True).then_inc(y_psum, 1)

            rounds(pe, body)

            pe.wait_ge(z_ready, NLN * B)
            for j in range(4):
                for k in range(4):
                    ins = tr(banks[j][:, P * k:P * k + P], z6[:, 4 * j + k, :], ident[:, :])
                ins.then_inc(zT6_psum, 1)
            for c in range(NT):
                if c % 4 == 0:
                    pe.wait_ge(zT6_ready, c // 4 + 1)
                ins = mm(o_ps[:, 0:P], wg_pad[:, 120 - E * c:248 - E * c], zT6[:, c, :], start=(c == 0), stop=(c == NT - 1))
            ins.then_inc(gate_psum, 1)
            pe.wait_ge(cmax_ready, 1)
            tr(t_ps[0:1, 0:P], g[:, 0:1], ident[:, :]).then_inc(cmaxT_psum, 1)
            pe.wait_ge(m8_ready, 1)
            mm(t_ps[:, 128:129], m8[0:1, P:2 * P], ones[0:1, 0:1], start=True, stop=True)
            mm(t_ps[:, 136:136 + E], ones[0:1, :], m8[0:1, P:P + E], start=True, stop=True).then_inc(mbc_psum, 1)
            for b in range(32):
                pe.wait_ge(cnt_ready, b + 1)
                mm(o_ps[:, 256:257], blockb[:, :], cntb[:, 0:1], start=True, stop=True).then_inc(tot_psum, 1)
            pe.wait_ge(ties_ready, 1)
            mm(t_ps[:, 144:145], blockf[:, :], g[:, 20:21], start=True, stop=True)
            mm(t_ps[:, 148:149], below[:, :], cum[:, P - 1:P], start=True, stop=True).then_inc(ties_psum, 1)
            pe.wait_ge(sel_ready, 1)
            mm(t_ps[:, 152:153], below[:, :], cum[:, P - 1:P], start=True, stop=True)
            mm(t_ps[:, 160:160 + E], ones[:, :], g[:, 24:24 + E], start=True, stop=True).then_inc(sel_psum, 1)
            pe.wait_ge(pos_ready, 1)
            tr(t_ps[:, 256:384], pos[:, :], ident[:, :]).then_inc(pos_psum, 1)
            for n in range(E * NT):
                e, c = n // NT, n % NT
                pe.wait_ge(onehot_ready, n + 1)
                for i in range(2):
                    ins = mm(st_ps[i][:, 2 * e:2 * e + 2], onehot[n % 8][:, P * i:P * i + P], tokid[:, c, :],
                             start=(c == 0), stop=(c == NT - 1))
                ins.then_inc(onehot_used, 1)

            def down(e):
                pe.wait_ge(hT_ready, e + 1)
                if e >= 2:
                    pe.wait_ge(y_ready, e - 1)
                for i in range(2):
                    for t in range(2):
                        ins = mm(quad_ps[e % 2][:, P * i:P * i + P], hT[e % 2][:, t, P * i:P * i + P],
                                 w2T[:, 2 * e + t, :], start=(t == 0), stop=(t == 1))
                ins.then_inc(down_psum, 1)

            pe.wait_ge(ids_ready, E)
            for e in range(E):
                for i in range(2):
                    pe.wait_ge(gathered[2 * e + i], 16)
                if e >= 2:
                    pe.wait_ge(wslot_ready, e - 1)
                for i in range(2):
                    ins = tr(lane_ps[e % 2][:, P * i:P * i + P], xg[:, 2 * e + i, :], ident[:, :])
                ins.then_inc(xgT_psum, 1)
                pe.wait_ge(xgT_ready, e + 1)
                for i in range(2):
                    ins = mm(lane_ps[e % 2][:, S + i:S + i + 1], xgT[:, 2 * e + i, :], wg_pad[:, 120 + e:121 + e],
                             start=True, stop=True)
                ins.then_inc(ws_psum, 1)
            for e in range(E):
                if e >= 2:
                    pe.wait_ge(hT_ready, e - 1)
                for t in range(2):
                    mm(score_ps[e % 2][:, S * t:S * t + S], w1T[:, 2 * e + t, :], xgT[:, 2 * e:2 * e + 2, :],
                       start=True, stop=True)
                    ins = mm(st_ps[e % 2][:, S * t:S * t + S], w3T[:, 2 * e + t, :], xgT[:, 2 * e:2 * e + 2, :],
                             start=True, stop=True)
                ins.then_inc(up_psum, 1)
                if e >= 1:
                    down(e - 1)
            down(E - 1)

        @block.vector
        def _(dve):
            n = [0]

            def link(ins):
                n[0] += 1
                ins.then_inc(dve_chain, 1)
                dve.wait_ge(dve_chain, n[0])

            ts, tt, stt = dve.tensor_scalar, dve.tensor_tensor, dve.scalar_tensor_tensor

            dve.wait_ge(ld_small, 16 * N_SMALL)
            ts(mask[:, :, :], maski, 0.0, None, ALU.not_equal).then_inc(dve_setup, 1)
            hdt = DT / 2
            v = [sv[:, i:i + 1] for i in range(32)]
            DR, NI, D2, T0, INV, AR, AI, CR, CI, Z0, M2, MH, RS, T1_, T2_, UR, UI, R = range(18)
            dve.memset(v[MH], -0.5)
            ts(v[NI], cols[:, CAI:CAI + 1], hdt, None, ALU.mult)
            link(ts(v[DR], cols[:, CAR:CAR + 1], -hdt, 1.0, ALU.mult, ALU.add))
            link(tt(v[T0], v[NI], v[NI], ALU.mult))
            link(stt(v[D2], v[DR], v[DR], v[T0], ALU.mult, ALU.add))
            link(dve.reciprocal(v[INV], v[D2]))
            link(ts(v[T1_], cols[:, CAR:CAR + 1], hdt, 1.0, ALU.mult, ALU.add))
            link(stt(v[T2_], v[T1_], v[DR], v[T0], ALU.mult, ALU.subtract))
            link(tt(v[AR], v[T2_], v[INV], ALU.mult))
            link(stt(v[AI], v[NI], 2.0, v[INV], ALU.mult, ALU.mult))
            rdt = DT ** 0.5
            link(stt(v[CR], v[DR], rdt, v[INV], ALU.mult, ALU.mult))
            link(stt(v[CI], v[NI], rdt, v[INV], ALU.mult, ALU.mult))
            link(tt(v[T0], v[AI], v[AI], ALU.mult))
            link(stt(v[T1_], v[AR], v[AR], v[T0], ALU.mult, ALU.add))
            link(ts(v[Z0], v[T1_], 0.0, None, ALU.is_equal))
            tt(v[M2], v[T1_], v[Z0], ALU.add).then_inc(tab_sq, 1)
            dve.wait_ge(tab_pow, 1)
            link(tt(v[T0], v[RS], v[RS], ALU.mult))
            link(tt(v[T0], v[T0], v[M2], ALU.mult))
            link(ts(v[T0], v[T0], -0.5, 1.5, ALU.mult, ALU.add))
            link(tt(v[RS], v[RS], v[T0], ALU.mult))
            link(stt(v[UR], v[AR], v[RS], v[Z0], ALU.mult, ALU.add))
            link(tt(v[UI], v[AI], v[RS], ALU.mult))
            link(tt(v[T0], v[AI], v[UI], ALU.mult))
            link(stt(v[R], v[AR], v[UR], v[T0], ALU.mult, ALU.add))
            dve.wait_ge(pool_const, 2)
            link(ts(rdec[:, :], rdec[:, :], v[R], None, ALU.mult))
            dve.memset(er[:, 0:1], 1.0)
            link(dve.memset(ei[:, 0:1], 0.0))
            w = 1
            while w < S:
                ts(stmp[:, 0:w], ei[:, 0:w], v[UI], None, ALU.mult)
                link(ts(stmp[:, P:P + w], er[:, 0:w], v[UI], None, ALU.mult))
                stt(er[:, w:2 * w], er[:, 0:w], v[UR], stmp[:, 0:w], ALU.mult, ALU.subtract)
                link(stt(ei[:, w:2 * w], ei[:, 0:w], v[UR], stmp[:, P:P + w], ALU.mult, ALU.add))
                tt(v[T0], v[UI], v[UI], ALU.mult)
                link(stt(v[T1_], v[UR], 2.0, v[UI], ALU.mult, ALU.mult))
                link(stt(v[UR], v[UR], v[UR], v[T0], ALU.mult, ALU.subtract))
                link(dve.tensor_copy(v[UI], v[T1_]))
                w *= 2
            link(ts(stmp, ei[:, :], v[CI], None, ALU.mult))
            link(stt(t1[:, :], er[:, :], v[CR], stmp, ALU.mult, ALU.subtract))
            link(ts(stmp, er[:, :], v[CI], None, ALU.mult))
            link(stt(t2[:, :], ei[:, :], v[CR], stmp, ALU.mult, ALU.add))
            ts(t2[:, :], t2[:, :], -1.0, None, ALU.mult)
            link(ts(esin[:, :], ei[:, :], -1.0, None, ALU.mult))
            for i in range(1, NTURN, 2):
                dve.wait_ge(setup_ps, i + 1)
                dve.tensor_copy(turn[i][1], banks[i % 6][:, :].rearrange("p (i c) -> p i c", c=P)).then_inc(setup_dve, 1)
            dve.wait_ge(setup_ps, NTURN + 2)
            dve.wait_ge(pool_step, POOL_SETUP)
            dve.tensor_copy(wg_pad[:, 120:128], o_ps[:, 0:E])
            dve.tensor_copy(cols[:, 0:4], o_ps[:, E:E + 4])
            dve.tensor_copy(svb[:, :], o_ps[:, 256:384])
            ts(mbar[:, :, :], t_ps[:, :].rearrange("p (t q) -> p t q", t=2), -1.0, 1.0, ALU.mult, ALU.add)
            ts(mbias[:, :, :], t_ps[:, :].rearrange("p (t q) -> p t q", t=2), -1.0, -BIG, ALU.add, ALU.mult)
            dve.wait_ge(act_setup, 1)
            tt(sgn[:, 2:3], sgn[:, 0:1], sgn[:, 1:2], ALU.mult).then_inc(dve_setup, 1)
            dve.wait_ge(dve_setup, 2)
            dve.wait_ge(ld_x, 16)

            def quad_no(r, l, p, q):
                return ((r * 2 + l) * LANES + p) * NQUAD + q

            def norm_stats(r, i, p):
                x = xs(r, p)
                dve.bn_stats(stat[p][:, 0, :], x[:, 0, :])
                link(dve.bn_stats(stat[p][:, 1, :], x[:, 1, :]))
                dve.bn_aggr(mv[p][:, 0, :], stat[p][:, 0, :])
                dve.bn_aggr(mv[p][:, 1, :], stat[p][:, 1, :]).then_inc(ln_stats, 1)

            def norm_apply(r, i, p):
                x = xs(r, p)
                o = z6s(r, p) if i == NLN - 1 else z[p]
                dve.wait_ge(ln_rstd, nth_ln(r, i, p))
                for t in range(2):
                    ins = ts(o[:, t, :], x[:, t, :], mv[p][:, t, 0:1], rstd[p][:, 2 + t:3 + t], ALU.subtract, ALU.mult)
                ins.then_inc(z_ready, 1)

            def residual(r, i, p, ps):
                dve.wait_ge(y_psum, y_no(r, i, p))
                link(tt(xs(r, p), xs(r, p), ps[:, S:2 * S].rearrange("p (t d) -> p t d", t=2), ALU.add))

            def split(p, src, bias, done):
                link(ts(parts[p][:, 0, :], src, bias, None, ALU.add))
                link(stt(rest[p][:, :], src, bias, parts[p][:, 0, :], ALU.add, ALU.subtract))
                link(dve.tensor_copy(parts[p][:, 1, :], rest[p][:, :]))
                tt(parts[p][:, 2, :], rest[p][:, :], parts[p][:, 1, :], ALU.subtract).then_inc(done, 1)

            def maximum(r, l, p, u):
                k = tile_no(r, l, p, u)
                qt, pair = u // 8, u % 8
                dve.wait_ge(s_psum, k + 1)
                s2 = score_ps[u % 2][:, :].rearrange("p (i k) -> p i k", i=2)
                if l == 0:
                    dve.tensor_reduce(mx[p][:, qt, 2 * pair:2 * pair + 2], s2, AX.X, ALU.max).then_inc(s_maxed, 1)
                else:
                    for i in range(2):
                        h = 2 * pair + i
                        ins = dve.tensor_tensor_reduce(junk[p][u % 2][:, i, :], s2[:, i, :], mask[:, qt, :], 1.0, -3.0e38,
                                                       ALU.mult, ALU.max, mx[p][:, qt, h:h + 1])
                    ins.then_inc(s_maxed, 1)

            def split_max(r, l, p):
                if l == 1:
                    dve.wait_ge(s_maxed, tile_no(r, l, p, NTILE - 1) + 1)
                    ts(emx[p][:, :, :], mx[p][:, :, :], -SCALE, -1.0e-9, ALU.mult, ALU.min).then_inc(m_neg, 1)
                dve.wait_ge(mT_psum, r * 2 * LANES + l * LANES + p + 1)
                src = lane_ps[p % 2][0:H, 0:S]
                link(ts(mparts[p][:, 0, :], src, -1.0, None, ALU.mult))
                link(stt(mrest[p][:, :], src, -1.0, mparts[p][:, 0, :], ALU.mult, ALU.subtract))
                link(dve.tensor_copy(mparts[p][:, 1, :], mrest[p][:, :]))
                tt(mparts[p][:, 2, :], mrest[p][:, :], mparts[p][:, 1, :], ALU.subtract).then_inc(m_split, 1)

            def normalise(r, l, p, q):
                k = quad_no(r, l, p, q)
                dve.wait_ge(t_psum, k + 1)
                wait(dve, norm_done, k - 1)
                onum, orec = onums[q % 2], orecs[q % 2]
                t4 = quad_ps[q % 2][:, S:2 * S].rearrange("p (t j c) -> p t j c", t=2, j=4)
                num, den = t4[:, :, :, 0:HD], t4[:, :, :, HD]
                if l == 1:
                    dve.wait_ge(emx_ready, nth(r, p))
                    link(tt(onum[:, :, :, :], mvx[p][:, :, 4 * q:4 * q + 4, :],
                            emx[p][:, :, 4 * q:4 * q + 4].unsqueeze(3).to_broadcast([P, 2, 4, 9]), ALU.mult))
                    link(tt(onum[:, :, :, :], t4[:, :, :, 0:9], onum[:, :, :, :], ALU.add))
                    num, den = onum[:, :, :, 0:HD], onum[:, :, :, HD]
                link(dve.reciprocal(orec[:, :, :], den))
                tt(att[p][:, :, 32 * q:32 * q + 32].rearrange("p t (j d) -> p t j d", d=HD), num,
                   orec[:, :, :].unsqueeze(3).to_broadcast([P, 2, 4, HD]), ALU.mult).then_inc(norm_done, 1)

            def attention(r, l):
                for p in range(LANES):
                    if l == 0:
                        dve.wait_ge(k_stored[p], 16 * 3 * (2 * r + 2))
                    else:
                        dve.wait_ge(q_stored[p], 16 * 3 * (2 * r + 1))
                    dve.wait_ge(q_psum, r * 2 * LANES + l * LANES + p + 1)
                    split(p, work_ps[p][:, S:2 * S], cols[:, CQ + l:CQ + l + 1], q_split)
                for u in range(NTILE):
                    maximum(r, l, 0, u)
                split_max(r, l, 0)
                for p in range(LANES - 1):
                    if p > 0:
                        normalise(r, l, p - 1, 2)
                        normalise(r, l, p - 1, 3)
                    for q in range(NQUAD):
                        for i in range(4):
                            maximum(r, l, p + 1, 4 * q + i)
                        if q == 2 and p > 0:
                            residual(r, 1 + 3 * l, p - 1, out_ps(p - 1))
                        if q >= 2:
                            normalise(r, l, p, q - 2)
                    split_max(r, l, p + 1)
                last, ln = LANES - 1, 2 + 3 * l
                normalise(r, l, last - 1, 2)
                normalise(r, l, last - 1, 3)
                residual(r, 1 + 3 * l, last - 1, out_ps(last - 1))
                normalise(r, l, last, 0)
                norm_stats(r, ln, 0)
                norm_stats(r, ln, 1)
                normalise(r, l, last, 1)
                norm_apply(r, ln, 0)
                norm_stats(r, ln, 2)
                normalise(r, l, last, 2)
                norm_apply(r, ln, 1)
                norm_apply(r, ln, 2)
                normalise(r, l, last, 3)
                residual(r, 1 + 3 * l, last, out_ps(last))
                norm_stats(r, ln, last)
                norm_apply(r, ln, last)

            def hashed_ffn(r):
                for p in range(LANES):
                    lg = lexp[p]
                    dve.wait_ge(lg_copied, nth(r, p))
                    link(dve.tensor_reduce(lmax[p][:, 0:2], lg[:, :, :], AX.X, ALU.max))
                    ts(lmax[p][:, 2:4], lmax[p][:, 0:2], -1.0, None, ALU.mult).then_inc(lg_max, 1)
                    for t in range(2):
                        ins = stt(rest[p][:, P * t:P * t + P], lg[:, t, :], lmax[p][:, t:t + 1], iota_rev[:, :],
                                  ALU.is_ge, ALU.mult)
                    link(ins)
                    link(dve.tensor_reduce(stat[p][:, 0, 0:2], rest[p][:, :].rearrange("p (t d) -> p t d", t=2),
                                           AX.X, ALU.max))
                    for t in range(2):
                        ins = ts(ytmp[p][:, P * t:P * t + P], iota_rev[:, :], stat[p][:, 0, t:t + 1], None, ALU.is_equal)
                    link(ins)
                    dve.tensor_reduce(hot[p][:, :, :], ytmp[p][:, :].rearrange("p (t g e) -> p t e g", t=2, e=E),
                                      AX.X, ALU.max).then_inc(hot_ready, 1)
                def select(p):
                    dve.wait_ge(lg_exp, nth(r, p))
                    dve.reciprocal(lmax[p][:, 6:8], lmax[p][:, 4:6])
                    for j in range(E // 2):
                        dve.wait_ge(bc_psum, nth(r, p, E // 2, j + 1))
                        if j == 0 and p >= 2:
                            dve.wait_ge(y_psum, y_no(r, 2, p - 2))
                        tt(zm[p % 2][:, 2 * j:2 * j + 2, :], zT[p][:, :].unsqueeze(1).to_broadcast([P, 2, S]),
                           banks[j][:, :].rearrange("p (i k) -> p i k", i=2), ALU.mult).then_inc(zm_ready, 1)

                def finish(p):
                    dve.wait_ge(y_psum, y_no(r, 2, p))
                    for t in range(2):
                        ins = ts(ytmp[p][:, P * t:P * t + P], work_ps[p][:, S + P * t:S + P * t + P], 0.0,
                                 lmax[p][:, 6 + t:7 + t], ALU.max, ALU.mult)
                    link(ins)
                    link(tt(xs(r, p), xs(r, p), ytmp[p][:, :].rearrange("p (t d) -> p t d", t=2), ALU.add))
                    norm_stats(r, 3, p)

                for p in range(LANES):
                    select(p)
                    if p > 0:
                        finish(p - 1)
                finish(LANES - 1)

            def sign_attention(r):
                for p in range(LANES):
                    norm_apply(r, 3, p)
                for p in range(LANES):
                    dve.wait_ge(sign_ready, nth(r, p))
                    ts(qb[p][:, :], kb[p][:, :], sgn[:, 2:3], None, ALU.mult).then_inc(qb_ready, 1)
                for p in range(LANES):
                    dve.wait_ge(tanh_done, nth(r, p))
                    stt(aw[p][:, :], th[p][:, :], 1.0, halfmask[:, :], ALU.add, ALU.mult).then_inc(aw_ready, 1)
                for p in range(LANES):
                    dve.wait_ge(y_psum, y_no(r, 3, p))
                    link(tt(ytmp[p][:, :].rearrange("p (t d) -> p t d", t=2),
                            work_ps[p][:, S:2 * S].rearrange("p (t d) -> p t d", t=2),
                            svb[:, :].unsqueeze(1).to_broadcast([P, 2, P]), ALU.mult))
                    link(tt(xs(r, p), xs(r, p), ytmp[p][:, :].rearrange("p (t d) -> p t d", t=2), ALU.add))
                    norm_stats(r, 4, p)
                for p in range(LANES):
                    norm_apply(r, 4, p)

            def body(r):
                for p in range(LANES):
                    norm_stats(r, 0, p)
                for l in range(2):
                    for p in range(LANES):
                        dve.wait_ge(k_psum, r * 2 * LANES + l * LANES + p + 1)
                        if l == 0:
                            wait(dve, q_stored[p], 16 * 3 * 2 * r)
                        else:
                            dve.wait_ge(k_stored[p], 16 * 3 * (2 * r + 1))
                        split(p, work_ps[p][:, S:2 * S], cols[:, CK + l:CK + l + 1], k_split)
                    if l == 0:
                        for p in range(LANES):
                            norm_apply(r, 0, p)
                for p in range(LANES):
                    dve.wait_ge(w_psum, nth(r, p))
                    tt(wa[p][:, 0, :], work_ps[p][:, S:2 * S], er[:, :], ALU.mult)
                    link(tt(wa[p][:, 1, :], work_ps[p][:, S:2 * S], esin[:, :], ALU.mult))
                    for i in range(2):
                        ins = dve.tensor_tensor_scan(ga[p][:, i, :], rdec[:, :], wa[p][:, i, :], 0.0, ALU.mult, ALU.add)
                    ins.then_inc(scan_done, 1)
                for p in range(LANES):
                    residual(r, 0, p, work_ps[p])
                    norm_stats(r, 1, p)
                for p in range(LANES):
                    norm_apply(r, 1, p)
                attention(r, 0)
                hashed_ffn(r)
                sign_attention(r)
                attention(r, 1)

            rounds(dve, body)

            dve.wait_ge(gate_psum, 1)
            link(dve.tensor_copy(sc[:, :], o_ps[:, 0:P]))
            dve.tensor_reduce(g[:, 0:1], sc[:, :], AX.X, ALU.max).then_inc(cmax_ready, 1)
            dve.wait_ge(cmaxT_psum, 1)
            link(dve.tensor_reduce(m8[0:1, 0:E], t_ps[0:1, 0:P].rearrange("p (c e) -> p e c", e=E), AX.X, ALU.max))
            ts(m8[0:1, P:2 * P].rearrange("p (c e) -> p c e", e=E), m8[0:1, 0:E].unsqueeze(1).to_broadcast([1, NT, E]),
               -1.0, None, ALU.mult).then_inc(m8_ready, 1)
            dve.wait_ge(mbc_psum, 1)
            dve.tensor_copy(nm8[:, :], t_ps[:, 136:136 + E])
            dve.tensor_copy(g[:, 2:3], t_ps[:, 128:129]).then_inc(nm_ready, 1)
            room = float(CAP) - 0.5

            def count(b, thr):
                ts(eq[:, :], sc[:, :], thr, None, ALU.is_ge, ALU.add, accum_out=cntb[:, 0:1]).then_inc(cnt_ready, 1)
                dve.wait_ge(tot_psum, 32 - b)

            count(31, 0.0)
            link(ts(U, o_ps[:, 256:257], room, -float(2 ** 31), ALU.is_ge, ALU.mult))
            link(ts(M, U, 31, -1, ALU.arith_shift_right, ALU.bitwise_xor))
            link(ts(M, M, -2 ** 31, None, ALU.bitwise_or))
            for b in range(30, -1, -1):
                link(ts(F, U, 2 ** b, None, ALU.bitwise_or))
                link(tt(F, F, M, ALU.bitwise_xor))
                count(b, F.bitcast(F32))
                link(ts(DB, o_ps[:, 256:257], room, float(2 ** b), ALU.is_ge, ALU.mult))
                link(tt(U, U, DB, ALU.bitwise_or))
            link(tt(F, U, M, ALU.bitwise_xor))
            thr = F.bitcast(F32)
            ts(sel[:, :], sc[:, :], thr, None, ALU.is_gt, ALU.add, accum_out=g[:, 20:21])
            link(ts(eq[:, :], sc[:, :], thr, None, ALU.is_equal))
            dve.tensor_tensor_scan(cum[:, :], ones[:, :], eq[:, :], 0.0, ALU.mult, ALU.add).then_inc(ties_ready, 1)
            dve.wait_ge(ties_psum, 1)
            ts(g[:, 4:5], t_ps[:, 144:145], -1.0, float(CAP), ALU.mult, ALU.add)
            link(dve.tensor_copy(g[:, 5:6], t_ps[:, 148:149]))
            link(ts(cum[:, :], cum[:, :], g[:, 5:6], g[:, 4:5], ALU.add, ALU.is_le))
            link(tt(eq[:, :], eq[:, :], cum[:, :], ALU.mult))
            link(tt(sel[:, :], sel[:, :], eq[:, :], ALU.add))
            dve.wait_ge(gate_exp, 1)
            dve.tensor_tensor_scan(cum[:, :], ones[:, :], sel[:, :], 0.0, ALU.mult, ALU.add)
            link(dve.tensor_tensor_reduce(eq[:, :], ex[:, :], sel[:, :], 1.0, 0.0, ALU.mult, ALU.add, g[:, 22:23]))
            ts(g[:, 24:24 + E], emask[:, :], g[:, 22:23], None, ALU.mult).then_inc(sel_ready, 1)
            dve.wait_ge(sel_psum, 1)
            dve.reciprocal(rs8[:, :], t_ps[:, 160:160 + E])
            link(dve.tensor_copy(g[:, 6:7], t_ps[:, 152:153]))
            link(stt(pos[:, :], cum[:, :], g[:, 6:7], sel[:, :], ALU.add, ALU.mult))
            ts(pos[:, :], pos[:, :], -1.0, None, ALU.add).then_inc(pos_ready, 1)
            dve.wait_ge(pos_psum, 1)
            link(dve.tensor_copy(posT[:, :], t_ps[:, 256:384]))
            for n_ in range(E * NT):
                e, c = n_ // NT, n_ % NT
                if n_ >= 8:
                    dve.wait_ge(onehot_used, n_ - 7)
                ts(onehot[n_ % 8], iota_slot[:, :], posT[:, E * c + e:E * c + e + 1], None, ALU.is_equal).then_inc(onehot_ready, 1)
                if c == NT - 1:
                    dve.wait_ge(onehot_used, n_ + 1)
                    for i in range(2):
                        ins = dve.tensor_copy(g[:, 40 + 2 * i:42 + 2 * i], st_ps[i][:, 2 * e:2 * e + 2])
                    link(ins)
                    for i in range(2):
                        ins = stt(ids[:, 2 * e + i:2 * e + i + 1], g[:, 41 + 2 * i:42 + 2 * i], float(P),
                                  g[:, 40 + 2 * i:41 + 2 * i], ALU.mult, ALU.add)
                    ins.then_inc(ids_ready, 1)

            def weigh(e):
                dve.wait_ge(down_psum, e + 1)
                dve.wait_ge(wslot_ready, e + 1)
                if e >= 2:
                    dve.wait_ge(scattered[0], 16 * (e - 1))
                    dve.wait_ge(scattered[1], 16 * (e - 1))
                for i in range(2):
                    ins = ts(ysc[e % 2][:, i, :], quad_ps[e % 2][:, P * i:P * i + P],
                             wslot[:, 2 * e + i:2 * e + i + 1], rs8[:, e:e + 1], ALU.mult, ALU.mult)
                ins.then_inc(y_ready, 1)

            for e in range(E):
                dve.wait_ge(silu_done, e + 1)
                if e >= 2:
                    dve.wait_ge(down_psum, e - 1)
                tt(hT[e % 2], act1[e % 2], st_ps[e % 2][:, :].rearrange("p (t c) -> p t c", t=2), ALU.mult).then_inc(hT_ready, 1)
                if e >= 1:
                    weigh(e - 1)
            weigh(E - 1)


_INS = ["x", "ctx_1024", "mask_SxS2_ik0", "L0_attn_A_real", "L0_attn_A_imag", "L0_attn_B", "L0_attn_C",
        "L0_xattn_Wq", "L0_xattn_bq", "L0_xattn_Wk", "L0_xattn_bk", "L0_xattn_Wv", "L0_xattn_bv", "L0_xattn_Wo",
        "L0_xattn_bo", "L0_ffn_Wg", "L0_ffn_bg", "L0_ffn_We", "L0_ffn_be", "L1_attn_bv_q", "L1_attn_bv_k",
        "L1_attn_bv_v", "L1_xattn_Wq", "L1_xattn_bq", "L1_xattn_Wk", "L1_xattn_bk", "L1_xattn_Wv", "L1_xattn_bv",
        "L1_xattn_Wo", "L1_xattn_bo", "L1_ffn_Wg", "L1_ffn_W1", "L1_ffn_W2", "L1_ffn_W3"]


def kernel(**inputs):
    import numpy as _np
    import concourse.bacc as _bacc
    from concourse import mybir as _mybir
    from concourse.bass_utils import run_bass_kernel_spmd as _run

    nc = _bacc.Bacc("TRN2", target_bir_lowering=False, num_devices=1)
    arrays, aps = {}, {}
    for name in _INS:
        arr = _np.ascontiguousarray(inputs[name])
        arrays[f"in_{name}"] = arr
        aps[name] = nc.dram_tensor(f"in_{name}", arr.shape, _mybir.dt.from_np(arr.dtype), kind="ExternalInput").ap()
    out = nc.dram_tensor("out", (B, S, D), F32, kind="ExternalOutput").ap()
    decoder(nc, aps, out)
    r = _run(nc, [arrays], core_ids=[0])
    return r.results[0]["out"]
```

```python
from contextlib import ExitStack

import concourse.bass as bass
from concourse import mybir

ALU = mybir.AluOpType
ACT = mybir.ActivationFunctionType
AX = mybir.AxisListType
F32 = mybir.dt.float32
BF16 = mybir.dt.bfloat16
I32 = mybir.dt.int32

P = 128
B, S, D = 8, 256, 128
NT = B * S // P
H, HD = 16, 8
E = 8
HID = 256
CAP = B * S // E
LANES = 4
ROUNDS = B // LANES
NLN = 6
SCALE = 1.0 / float(HD) ** 0.5
BIG = -1.0e30
DT = 0.01
SPLITS = 6
MROW = SPLITS * HD
KROWS = MROW + 3
NTILE = 16
NQUAD = 4


def decoder(nc, a, out):
    ctx = ExitStack()
    with ctx:
        def sb(name, shape, dt=F32):
            return ctx.enter_context(nc.sbuf_tensor(name, shape, dt))

        def sem(name):
            return ctx.enter_context(nc.semaphore(name))

        def lanes(name, shape, dt=F32):
            return [sb(f"{name}{p}", shape, dt) for p in range(LANES)]

        def bank(name):
            return ctx.enter_context(nc.psum_tensor(name, [P, 512], F32))

        score_ps = [bank(f"score_ps{i}") for i in range(2)]
        st_ps = [bank(f"st_ps{i}") for i in range(2)]
        lane_ps = [bank(f"lane_ps{i}") for i in range(2)]
        o_ps, t_ps = bank("o_ps"), bank("t_ps")
        quad_ps = [o_ps, t_ps]
        banks = score_ps + st_ps + lane_ps + [o_ps, t_ps]
        work_ps = lane_ps + quad_ps
        value_ps = st_ps + score_ps

        def turn_bank(i):
            return (lane_ps + score_ps)[i % 4]

        def out_ps(p):
            return lane_ps[p % 2] if p < LANES - 1 else score_ps[0]

        ident = sb("ident", [P, P])
        identb = sb("identb", [P, P], BF16)
        ones = sb("ones", [P, P])
        iota_rev = sb("iota_rev", [P, P])
        iota16 = sb("iota16", [P, 16])
        tokp = sb("tokp", [P, 2])
        tilec = sb("tilec", [P, NT])
        digits = sb("digits", [P, 3], I32)
        halfmask = sb("halfmask", [P, 384])
        selb = sb("selb", [E, E, P], BF16)
        blockb = sb("blockb", [P, P], BF16)
        below = sb("below", [P, P])
        emask = sb("emask", [P, E])
        wT = sb("wT", [P, 10, P])
        WQ, WK, WV, WO, SB, SC = 0, 2, 4, 6, 8, 9
        w_hash = sb("w_hash", [P, P])
        w_exp = sb("w_exp", [P, E, P])
        b_exp = sb("b_exp", [E, P])
        rows = sb("rows", [1, 3, P])
        rows3 = sb("rows3", [3, 3, P], BF16)
        ones3 = sb("ones3", [3, P], BF16)
        cols = sb("cols", [P, 12])
        CQ, CK, CAR, CAI, CSQ, CSK, CV = 0, 2, 4, 5, 6, 7, 8
        sgn = sb("sgn", [P, 4])
        svb = sb("svb", [P, P])
        wg_pad = sb("wg_pad", [P, 248])
        w1n = sb("w1n", [P, 2 * E, P])
        w3n = sb("w3n", [P, 2 * E, P])
        w2n = sb("w2n", [P, E, HID])
        mask = sb("mask", [P, 2, S])
        mbar = sb("mbar", [P, 2, S])
        mbias = sb("mbias", [P, 2, S], BF16)
        blockf = sb("blockf", [P, P])
        er, ei = sb("er", [P, S]), sb("ei", [P, S])
        esin = ei
        t1, t2 = sb("t1", [P, S]), sb("t2", [P, S])
        rdec = sb("rdec", [P, S])
        sv = sb("sv", [P, 32])

        x_all = sb("x_all", [P, NT, D])
        z6 = sb("z6", [P, NT, D])
        nat = z6[:, 0:10, :]
        stat = lanes("stat", [P, 2, 6])
        mv_all = sb("mv_all", [P, LANES, 2, 2])
        mv = [mv_all[:, p, :, :] for p in range(LANES)]
        var_eps, inv_root, half, shift = (sb(n_, [P, LANES, 2]) for n_ in ("var_eps", "inv_root", "half", "shift"))
        z = lanes("z", [P, 2, D])
        zT = lanes("zT", [P, S])
        probs_all = sb("probs_all", [P, 16, S])
        probs = [probs_all[:, 2 * i:2 * i + 2, :] for i in range(8)]
        zm = [probs_all[:, 0:E, :], probs_all[:, E:2 * E, :]]
        wa = [probs_all[:, 4 * p:4 * p + 2, :] for p in range(LANES)]
        ga = [probs_all[:, 4 * p + 2:4 * p + 4, :] for p in range(LANES)]
        ha = wa
        ytmp = lanes("ytmp", [P, S])
        parts = lanes("parts", [P, 3, S], BF16)
        rest = lanes("rest", [P, S])
        kst_all = sb("kst_all", [P, 2 * LANES * 8, S], BF16)
        kst = [[kst_all[:, 8 * (LANES * l + p):8 * (LANES * l + p) + 8, :] for p in range(LANES)] for l in range(2)]
        qst_all = sb("qst_all", [P, LANES * 8, S], BF16)
        qst = [qst_all[:, 8 * p:8 * p + 8, :] for p in range(LANES)]
        vx = [lanes(f"vx{l}_", [P, 2, H, 9]) for l in range(2)]
        mvx = lanes("mvx", [P, 2, H, 9])
        mx = lanes("mx", [P, 2, H])
        emx = lanes("emx", [P, 2, H])
        mparts = lanes("mparts", [H, 3, S], BF16)
        mrest = lanes("mrest", [H, S])
        maski = probs[0].bitcast(I32)
        stmp = probs_all[:, 2, :]
        wg_nat = probs_all[0:E, 3, 0:P]
        row_parts = probs_all[0:1, 9:12, :].rearrange("p a n -> p (a n)").bitcast(BF16)[:, 0:9 * P].rearrange(
            "p (s a n) -> p s a n", s=3, a=3)
        row_rest = probs_all[0:1, 13:15, :].rearrange("p a n -> p (a n)")[:, 0:3 * P].rearrange("p (a n) -> p a n", a=3)
        svrow, svs = probs_all[0:1, 4, 0:P], probs_all[0:1, 4, P:S]
        qk_perm = probs_all[0:1, 7:9, :].rearrange("p a (b n) -> p (a b) n", b=2)
        qk_rows = probs_all[0:1, 5:7, :].rearrange("p a (b n) -> p (a b) n", b=2)
        oT = [sb(f"oT{i}", [P, S]) for i in range(2)]
        onums = [sb(f"onum{i}", [P, 2, 4, 9]) for i in range(2)]
        orecs = [sb(f"orec{i}", [P, 2, 4]) for i in range(2)]
        turned = sb("turned", [P, 2 * LANES, S])
        ctxT = [turned[:, p, :] for p in range(LANES)]
        att = [t.rearrange("p (t d) -> p t d", t=2) for t in ctxT]
        attT = [turned[:, LANES + p, :] for p in range(LANES)]
        lexp = [t.rearrange("p (t d) -> p t d", t=2) for t in attT]
        lmax = lanes("lmax", [P, 8])
        hot = lanes("hot", [P, 2, E])
        hotT = [mrest[p][0:E, :] for p in range(LANES)]
        hotTb = [mparts[p][0:E, 0, :] for p in range(LANES)]
        kb = [parts[p][:, 0, :] for p in range(LANES)]
        qb = [parts[p][:, 1, :] for p in range(LANES)]
        th = lanes("th", [P, 384])
        ctx_in = [th[p][:, 0:S].rearrange("p (t d) -> p t d", t=2) for p in range(LANES)]
        aw = th
        junk = [[t[p][:, :].bitcast(BF16).rearrange("p (i k) -> p i k", i=2) for t in (ytmp, rest)] for p in range(LANES)]

        qst_f = qst_all[:, :, :].rearrange("p a n -> p (a n)").bitcast(F32)
        w1T = qst_f[:, 0:2 * E * P].rearrange("p (a n) -> p a n", n=P)
        w3T = qst_f[:, 2 * E * P:4 * E * P].rearrange("p (a n) -> p a n", n=P)
        w2T = turned[:, :, :].rearrange("p a (b n) -> p (a b) n", n=P)
        kst_f = kst_all[:, :, :].rearrange("p a n -> p (a n)").bitcast(F32)
        zT6, xgT, xg = (kst_f[:, 2 * E * P * i:2 * E * P * (i + 1)].rearrange("p (a n) -> p a n", n=P) for i in range(3))
        sc, ex, eq, cum = er[:, 0:P], er[:, P:S], ei[:, 0:P], ei[:, P:S]
        sel, pos = t1[:, 0:P], t1[:, P:S]
        g = sb("g", [P, 64])
        uthr = sb("uthr", [P, 12], I32)
        V, DB, F, NF = uthr[:, 0:1], uthr[:, 1:2], uthr[:, 2:5], uthr[:, 5:8]
        shifted = sb("shifted", [P, 16, 3], I32)
        cntb = sb("cntb", [P, 4], BF16)
        cand = [eq, cum, sel]
        m8 = ytmp[0][0:1, :]
        probs_b = probs_all[:, :, :].rearrange("p a n -> p (a n)").bitcast(BF16)
        hot_high = probs_b[:, 0:P * 16].rearrange("p (n k) -> p n k", k=16)
        hot_low = probs_b[:, P * 16:2 * P * 16].rearrange("p (n k) -> p n k", k=16)
        place = probs_b[:, 2 * P * 16:4 * P * 16].rearrange("p (v n k) -> p v n k", v=2, k=16)
        slot_i, high_i = ei[:, 0:P].bitcast(I32), t2[:, P:S].bitcast(I32)
        high_f, low_f = t2[:, 0:P], t1[:, P:S]
        idpair = sb("idpair", [16, 32 * E])
        idrows = sb("idrows", [16, E, 16], I32)
        ids = sb("ids", [P, 2 * E], I32)
        wslot = sb("wslot", [P, 2 * E])
        wlog = sb("wlog", [P, 2 * E])
        nm8 = sb("nm8", [P, E])
        rs8 = sb("rs8", [P, E])
        act1 = [probs_all[:, 8 + 2 * i:10 + 2 * i, :] for i in range(2)]
        hT = [probs_all[:, 12 + 2 * i:14 + 2 * i, :] for i in range(2)]
        ysc = [oT[i][:, :].rearrange("p (i c) -> p i c", i=2) for i in range(2)]

        def dram(name, shape, dt):
            return nc.dram_tensor(name, shape, dt, kind="Internal").ap()

        kscr = [[dram(f"kscr{l}{p}", (SPLITS, P, S), BF16) for p in range(LANES)] for l in range(2)]
        qscr = [dram(f"qscr{p}", (SPLITS, P, S), BF16) for p in range(LANES)]
        mscr = [dram(f"mscr{p}", (H, 3, S), BF16) for p in range(LANES)]
        idscr = dram("idscr", (E, CAP), I32)
        zrows = dram("zrows", (B * S, D), F32)

        ld_small, ld_x, ld_moe = sem("ld_small"), sem("ld_x"), sem("ld_moe")
        pool_const, pool_step = sem("pool_const"), sem("pool_step")
        act_setup, dve_setup = sem("act_setup"), sem("dve_setup")
        setup_ps, setup_act = sem("setup_ps"), sem("setup_act")
        dve_chain = sem("dve_chain")
        tab_sq, tab_pow = sem("tab_sq"), sem("tab_pow")
        rows_split, rows_ld = sem("rows_split"), sem("rows_ld")
        ctx_ld = [sem(f"ctx_ld{p}") for p in range(LANES)]
        ctxT_psum, ctxT_ready = sem("ctxT_psum"), sem("ctxT_ready")
        k_raw = sem("k_raw")
        k_psum, k_split = sem("k_psum"), [sem(f"k_split{l}") for l in range(2)]
        v_psum, v_ready = sem("v_psum"), sem("v_ready")
        mv_psum, mv_ready = sem("mv_psum"), sem("mv_ready")
        k_stored = [sem(f"k_stored{p}") for p in range(LANES)]
        k_stacked = [sem(f"k_stacked{p}") for p in range(LANES)]
        ln_stats, ln_rstd, z_ready = sem("ln_stats"), sem("ln_rstd"), sem("z_ready")
        zT_psum, zT_ready = sem("zT_psum"), sem("zT_ready")
        w_psum, scan_done, h_ready = sem("w_psum"), sem("scan_done"), sem("h_ready")
        y_psum = sem("y_psum")
        q_psum, q_split = sem("q_psum"), sem("q_split")
        q_high, q_rest, q_mid = sem("q_high"), sem("q_rest"), sem("q_mid")
        q_stored = [sem(f"q_stored{p}") for p in range(LANES)]
        q_stacked = [sem(f"q_stacked{p}") for p in range(LANES)]
        s_psum, s_maxed = sem("s_psum"), sem("s_maxed")
        mT_psum, m_split = sem("mT_psum"), sem("m_split")
        m_neg, emx_ready = sem("m_neg"), sem("emx_ready")
        m_stored = [sem(f"m_stored{p}") for p in range(LANES)]
        m_stacked = [sem(f"m_stacked{p}") for p in range(LANES)]
        st_psum, exp_done = sem("st_psum"), sem("exp_done")
        pv_done, o_evac = sem("pv_done"), sem("o_evac")
        t_psum, norm_done = sem("t_psum"), sem("norm_done")
        attT_psum, attT_ready = sem("attT_psum"), sem("attT_ready")
        lg_psum, lg_copied, lg_max, lg_exp = sem("lg_psum"), sem("lg_copied"), sem("lg_max"), sem("lg_exp")
        hot_ready, hotT_psum, hotT_ready = sem("hot_ready"), sem("hotT_psum"), sem("hotT_ready")
        bc_psum, zm_ready = sem("bc_psum"), sem("zm_ready")
        sign_ready, qb_ready, sg_psum = sem("sign_ready"), sem("qb_ready"), sem("sg_psum")
        tanh_done, aw_ready = sem("tanh_done"), sem("aw_ready")
        rows_out = sem("rows_out")
        zT6_psum, zT6_ready, gate_psum = sem("zT6_psum"), sem("zT6_ready"), sem("gate_psum")
        cmax_ready, cmaxT_psum, m8_ready, mbc_psum = sem("cmax_ready"), sem("cmaxT_psum"), sem("m8_ready"), sem("mbc_psum")
        nm_ready, gate_exp = sem("nm_ready"), sem("gate_exp")
        cnt_ready, tot_psum = sem("cnt_ready"), sem("tot_psum")
        ties_ready, ties_psum = sem("ties_ready"), sem("ties_psum")
        sel_ready, sel_psum = sem("sel_ready"), sem("sel_psum")
        pos_ready, pos_psum = sem("pos_ready"), sem("pos_psum")
        moe_turned, moe_wT = sem("moe_turned"), sem("moe_wT")
        hot_low_ready = sem("hot_low_ready")
        hot_tiles, id_psum, idrows_ready = sem("hot_tiles"), sem("id_psum"), sem("idrows_ready")
        ids_stored, ids_ready = sem("ids_stored"), sem("ids_ready")
        ws_added = sem("ws_added")
        gathered = [sem(f"gathered{i}") for i in range(2 * E)]
        xgT_psum, xgT_ready, ws_psum, wslot_ready = sem("xgT_psum"), sem("xgT_ready"), sem("ws_psum"), sem("wslot_ready")
        up_psum, tanh1_done, hT_ready = sem("up_psum"), sem("tanh1_done"), sem("hT_ready")
        down_psum, y_ready = sem("down_psum"), sem("y_ready")
        scattered = [sem(f"scattered{i}") for i in range(2)]

        block = ctx.enter_context(nc.Block())

        def nth(r, p, n=1, k=None):
            return (LANES * r + p) * n + (n if k is None else k)

        def nth_ln(r, i, p):
            return r * NLN * LANES + i * LANES + p + 1

        def nth_zp(r, i, p):
            return r * (NLN - 1) * LANES + i * LANES + p + 1

        def y_no(r, i, p):
            return (r * 5 + i) * LANES + p + 1

        def tile_no(r, l, p, u):
            return ((r * 2 + l) * LANES + p) * NTILE + u

        def wait(eng, s, v):
            if isinstance(v, int) and v <= 0:
                return
            eng.wait_ge(s, v)

        AHEAD = ((0, 5), (5, 11), (11, 16), (16, 16))
        EARLY = 8

        def ahead(l, p, q):
            return ((EARLY, 13), (13, 16), (16, 16), (16, 16))[q] if l == 1 and p == 0 else AHEAD[q]

        def head_at(h):
            return 64 * (h // 8), h % 8

        def xs(r, p):
            return x_all[:, bass.ds(2 * (LANES * r + p), 2), :] if not isinstance(r, int) else \
                x_all[:, 2 * (LANES * r + p):2 * (LANES * r + p) + 2, :]

        def z6s(r, p):
            t = 2 * (LANES * r + p)
            return z6[:, bass.ds(t, 2), :] if not isinstance(r, int) else z6[:, t:t + 2, :]

        def rounds(eng, body):
            body(0)
            for r in range(1, ROUNDS):
                body(r)

        turn = [([nat[:, i, :] for i in range(4 * j, 4 * j + 4)], wT[:, 4 * j:4 * j + 4, :]) for j in range(2)]
        turn.append(([nat[:, 8, :], nat[:, 9, :]], wT[:, 8:10, :]))
        NTURN = len(turn)
        turn_moe = []
        for src, dst in ((w1n, w1T), (w3n, w3T)):
            turn_moe += [([src[:, i, :] for i in range(4 * j, 4 * j + 4)], dst[:, 4 * j:4 * j + 4, :]) for j in range(4)]
        turn_moe += [([w2n[:, 2 * j + i // 2, P * (i % 2):P * (i % 2) + P] for i in range(4)],
                      w2T[:, 4 * j:4 * j + 4, :]) for j in range(4)]
        AHEAD_E = 5
        DIGITS = [(b, 2) for b in range(29, 0, -2)] + [(0, 1)]
        N_SMALL = 15 + 4 + 6 + 4

        @block.sync
        def _(sp):
            small = [
                (nat[:, WQ, :], a["L0_xattn_Wq"]), (nat[:, WQ + 1, :], a["L1_xattn_Wq"]),
                (nat[:, WK, :], a["L0_xattn_Wk"]), (nat[:, WK + 1, :], a["L1_xattn_Wk"]),
                (nat[:, WV, :], a["L0_xattn_Wv"]), (nat[:, WV + 1, :], a["L1_xattn_Wv"]),
                (nat[:, WO, :], a["L0_xattn_Wo"]), (nat[:, WO + 1, :], a["L1_xattn_Wo"]),
                (nat[:, SB, :], a["L0_attn_B"]), (nat[:, SC, :], a["L0_attn_C"]),
                (w_hash[:, :], a["L0_ffn_Wg"]), (w_exp[:, :, :], a["L0_ffn_We"].rearrange("e d f -> d e f")),
                (b_exp[:, :], a["L0_ffn_be"]), (wg_nat, a["L1_ffn_Wg"]),
                (maski, a["mask_SxS2_ik0"].rearrange("(t p) k -> p t k", p=P)),
            ]
            for i, n in enumerate(("L0_xattn_bq", "L1_xattn_bq", "L0_xattn_bk", "L1_xattn_bk")):
                small.append((qk_rows[:, i, :], a[n].rearrange("(o n) -> o n", o=1)))
            for i, n in enumerate(("L0_xattn_bo", "L1_xattn_bo", "L0_ffn_bg")):
                small.append((rows[0:1, i, :], a[n].rearrange("(o n) -> o n", o=1)))
            small.append((svrow, a["L1_attn_bv_v"].rearrange("(o n) -> o n", o=1)))
            for c, n in ((CV, "L0_xattn_bv"), (CV + 1, "L1_xattn_bv"), (CAR, "L0_attn_A_real"), (CAI, "L0_attn_A_imag"), (CSQ, "L1_attn_bv_q"), (CSK, "L1_attn_bv_k")):
                small.append((cols[:, c:c + 1], a[n].rearrange("(n o) -> n o", o=1)))
            assert len(small) == N_SMALL
            for dst, src in small:
                sp.dma_start(dst, src).then_inc(ld_small, 16)
            sp.dma_start(x_all[:, :, :], a["x"].rearrange("b (t p) d -> p (b t) d", p=P)).then_inc(ld_x, 16)
            sp.dma_start(w1n[:, :, :], a["L1_ffn_W1"].rearrange("e (t p) c -> p (e t) c", p=P)).then_inc(ld_moe, 16)
            sp.dma_start(w3n[:, :, :], a["L1_ffn_W3"].rearrange("e (t p) c -> p (e t) c", p=P)).then_inc(ld_moe, 16)
            sp.dma_start(w2n[:, :, :], a["L1_ffn_W2"].rearrange("e c h -> c e h")).then_inc(ld_moe, 16)

            K_PARTS, Q_PARTS = ((0, 0, 0), (1, 1), (2,)), ((0, 1, 2), (0, 1), (0,))

            sp.wait_ge(rows_split, 1)
            for j in range(3):
                sp.dma_start(rows3[j:j + 1, :, :], row_parts[:, j, :, :]).then_inc(rows_ld, 16)

            def store_parts(p, scr, plan, s):
                slot = 0
                for run in plan:
                    n = len(run)
                    src = parts[p][:, run[0]:run[0] + 1, :].to_broadcast([P, n, S]) if run[0] == run[-1] else \
                        parts[p][:, 0:n, :]
                    sp.dma_start(scr[slot:slot + n].rearrange("s p n -> p s n"), src).then_inc(s, 16)
                    slot += n

            def load_stack(dst, scr, s):
                rows_ = scr.rearrange("s (d e t) n -> e (s d) t n", d=HD, e=2)
                for e in range(2):
                    sp.dma_start(dst[64 * e:64 * e + MROW, :, :], rows_[e]).then_inc(s, 16)

            def stack_q(r, l, p):
                sp.wait_ge(q_stored[p], 16 * 3 * (2 * r + l + 1))
                load_stack(qst[p], qscr[p], q_stacked[p])

            def body(r):
                for p in range(LANES):
                    if r > 0:
                        sp.wait_ge(y_psum, y_no(r - 1, 3, p))
                    sp.dma_start(ctx_in[p][:, :, :],
                                 a["ctx_1024"][LANES * r + p].rearrange("(t p) d -> p t d", p=P)).then_inc(ctx_ld[p], 16)
                keys(r, 0)
                for l in range(2):
                    for p in range(LANES):
                        sp.wait_ge(q_split, nth(r, p) + l * LANES + r * LANES)
                        store_parts(p, qscr[p], Q_PARTS, q_stored[p])
                        if p > 0:
                            stack_q(r, l, p - 1)
                    stack_q(r, l, LANES - 1)
                    for p in range(LANES):
                        sp.wait_ge(m_split, nth(r, p) + l * LANES + r * LANES)
                        sp.dma_start(mscr[p], mparts[p][:, :, :]).then_inc(m_stored[p], 16)
                        sp.wait_ge(m_stored[p], 16 * (2 * r + l + 1))
                        for e in range(2):
                            sp.dma_start(qst[p][64 * e + MROW:64 * e + KROWS, :, :],
                                         mscr[p][8 * e:8 * e + 8].rearrange("t j n -> j t n")).then_inc(m_stacked[p], 16)
                        if l == 0 and p == 0:
                            keys(r, 1)

            def keys(r, l):
                for p in range(LANES):
                    sp.wait_ge(k_split[l], nth(r, p))
                    store_parts(p, kscr[l][p], K_PARTS, k_stored[p])
                for p in range(LANES):
                    sp.wait_ge(k_stored[p], 16 * 3 * (2 * r + l + 1))
                    sp.wait_ge(pool_const, 4)
                    load_stack(kst[l][p], kscr[l][p], k_stacked[p])

            rounds(sp, body)
            sp.wait_ge(z_ready, NLN * B)
            sp.dma_start(zrows.rearrange("(t p) d -> p t d", p=P), z6[:, :, :]).then_inc(rows_out, 16)
            sp.dma_start(out.rearrange("b (t p) d -> p (b t) d", p=P), x_all[:, :, :]).then_inc(rows_out, 16)
            sp.wait_ge(idrows_ready, 1)
            sp.dma_start(idscr.rearrange("e (h l) -> h e l", l=16), idrows[:, :, :]).then_inc(ids_stored, 16)
            sp.wait_ge(ids_stored, 16)
            sp.dma_start(ids[:, :].rearrange("p (e i) -> p e i", i=2), idscr.rearrange("e (p i) -> p e i", i=2)
                         ).then_inc(ids_ready, 16)
            sp.wait_ge(rows_out, 32)
            for i in range(2):
                sp.wait_ge(scattered[i], 16 * E)


        @block.gpsimd
        def _(pool):
            n = [0]

            def step(ins):
                n[0] += 1
                ins.then_inc(pool_step, 1)
                pool.wait_ge(pool_step, n[0])

            step(pool.memset(ident[:, :], 0.0))
            step(pool.affine_select(out=ident[:, :], in_=ident[:, :], compare_op=ALU.not_equal, fill=1.0,
                                    base=0, pattern=[[-1, P]], channel_multiplier=1))
            pool.memset(ones[:, :], 1.0)
            pool.memset(rdec[:, :], 1.0).then_inc(pool_const, 1)
            pool.memset(wg_pad[:, :], 0.0)
            pool.memset(ones3[:, :], 1.0)
            pool.tensor_copy(identb[:, :], ident[:, :]).then_inc(pool_const, 1)
            for p in range(LANES):
                for l in range(2):
                    pool.memset(vx[l][p][:, :, :, :], 1.0)
            pool.memset(half[:, :, :], -0.5).then_inc(pool_const, 1)
            pool.wait_ge(tab_sq, 1)
            pool.tensor_tensor(sv[:, 12:13], sv[:, 10:11], sv[:, 11:12], ALU.pow).then_inc(tab_pow, 1)
            pool.wait_ge(tab_pow, 1)
            step(pool.memset(kst_f[32:64, :], 1.0 + 0x3F80 / float(2 ** 23)))
            pool.memset(kst_f[96:128, :], 1.0 + 0x3F80 / float(2 ** 23)).then_inc(pool_const, 1)
            pool.wait_ge(pool_const, 4)

            def constants():
                pool.iota(iota_rev[:, :], pattern=[[-1, P]], base=P, channel_multiplier=0,
                          allow_small_or_imprecise_dtypes=True)
                pool.iota(iota16[:, :], pattern=[[1, 16]], base=0, channel_multiplier=0,
                          allow_small_or_imprecise_dtypes=True)
                pool.iota(tokp[:, :], pattern=[[0, 2]], base=0, channel_multiplier=1,
                          allow_small_or_imprecise_dtypes=True)
                pool.iota(tilec[:, :], pattern=[[1, NT]], base=0, channel_multiplier=0,
                          allow_small_or_imprecise_dtypes=True)
                pool.iota(digits[:, :], pattern=[[1, 3]], base=1, channel_multiplier=0)
                step(pool.memset(halfmask[:, :], 0.5))
                for c in (0, 256):
                    step(pool.affine_select(out=halfmask[:, c:c + P], in_=halfmask[:, c:c + P], compare_op=ALU.is_ge,
                                            fill=0.0, base=0, pattern=[[1, P]], channel_multiplier=-1))
                step(pool.memset(selb[:, :, :], 0.0))
                step(pool.affine_select(out=selb[:, :, :], in_=selb[:, :, :], compare_op=ALU.not_equal, fill=1.0,
                                        base=0, pattern=[[-1, E], [0, P]], channel_multiplier=1))
                step(pool.memset(emask[:, :], 0.0))
                for i in range(NT):
                    step(pool.affine_select(out=emask[:, :], in_=emask[:, :], compare_op=ALU.not_equal, fill=1.0,
                                            base=-E * i, pattern=[[-1, E]], channel_multiplier=1))
                step(pool.tensor_copy(below[:, :].rearrange("p (c e) -> p c e", e=E),
                                      emask[:, :].unsqueeze(1).to_broadcast([P, NT, E])))
                pool.tensor_copy(blockf[:, :], below[:, :])
                step(pool.tensor_copy(blockb[:, :], below[:, :]))
                pool.affine_select(out=below[:, :].rearrange("p (c e) -> p c e", e=E),
                                   in_=below[:, :].rearrange("p (c e) -> p c e", e=E), compare_op=ALU.is_gt,
                                   fill=0.0, base=0, pattern=[[E, NT], [0, E]], channel_multiplier=-1
                                   ).then_inc(pool_const, 1)

            def norm(r, i, p, n_):
                at = slice(p, p + n_)
                pool.wait_ge(ln_stats, nth_ln(r, i, p + n_ - 1))
                pool.tensor_scalar(shift[:, at, :], mv_all[:, at, :, 0], -1.0, None, ALU.mult)
                step(pool.tensor_scalar(var_eps[:, at, :], mv_all[:, at, :, 1], 1e-5, None, ALU.add))
                ins = pool.tensor_tensor(inv_root[:, at, :], var_eps[:, at, :], half[:, at, :], ALU.pow)
                if i != 3:
                    step(ins)
                    ins = pool.tensor_tensor(shift[:, at, :], shift[:, at, :], inv_root[:, at, :], ALU.mult)
                ins.then_inc(ln_rstd, n_)

            def split(r, p):
                pool.wait_ge(k_raw, nth(r, p))
                if r > 0:
                    pool.wait_ge(q_stored[p], 16 * 3 * 2 * r)
                src = ytmp[p][:, :]
                step(pool.tensor_copy(parts[p][:, 0, :], src))
                step(pool.tensor_tensor(rest[p][:, :], src, parts[p][:, 0, :], ALU.subtract))
                step(pool.tensor_copy(parts[p][:, 1, :], rest[p][:, :]))
                pool.tensor_tensor(parts[p][:, 2, :], rest[p][:, :], parts[p][:, 1, :], ALU.subtract).then_inc(k_split[0], 1)

            def body(r):
                for i in range(NLN):
                    for p, n_ in ((1, 2), (3, 1)) if i == 1 else {1: ((0, 1), (1, 2), (3, 1)), 2: ((0, 2), (2, 1), (3, 1))}.get(i % 3, ((0, 2), (2, 2))):
                        norm(r, i, p, n_)
                    if i == 0:
                        for p in range(LANES):
                            if p == LANES - 1:
                                norm(r, 1, 0, 1)
                            split(r, p)
                    if i == 1 and r == 0:
                        constants()

            rounds(pool, body)

            def gather(e):
                for k in (2 * e, 2 * e + 1):
                    pool.indirect_dma_start(out=xg[:, k, :], out_offset=None, in_=zrows[:, :],
                                            in_offset=bass.IndirectOffsetOnAxis(ap=ids[:, k:k + 1], axis=0)
                                            ).then_inc(gathered[k], 16)

            def scatter(e):
                pool.wait_ge(y_ready, e + 1)
                if e > 0:
                    pool.wait_ge(scattered[0], 16 * e)
                    pool.wait_ge(scattered[1], 16 * e)
                for i in range(2):
                    k = 2 * e + i
                    pool.indirect_dma_start(out=out.rearrange("b s d -> (b s) d"),
                                            out_offset=bass.IndirectOffsetOnAxis(ap=ids[:, k:k + 1], axis=0),
                                            in_=ysc[e % 2][:, i, :], in_offset=None, compute_op=ALU.add,
                                            ).then_inc(scattered[i], 16)

            pool.wait_ge(hot_low_ready, 1)
            pool.tensor_tensor(place[:, 1, :, :].rearrange("p (c e) k -> p c (e k)", e=E),
                               hot_low.rearrange("p (c e) k -> p c (e k)", e=E),
                               tilec[:, :].unsqueeze(2).to_broadcast([P, NT, E * 16]), ALU.mult).then_inc(hot_tiles, 1)
            pool.wait_ge(rows_out, 32)
            pool.wait_ge(ids_ready, 16)
            for e in range(AHEAD_E):
                gather(e)
            for e in range(E):
                scatter(e)
                if e + AHEAD_E < E:
                    gather(e + AHEAD_E)

        @block.scalar
        def _(act):
            def copy(o, i):
                return act.activation(o, i, ACT.Copy)

            act.wait_ge(ld_small, 16 * N_SMALL)
            act.wait_ge(pool_const, 3)
            act.activation(sgn[:, 0:2], cols[:, CSQ:CSQ + 2], ACT.Sign)
            copy(qk_perm.rearrange("p k (d h) -> p k h d", d=HD), qk_rows.rearrange("p k (h d) -> p k h d", d=HD))
            act.activation(svs, svrow, ACT.Sign).then_inc(act_setup, 1)
            for i in range(NTURN):
                act.wait_ge(setup_ps, i + 1)
                n = len(turn[i][0]) * P
                src, dst = banks[i][:, 0:n].rearrange("p (k n) -> p k n", n=P), turn[i][1]
                if i == 0:
                    src = src.rearrange("p k (h d) -> p k h d", d=HD)
                    dst = dst.rearrange("p k (d h) -> p k h d", d=HD)
                copy(dst, src).then_inc(setup_act, 1)

            def norm_apply(r, i, p):
                o = z6s(r, p) if i == NLN - 1 else z[p]
                act.wait_ge(ln_rstd, nth_ln(r, i, p))
                for t in range(2):
                    ins = act.activation(o[:, t, :], xs(r, p)[:, t, :], ACT.Identity, bias=shift[:, p, t:t + 1],
                                         scale=inv_root[:, p, t:t + 1])
                ins.then_inc(z_ready, 1)

            def zt(r, i, p):
                act.wait_ge(zT_psum, nth_zp(r, i, p))
                copy(zT[p][:, :], work_ps[p][:, 0:S]).then_inc(zT_ready, 1)

            def exps(r, l, p, v):
                n = tile_no(r, l, p, v)
                act.wait_ge(st_psum, n + 1)
                wait(act, pv_done, (n // 4 if isinstance(n, int) else quad_no(r, l, p, v // 4)) - 1)
                act.activation(probs[v % 8][:, :, :], st_ps[v % 2][:, :], ACT.Exp, scale=SCALE).then_inc(exp_done, 1)

            def quad_no(r, l, p, q):
                return ((r * 2 + l) * LANES + p) * NQUAD + q

            def evac(r, l, p, q):
                n = quad_no(r, l, p, q)
                act.wait_ge(pv_done, n + 1)
                wait(act, t_psum, n - 1)
                copy(oT[q % 2][:, :], quad_ps[q % 2][:, 0:S]).then_inc(o_evac, 1)

            def high(r, l, p):
                act.wait_ge(q_psum, (2 * r + l) * LANES + p + 1)
                act.wait_ge(k_stored[p], 16 * 3 * (2 * r + l + 1))
                act.activation(parts[p][:, 0, :], work_ps[p][:, S:2 * S], ACT.Identity,
                               bias=cols[:, CQ + l:CQ + l + 1]).then_inc(q_high, 1)

            def mid(r, l, p):
                act.wait_ge(q_rest, (2 * r + l) * LANES + p + 1)
                copy(parts[p][:, 1, :], rest[p][:, :]).then_inc(q_mid, 1)

            def turned_out(r, l, p):
                act.wait_ge(attT_psum, r * 2 * LANES + l * LANES + p + 1)
                copy(attT[p], out_ps(p)[:, 0:S]).then_inc(attT_ready, 1)

            def body(r):
                for p in range(LANES):
                    act.wait_ge(ctxT_psum, nth(r, p))
                    copy(ctxT[p][:, :], work_ps[p][:, 0:S]).then_inc(ctxT_ready, 1)
                for p in range(LANES):
                    norm_apply(r, 0, p)
                def vals(p, l):
                    act.wait_ge(v_psum, r * 2 * LANES + l * LANES + p + 1)
                    copy(vx[l][p][:, :, :, 0:HD],
                         value_ps[p][:, 0:S].rearrange("p (t h d) -> p t h d", h=H, d=HD)).then_inc(v_ready, 1)

                for p in range(LANES):
                    act.wait_ge(k_psum, 2 * r * LANES + p + 1)
                    act.activation(ytmp[p][:, :], work_ps[p][:, S:2 * S], ACT.Identity,
                                   bias=cols[:, CK:CK + 1]).then_inc(k_raw, 1)
                for p in range(LANES):
                    vals(p, 0)
                for p in range(LANES):
                    zt(r, 0, p)
                for p in range(LANES):
                    vals(p, 1)
                for p in range(LANES):
                    act.wait_ge(mv_psum, nth(r, p))
                    copy(mvx[p][:, :, :, :], value_ps[p][:, 0:2 * H * 9]).then_inc(mv_ready, 1)
                for l in range(2):
                    if l == 1:
                        for p in range(LANES):
                            zt(r, 2, p)
                        for p in range(LANES):
                            act.wait_ge(lg_psum, nth(r, p))
                            copy(lexp[p][:, :, :], work_ps[p][:, S:2 * S]).then_inc(lg_copied, 1)
                        for p in range(LANES):
                            act.wait_ge(lg_max, nth(r, p))
                            for t in range(2):
                                ins = act.activation(th[p][:, P * t:P * t + P], lexp[p][:, t, :], ACT.Exp,
                                                     bias=lmax[p][:, 2 + t:3 + t], accum_out=lmax[p][:, 4 + t:5 + t])
                            ins.then_inc(lg_exp, 1)
                        for p in range(LANES):
                            act.wait_ge(hotT_psum, nth(r, p))
                            copy(hotT[p][:, :], work_ps[p][0:E, 0:S])
                            copy(hotTb[p][:, :], work_ps[p][0:E, 0:S]).then_inc(hotT_ready, 1)
                        for p in range(LANES):
                            act.wait_ge(zT_psum, nth_zp(r, 3, p))
                            act.activation(kb[p][:, :], work_ps[p][:, 0:S], ACT.Sign).then_inc(sign_ready, 1)
                        for p in range(LANES):
                            act.wait_ge(sg_psum, nth(r, p))
                            act.activation(th[p][:, :], work_ps[p][:, 0:384], ACT.Tanh,
                                           scale=2.0 / float(D) ** 0.5).then_inc(tanh_done, 1)
                    norm_apply(r, 1 + 3 * l, 0)
                    zt(r, 1 + 3 * l, 0)
                    norm_apply(r, 1 + 3 * l, 1)
                    high(r, l, 0)
                    norm_apply(r, 1 + 3 * l, 2)
                    mid(r, l, 0)
                    zt(r, 1 + 3 * l, 1)
                    norm_apply(r, 1 + 3 * l, 3)
                    high(r, l, 1)
                    zt(r, 1 + 3 * l, 2)
                    mid(r, l, 1)
                    zt(r, 1 + 3 * l, 3)
                    high(r, l, 2)
                    high(r, l, 3)
                    mid(r, l, 2)
                    mid(r, l, 3)
                    for p in range(LANES):
                        if l == 1:
                            act.wait_ge(m_neg, nth(r, p))
                            act.activation(emx[p][:, :, :], emx[p][:, :, :], ACT.Exp).then_inc(emx_ready, 1)
                        for q in range(NQUAD):
                            for i in range(4):
                                exps(r, l, p, 4 * q + i)
                            if q == 0 and p > 0:
                                turned_out(r, l, p - 1)
                            if q >= 1:
                                evac(r, l, p, q - 1)
                        if p == LANES - 1:
                            for pp in range(LANES - 1):
                                norm_apply(r, 2 + 3 * l, pp)
                        evac(r, l, p, NQUAD - 1)
                    turned_out(r, l, LANES - 1)
                    norm_apply(r, 2 + 3 * l, LANES - 1)

            rounds(act, body)

            for j in range(4):
                act.wait_ge(zT6_psum, j + 1)
                copy(zT6[:, 4 * j:4 * j + 4, :], banks[j][:, :]).then_inc(zT6_ready, 1)
            act.wait_ge(nm_ready, 1)
            act.activation(ex[:, :], sc[:, :], ACT.Exp, bias=g[:, 2:3]).then_inc(gate_exp, 1)
            for i in range(len(turn_moe)):
                act.wait_ge(moe_turned, i + 1)
                copy(turn_moe[i][1], turn_bank(i)[:, :].rearrange("p (k n) -> p k n", n=P)).then_inc(moe_wT, 1)
            def turned_in(e):
                act.wait_ge(xgT_psum, e + 1)
                copy(xgT[:, 2 * e:2 * e + 2, :], lane_ps[e % 2][:, 0:S]).then_inc(xgT_ready, 1)

            def gated(e):
                act.wait_ge(up_psum, e + 1)
                if e >= 2:
                    act.wait_ge(hT_ready, e - 1)
                act.activation(act1[e % 2], score_ps[e % 2][:, :], ACT.Tanh, scale=0.5).then_inc(tanh1_done, 1)
                act.wait_ge(ws_added, e + 1)
                act.activation(wslot[:, 2 * e:2 * e + 2], wlog[:, 2 * e:2 * e + 2], ACT.Exp).then_inc(wslot_ready, 1)

            turned_in(0)
            turned_in(1)
            for e in range(E):
                gated(e)
                if e + 2 < E:
                    turned_in(e + 2)

        @block.tensor
        def _(pe):
            mm = nc.tensor.matmul
            tr = nc.tensor.transpose
            pe.wait_ge(pool_const, 1)
            pe.wait_ge(ld_small, 16 * N_SMALL)
            for i, (srcs, _) in enumerate(turn):
                for k, s in enumerate(srcs):
                    ins = tr(banks[i][:, P * k:P * k + P], s, ident[:, :])
                ins.then_inc(setup_ps, 1)
            pe.wait_ge(setup_act, 2)
            for l in range(2):
                mm(lane_ps[0][0:1, P * l:P * l + P], cols[:, CV + l:CV + l + 1], wT[:, WO + l, :], start=True, stop=True)
            tr(o_ps[:, 0:E], wg_nat, ident[0:E, 0:E])
            pe.wait_ge(act_setup, 1)
            for i in range(4):
                mm(o_ps[:, E + i:E + i + 1], qk_perm[:, i, :], ones[0:1, 0:1], start=True, stop=True)
            mm(o_ps[:, 256:384], ones[0:1, :], svs, start=True, stop=True).then_inc(setup_ps, 1)
            pe.wait_ge(dve_setup, 1)
            for kt in range(2):
                for qt in range(2):
                    ins = tr(t_ps[:, S * kt + P * qt:S * kt + P * qt + P], mask[:, qt, P * kt:P * kt + P], ident[:, :])
            ins.then_inc(setup_ps, 1)
            pe.wait_ge(setup_act, NTURN)
            pe.wait_ge(dve_setup, 2)
            pe.wait_ge(rows_split, 1)

            def quad_no(r, l, p, q):
                return ((r * 2 + l) * LANES + p) * NQUAD + q

            def zt(r, i, p):
                pe.wait_ge(z_ready, nth_ln(r, i, p))
                for t in range(2):
                    ins = tr(work_ps[p][:, P * t:P * t + P], z[p][:, t, :], ident[:, :])
                ins.then_inc(zT_psum, 1)

            def score_tile(r, l, p, u):
                n = tile_no(r, l, p, u)
                if u == 0:
                    if l == 0 and p == 0:
                        pe.wait_ge(mv_ready, LANES * (r + 1))
                    pe.wait_ge(q_stacked[p], 16 * 2 * (2 * r + l + 1))
                    pe.wait_ge(k_stacked[p], 16 * 2 * (2 * r + l + 1))
                wait(pe, s_maxed, n - 1)
                qt, pair = u // 8, u % 8
                for i in range(2):
                    r0, t = head_at(2 * pair + i)
                    ins = mm(score_ps[u % 2][:, S * i:S * i + S], qst[p][r0:r0 + MROW, t, P * qt:P * qt + P],
                             kst[l][p][r0:r0 + MROW, t, :], start=True, stop=True)
                ins.then_inc(s_psum, 1)

            def st_tile(r, l, p, v):
                n = tile_no(r, l, p, v)
                if v == 0:
                    pe.wait_ge(m_stacked[p], 16 * 2 * (2 * r + l + 1))
                wait(pe, exp_done, n - 1)
                pair, kt = v // 2, v % 2
                if l == 1:
                    mm(st_ps[v % 2][:, :], identb[:, :], mbias[:, kt, :].unsqueeze(1).to_broadcast([P, 2, S]),
                       start=True, stop=False)
                for i in range(2):
                    r0, t = head_at(2 * pair + i)
                    ins = mm(st_ps[v % 2][:, S * i:S * i + S], kst[l][p][r0:r0 + KROWS, t, P * kt:P * kt + P],
                             qst[p][r0:r0 + KROWS, t, :], start=(l == 0), stop=(l == 0 or i == 1))
                ins.then_inc(st_psum, 1)

            def values(r, l, p, q):
                n = quad_no(r, l, p, q)
                pe.wait_ge(exp_done, 4 * n + 4)
                if p == 0 and q == 0:
                    if l == 0:
                        pe.wait_ge(k_split[1], LANES * (r + 1))
                    else:
                        pe.wait_ge(q_split, (2 * r + l) * LANES + LANES)
                wait(pe, norm_done, n - 1)
                for kt in range(2):
                    for j in range(4):
                        h = 4 * q + j
                        ins = mm(quad_ps[q % 2][32 * j:32 * j + 9, 0:S], vx[l][p][:, kt, h, :],
                                 probs[(4 * q + 2 * (j // 2) + kt) % 8][:, j % 2, :], start=(kt == 0), stop=(kt == 1),
                                 skip_group_check=True)
                ins.then_inc(pv_done, 1)

            def turn_out(r, l, p, q):
                n = quad_no(r, l, p, q)
                pe.wait_ge(o_evac, n + 1)
                for t in range(2):
                    ins = tr(quad_ps[q % 2][:, S + P * t:S + P * t + P], oT[q % 2][:, P * t:P * t + P], ident[:, :])
                ins.then_inc(t_psum, 1)

            def project(ps, lhs, w, brow, done):
                pe.wait_ge(rows_ld, 48)
                for t in range(2):
                    y = ps[:, S + P * t:S + P * t + P]
                    mm(y, ones3[:, :], rows3[:, brow, :], start=True, stop=False)
                    ins = mm(y, lhs[:, P * t:P * t + P], w, start=False, stop=True)
                ins.then_inc(done, 1)

            def keys(p, l):
                mm(work_ps[p][:, S:2 * S], wT[:, WK + l, :], ctxT[p], start=True, stop=True).then_inc(k_psum, 1)

            def body(r):
                for p in range(LANES):
                    wait(pe, z_ready, nth_ln(r - 1, NLN - 1, p) if not isinstance(r, int) or r > 0 else 0)
                    pe.wait_ge(ctx_ld[p], 16 * (r + 1))
                    for t in range(2):
                        ins = tr(work_ps[p][:, P * t:P * t + P], ctx_in[p][:, t, :], ident[:, :])
                    ins.then_inc(ctxT_psum, 1)
                def vals(p, l):
                    for t in range(2):
                        v = value_ps[p][:, P * t:P * t + P]
                        ins = mm(v, ctxT[p][:, P * t:P * t + P], wT[:, WV + l, :], start=True, stop=True)
                    ins.then_inc(v_psum, 1)

                for p in range(LANES):
                    pe.wait_ge(ctxT_ready, nth(r, p))
                    keys(p, 0)
                    vals(p, 0)
                for p in range(LANES):
                    pe.wait_ge(k_raw, nth(r, p))
                    zt(r, 0, p)
                for p in range(LANES):
                    pe.wait_ge(v_ready, r * 2 * LANES + p + 1)
                    vals(p, 1)
                    pe.wait_ge(zT_ready, nth_zt(r, 0, p))
                    mm(work_ps[p][:, S:2 * S], wT[:, SB, :], zT[p][:, :], start=True, stop=True).then_inc(w_psum, 1)
                for p in range(LANES):
                    pe.wait_ge(v_ready, r * 2 * LANES + LANES + p + 1)
                    for qt in range(2):
                        for kt in range(2):
                            ins = mm(value_ps[p][:, 144 * qt:144 * qt + 144].rearrange("p (h d) -> p h d", d=9),
                                     mbar[:, kt, P * qt:P * qt + P], vx[1][p][:, kt, :, 0:9], start=(kt == 0), stop=(kt == 1))
                    ins.then_inc(mv_psum, 1)
                for p in range(LANES):
                    pe.wait_ge(h_ready, nth(r, p))
                    for t in range(2):
                        ins = mm(work_ps[p][:, S + P * t:S + P * t + P], ha[p][:, 0, P * t:P * t + P], wT[:, SC, :],
                                 start=True, stop=True)
                    ins.then_inc(y_psum, 1)
                for l in range(2):
                    if l == 1:
                        ffn(r)
                        sign_attention(r)
                    for p in range(LANES):
                        zt(r, 1 + 3 * l, p)
                        pe.wait_ge(zT_ready, nth_zt(r, 1 + 3 * l, p))
                        mm(work_ps[p][:, S:2 * S], wT[:, WQ + l, :], zT[p][:, :], start=True, stop=True).then_inc(q_psum, 1)
                    for u in range(NTILE):
                        score_tile(r, l, 0, u)
                    maxima(r, l, 0)
                    if l == 0:
                        for p in range(LANES):
                            if p == 0:
                                pe.wait_ge(m_split, r * 2 * LANES + 1)
                            pe.wait_ge(q_split, r * 2 * LANES + p + 1)
                            keys(p, 1)
                    else:
                        for u in range(EARLY):
                            score_tile(r, l, 1, u)
                    for p in range(LANES):
                        attend(r, l, p)

            def nth_zt(r, i, p):
                return r * (NLN - 2) * LANES + (i - (1 if i > 3 else 0)) * LANES + p + 1

            def maxima(r, l, p):
                pe.wait_ge(s_maxed, tile_no(r, l, p, NTILE - 1) + 1)
                for t in range(2):
                    ins = tr(lane_ps[p % 2][0:H, P * t:P * t + P], mx[p][:, t, :], ident[:, :])
                ins.then_inc(mT_psum, 1)

            def turn_attention(r, l, p):
                pe.wait_ge(norm_done, quad_no(r, l, p, NQUAD - 1) + 1)
                for t in range(2):
                    ins = tr(out_ps(p)[:, P * t:P * t + P], att[p][:, t, :], ident[:, :])
                ins.then_inc(attT_psum, 1)

            def project_attention(r, l, p):
                pe.wait_ge(attT_ready, r * 2 * LANES + l * LANES + p + 1)
                project(out_ps(p), attT[p], wT[:, WO + l, :], l, y_psum)

            def attend(r, l, p):
                for q in range(NQUAD):
                    first, end = ahead(l, p, q)
                    u = first
                    for i in range(4):
                        st_tile(r, l, p, 4 * q + i)
                        while p + 1 < LANES and u < end - (3 - i) * (end - first) // 4:
                            score_tile(r, l, p + 1, u)
                            u += 1
                    if q == 2 and p + 1 < LANES:
                        maxima(r, l, p + 1)
                    if q == 0 and p > 0:
                        turn_attention(r, l, p - 1)
                    if q >= 1:
                        values(r, l, p, q - 1)
                    if q == 1 and p > 0:
                        project_attention(r, l, p - 1)
                    if q >= 2:
                        turn_out(r, l, p, q - 2)
                values(r, l, p, NQUAD - 1)
                turn_out(r, l, p, NQUAD - 2)
                turn_out(r, l, p, NQUAD - 1)
                if p == LANES - 1:
                    turn_attention(r, l, p)
                    project_attention(r, l, p)

            def ffn(r):
                pe.wait_ge(pool_const, 5)
                for p in range(LANES):
                    zt(r, 2, p)
                for p in range(LANES):
                    pe.wait_ge(zT_ready, nth_zt(r, 2, p))
                    project(work_ps[p], zT[p], w_hash[:, :], 2, lg_psum)
                for p in range(LANES):
                    pe.wait_ge(hot_ready, nth(r, p))
                    for t in range(2):
                        ins = tr(work_ps[p][0:E, P * t:P * t + P], hot[p][:, t, :], ident[:, :])
                    ins.then_inc(hotT_psum, 1)
                for p in range(LANES):
                    if p == 0:
                        spread(r, 0)
                    if p + 1 < LANES:
                        spread(r, p + 1)
                    pe.wait_ge(zm_ready, nth(r, p, E // 2))
                    for t in range(2):
                        y = work_ps[p][:, S + P * t:S + P * t + P]
                        mm(y, hotT[p][:, P * t:P * t + P], b_exp[:, :], start=True, stop=False)
                        for e in range(E):
                            ins = mm(y, zm[p % 2][:, e, P * t:P * t + P], w_exp[:, e, :], start=False, stop=(e == E - 1))
                    ins.then_inc(y_psum, 1)

            def spread(r, p):
                pe.wait_ge(hotT_ready, nth(r, p))
                for e in range(E):
                    if p > 0 and e % 2 == 0:
                        pe.wait_ge(zm_ready, nth(r, p - 1, E // 2, e // 2 + 1))
                    ins = mm(banks[e // 2][:, S * (e % 2):S * (e % 2) + S], selb[:, e, :], hotTb[p],
                             start=True, stop=True)
                    if e % 2 == 1:
                        ins.then_inc(bc_psum, 1)

            def sign_attention(r):
                for p in range(LANES):
                    zt(r, 3, p)
                for p in range(LANES):
                    pe.wait_ge(qb_ready, nth(r, p))
                    mm(work_ps[p][:, 0:S], kb[p][:, 0:P], qb[p][:, :], start=True, stop=True)
                    mm(work_ps[p][:, S:S + P], kb[p][:, P:S], qb[p][:, P:S], start=True, stop=True).then_inc(sg_psum, 1)
                for p in range(LANES):
                    pe.wait_ge(aw_ready, nth(r, p))
                    mm(work_ps[p][:, S:S + P], aw[p][:, 0:P], z[p][:, 0, :], start=True, stop=True)
                    mm(work_ps[p][:, S + P:2 * S], aw[p][:, P:S], z[p][:, 0, :], start=True, stop=False)
                    mm(work_ps[p][:, S + P:2 * S], aw[p][:, S:384], z[p][:, 1, :], start=False, stop=True).then_inc(y_psum, 1)

            rounds(pe, body)

            pe.wait_ge(z_ready, NLN * B)
            for j in range(4):
                for k in range(4):
                    ins = tr(banks[j][:, P * k:P * k + P], z6[:, 4 * j + k, :], ident[:, :])
                ins.then_inc(zT6_psum, 1)
            for c in range(NT):
                if c % 4 == 0:
                    pe.wait_ge(zT6_ready, c // 4 + 1)
                ins = mm(o_ps[:, 0:P], wg_pad[:, 120 - E * c:248 - E * c], zT6[:, c, :], start=(c == 0), stop=(c == NT - 1))
            ins.then_inc(gate_psum, 1)
            pe.wait_ge(cmax_ready, 1)
            tr(t_ps[0:1, 0:P], g[:, 0:1], ident[:, :]).then_inc(cmaxT_psum, 1)
            pe.wait_ge(m8_ready, 1)
            mm(t_ps[:, 128:129], m8[0:1, P:2 * P], ones[0:1, 0:1], start=True, stop=True)
            mm(t_ps[:, 136:136 + E], ones[0:1, :], m8[0:1, P:P + E], start=True, stop=True).then_inc(mbc_psum, 1)
            pe.wait_ge(ld_moe, 48)
            for step_ in range(1 + len(DIGITS)):
                n = 1 if step_ == 0 else 2 ** DIGITS[step_ - 1][1] - 1
                pe.wait_ge(cnt_ready, step_ + 1)
                mm(o_ps[:, 256:256 + n], blockb[:, :], cntb[:, 0:n], start=True, stop=True).then_inc(tot_psum, 1)
                if step_ < len(turn_moe):
                    if step_ >= 4:
                        pe.wait_ge(moe_wT, step_ - 3)
                    for k, src in enumerate(turn_moe[step_][0]):
                        ins = tr(turn_bank(step_)[:, P * k:P * k + P], src, ident[:, :])
                    ins.then_inc(moe_turned, 1)
            pe.wait_ge(ties_ready, 1)
            mm(t_ps[:, 144:145], blockf[:, :], g[:, 20:21], start=True, stop=True)
            mm(t_ps[:, 148:149], below[:, :], cum[:, P - 1:P], start=True, stop=True).then_inc(ties_psum, 1)
            pe.wait_ge(sel_ready, 1)
            mm(t_ps[:, 152:153], below[:, :], cum[:, P - 1:P], start=True, stop=True)
            mm(t_ps[:, 160:160 + E], ones[:, :], g[:, 24:24 + E], start=True, stop=True).then_inc(sel_psum, 1)
            pe.wait_ge(pos_ready, 1)
            tr(t_ps[:, 256:384], pos[:, :], ident[:, :]).then_inc(pos_psum, 1)
            pe.wait_ge(hot_tiles, 2)
            for e in range(E):
                for c in range(NT):
                    n = E * c + e
                    ins = mm(st_ps[0][0:16, 32 * e:32 * e + 32].rearrange("p (v k) -> p v k", v=2), hot_high[:, n, :],
                             place[:, :, n, :], start=(c == 0), stop=(c == NT - 1))
            ins.then_inc(id_psum, 1)

            def down(e):
                pe.wait_ge(hT_ready, e + 1)
                if e >= 2:
                    pe.wait_ge(y_ready, e - 1)
                for i in range(2):
                    for t in range(2):
                        ins = mm(quad_ps[e % 2][:, P * i:P * i + P], hT[e % 2][:, t, P * i:P * i + P],
                                 w2T[:, 2 * e + t, :], start=(t == 0), stop=(t == 1))
                ins.then_inc(down_psum, 1)

            pe.wait_ge(moe_wT, len(turn_moe))

            def turn_in(e):
                for i in range(2):
                    pe.wait_ge(gathered[2 * e + i], 16)
                if e >= 2:
                    pe.wait_ge(ws_added, e - 1)
                for i in range(2):
                    ins = tr(lane_ps[e % 2][:, P * i:P * i + P], xg[:, 2 * e + i, :], ident[:, :])
                ins.then_inc(xgT_psum, 1)

            def score_again(e):
                pe.wait_ge(xgT_ready, e + 1)
                for i in range(2):
                    ins = mm(lane_ps[e % 2][:, S + i:S + i + 1], xgT[:, 2 * e + i, :], wg_pad[:, 120 + e:121 + e],
                             start=True, stop=True)
                ins.then_inc(ws_psum, 1)

            turn_in(0)
            turn_in(1)
            for e in range(E):
                score_again(e)
                if e >= 2:
                    pe.wait_ge(hT_ready, e - 1)
                for t in range(2):
                    mm(score_ps[e % 2][:, S * t:S * t + S], w1T[:, 2 * e + t, :], xgT[:, 2 * e:2 * e + 2, :],
                       start=True, stop=True)
                    ins = mm(st_ps[e % 2][:, S * t:S * t + S], w3T[:, 2 * e + t, :], xgT[:, 2 * e:2 * e + 2, :],
                             start=True, stop=True)
                ins.then_inc(up_psum, 1)
                if e >= 1:
                    down(e - 1)
                if e + 2 < E:
                    turn_in(e + 2)
            down(E - 1)

        @block.vector
        def _(dve):
            n = [0]

            def link(ins):
                n[0] += 1
                ins.then_inc(dve_chain, 1)
                dve.wait_ge(dve_chain, n[0])

            ts, tt, stt = dve.tensor_scalar, dve.tensor_tensor, dve.scalar_tensor_tensor

            dve.wait_ge(ld_small, 16 * N_SMALL)
            ts(mask[:, :, :], maski, 0.0, None, ALU.not_equal).then_inc(dve_setup, 1)
            hdt = DT / 2
            v = [sv[:, i:i + 1] for i in range(32)]
            DR, NI, D2, T0, INV, AR, AI, CR, CI, Z0, M2, MH, RS, T1_, T2_, UR, UI, R, UR2, UI2 = range(20)
            dve.memset(v[MH], -0.5)
            ts(v[NI], cols[:, CAI:CAI + 1], hdt, None, ALU.mult)
            link(ts(v[DR], cols[:, CAR:CAR + 1], -hdt, 1.0, ALU.mult, ALU.add))
            link(tt(v[T0], v[NI], v[NI], ALU.mult))
            link(stt(v[D2], v[DR], v[DR], v[T0], ALU.mult, ALU.add))
            link(dve.reciprocal(v[INV], v[D2]))
            link(ts(v[T1_], cols[:, CAR:CAR + 1], hdt, 1.0, ALU.mult, ALU.add))
            link(stt(v[T2_], v[T1_], v[DR], v[T0], ALU.mult, ALU.subtract))
            link(tt(v[AR], v[T2_], v[INV], ALU.mult))
            link(stt(v[AI], v[NI], 2.0, v[INV], ALU.mult, ALU.mult))
            rdt = DT ** 0.5
            link(stt(v[CR], v[DR], rdt, v[INV], ALU.mult, ALU.mult))
            link(stt(v[CI], v[NI], rdt, v[INV], ALU.mult, ALU.mult))
            link(tt(v[T0], v[AI], v[AI], ALU.mult))
            link(stt(v[T1_], v[AR], v[AR], v[T0], ALU.mult, ALU.add))
            link(ts(v[Z0], v[T1_], 0.0, None, ALU.is_equal))
            tt(v[M2], v[T1_], v[Z0], ALU.add).then_inc(tab_sq, 1)
            dve.wait_ge(setup_ps, NTURN + 2)
            dve.wait_ge(pool_const, 2)
            link(tt(rows[:, 0:2, :], rows[:, 0:2, :], lane_ps[0][0:1, 0:2 * P].rearrange("p (a n) -> p a n", a=2), ALU.add))
            link(dve.tensor_copy(row_parts[:, 0, :, :], rows[:, :, :]))
            link(tt(row_rest, rows[:, :, :], row_parts[:, 0, :, :], ALU.subtract))
            link(dve.tensor_copy(row_parts[:, 1, :, :], row_rest))
            tt(row_parts[:, 2, :, :], row_rest, row_parts[:, 1, :, :], ALU.subtract).then_inc(rows_split, 1)
            dve.tensor_copy(wg_pad[:, 120:128], o_ps[:, 0:E])
            dve.tensor_copy(cols[:, 0:4], o_ps[:, E:E + 4])
            dve.tensor_copy(svb[:, :], o_ps[:, 256:384])
            ts(mbar[:, :, :], t_ps[:, :].rearrange("p (t q) -> p t q", t=2), -1.0, 1.0, ALU.mult, ALU.add)
            ts(mbias[:, :, :], t_ps[:, :].rearrange("p (t q) -> p t q", t=2), -1.0, -BIG, ALU.add, ALU.mult)
            dve.wait_ge(act_setup, 1)
            tt(sgn[:, 2:3], sgn[:, 0:1], sgn[:, 1:2], ALU.mult).then_inc(dve_setup, 1)
            dve.wait_ge(dve_setup, 2)

            def quad_no(r, l, p, q):
                return ((r * 2 + l) * LANES + p) * NQUAD + q

            def norm_stats(r, i, p):
                x = xs(r, p)
                wait(dve, z_ready, nth_ln(r, i, p) - LANES)
                dve.bn_stats(stat[p][:, 0, :], x[:, 0, :])
                link(dve.bn_stats(stat[p][:, 1, :], x[:, 1, :]))
                dve.bn_aggr(mv[p][:, 0, :], stat[p][:, 0, :])
                dve.bn_aggr(mv[p][:, 1, :], stat[p][:, 1, :]).then_inc(ln_stats, 1)

            def norm_apply(r, i, p):
                x = xs(r, p)
                dve.wait_ge(ln_rstd, nth_ln(r, i, p))
                for t in range(2):
                    ins = ts(z[p][:, t, :], x[:, t, :], mv[p][:, t, 0:1], inv_root[:, p, t:t + 1], ALU.subtract, ALU.mult)
                ins.then_inc(z_ready, 1)

            def residual(r, i, p, ps):
                dve.wait_ge(y_psum, y_no(r, i, p))
                link(tt(xs(r, p), xs(r, p), ps[:, S:2 * S].rearrange("p (t d) -> p t d", t=2), ALU.add))

            def split(p, src, bias, done):
                link(ts(parts[p][:, 0, :], src, bias, None, ALU.add))
                link(stt(rest[p][:, :], src, bias, parts[p][:, 0, :], ALU.add, ALU.subtract))
                link(dve.tensor_copy(parts[p][:, 1, :], rest[p][:, :]))
                tt(parts[p][:, 2, :], rest[p][:, :], parts[p][:, 1, :], ALU.subtract).then_inc(done, 1)

            def maximum(r, l, p, u):
                k = tile_no(r, l, p, u)
                qt, pair = u // 8, u % 8
                dve.wait_ge(s_psum, k + 1)
                s2 = score_ps[u % 2][:, :].rearrange("p (i k) -> p i k", i=2)
                if l == 0:
                    dve.tensor_reduce(mx[p][:, qt, 2 * pair:2 * pair + 2], s2, AX.X, ALU.max).then_inc(s_maxed, 1)
                else:
                    for i in range(2):
                        h = 2 * pair + i
                        ins = dve.tensor_tensor_reduce(junk[p][u % 2][:, i, :], s2[:, i, :], mask[:, qt, :], 1.0, -3.0e38,
                                                       ALU.mult, ALU.max, mx[p][:, qt, h:h + 1])
                    ins.then_inc(s_maxed, 1)

            def split_max(r, l, p):
                if l == 1:
                    dve.wait_ge(s_maxed, tile_no(r, l, p, NTILE - 1) + 1)
                    ts(emx[p][:, :, :], mx[p][:, :, :], -SCALE, -1.0e-9, ALU.mult, ALU.min).then_inc(m_neg, 1)
                dve.wait_ge(mT_psum, r * 2 * LANES + l * LANES + p + 1)
                src = lane_ps[p % 2][0:H, 0:S]
                link(ts(mparts[p][:, 0, :], src, -1.0, None, ALU.mult))
                link(stt(mrest[p][:, :], src, -1.0, mparts[p][:, 0, :], ALU.mult, ALU.subtract))
                link(dve.tensor_copy(mparts[p][:, 1, :], mrest[p][:, :]))
                tt(mparts[p][:, 2, :], mrest[p][:, :], mparts[p][:, 1, :], ALU.subtract).then_inc(m_split, 1)

            def normalise(r, l, p, q):
                k = quad_no(r, l, p, q)
                dve.wait_ge(t_psum, k + 1)
                wait(dve, norm_done, k - 1)
                onum, orec = onums[q % 2], orecs[q % 2]
                t4 = quad_ps[q % 2][:, S:2 * S].rearrange("p (t j c) -> p t j c", t=2, j=4)
                num, den = t4[:, :, :, 0:HD], t4[:, :, :, HD]
                if l == 1:
                    dve.wait_ge(emx_ready, nth(r, p))
                    link(tt(onum[:, :, :, :], mvx[p][:, :, 4 * q:4 * q + 4, :],
                            emx[p][:, :, 4 * q:4 * q + 4].unsqueeze(3).to_broadcast([P, 2, 4, 9]), ALU.mult))
                    link(tt(onum[:, :, :, :], t4[:, :, :, 0:9], onum[:, :, :, :], ALU.add))
                    num, den = onum[:, :, :, 0:HD], onum[:, :, :, HD]
                link(dve.reciprocal(orec[:, :, :], den))
                tt(att[p][:, :, 32 * q:32 * q + 32].rearrange("p t (j d) -> p t j d", d=HD), num,
                   orec[:, :, :].unsqueeze(3).to_broadcast([P, 2, 4, HD]), ALU.mult).then_inc(norm_done, 1)

            def attention(r, l):
                def left(p):
                    dve.wait_ge(q_high, (2 * r + l) * LANES + p + 1)
                    stt(rest[p][:, :], work_ps[p][:, S:2 * S], cols[:, CQ + l:CQ + l + 1], parts[p][:, 0, :],
                        ALU.add, ALU.subtract).then_inc(q_rest, 1)

                def low(p):
                    dve.wait_ge(q_mid, (2 * r + l) * LANES + p + 1)
                    tt(parts[p][:, 2, :], rest[p][:, :], parts[p][:, 1, :], ALU.subtract).then_inc(q_split, 1)

                left(0)
                low(0)
                left(1)
                low(1)
                left(2)
                left(3)
                low(2)
                low(3)
                for u in range(NTILE):
                    maximum(r, l, 0, u)
                split_max(r, l, 0)
                if l == 0:
                    for p in range(LANES):
                        dve.wait_ge(k_psum, r * 2 * LANES + LANES + p + 1)
                        dve.wait_ge(q_stored[p], 16 * 3 * (2 * r + 1))
                        split(p, work_ps[p][:, S:2 * S], cols[:, CK + 1:CK + 2], k_split[1])
                else:
                    for u in range(EARLY):
                        maximum(r, l, 1, u)
                for p in range(LANES - 1):
                    if p > 0:
                        normalise(r, l, p - 1, 2)
                        normalise(r, l, p - 1, 3)
                    for q in range(NQUAD):
                        if q == 2 and p > 0:
                            residual(r, 1 + 3 * l, p - 1, out_ps(p - 1))
                        for u in range(*ahead(l, p, q)):
                            maximum(r, l, p + 1, u)
                        if q == 2:
                            split_max(r, l, p + 1)
                        if q >= 2:
                            normalise(r, l, p, q - 2)
                last, ln = LANES - 1, 2 + 3 * l
                normalise(r, l, last - 1, 2)
                normalise(r, l, last - 1, 3)
                residual(r, 1 + 3 * l, last - 1, out_ps(last - 1))
                normalise(r, l, last, 0)
                norm_stats(r, ln, 0)
                norm_stats(r, ln, 1)
                normalise(r, l, last, 1)
                norm_stats(r, ln, 2)
                normalise(r, l, last, 2)
                normalise(r, l, last, 3)
                residual(r, 1 + 3 * l, last, out_ps(last))
                norm_stats(r, ln, last)

            def hashed_ffn(r):
                dve.wait_ge(pool_const, 5)
                for p in range(LANES):
                    lg = lexp[p]
                    dve.wait_ge(lg_copied, nth(r, p))
                    link(dve.tensor_reduce(lmax[p][:, 0:2], lg[:, :, :], AX.X, ALU.max))
                    ts(lmax[p][:, 2:4], lmax[p][:, 0:2], -1.0, None, ALU.mult).then_inc(lg_max, 1)
                    for t in range(2):
                        ins = stt(rest[p][:, P * t:P * t + P], lg[:, t, :], lmax[p][:, t:t + 1], iota_rev[:, :],
                                  ALU.is_ge, ALU.mult)
                    link(ins)
                    link(dve.tensor_reduce(stat[p][:, 0, 0:2], rest[p][:, :].rearrange("p (t d) -> p t d", t=2),
                                           AX.X, ALU.max))
                    for t in range(2):
                        ins = ts(ytmp[p][:, P * t:P * t + P], iota_rev[:, :], stat[p][:, 0, t:t + 1], None, ALU.is_equal)
                    link(ins)
                    dve.tensor_reduce(hot[p][:, :, :], ytmp[p][:, :].rearrange("p (t g e) -> p t e g", t=2, e=E),
                                      AX.X, ALU.max).then_inc(hot_ready, 1)
                def select(p):
                    dve.wait_ge(lg_exp, nth(r, p))
                    dve.reciprocal(lmax[p][:, 6:8], lmax[p][:, 4:6])
                    for j in range(E // 2):
                        dve.wait_ge(bc_psum, nth(r, p, E // 2, j + 1))
                        if j == 0 and p >= 2:
                            dve.wait_ge(y_psum, y_no(r, 2, p - 2))
                        tt(zm[p % 2][:, 2 * j:2 * j + 2, :], zT[p][:, :].unsqueeze(1).to_broadcast([P, 2, S]),
                           banks[j][:, :].rearrange("p (i k) -> p i k", i=2), ALU.mult).then_inc(zm_ready, 1)

                def finish(p):
                    dve.wait_ge(y_psum, y_no(r, 2, p))
                    for t in range(2):
                        ins = ts(ytmp[p][:, P * t:P * t + P], work_ps[p][:, S + P * t:S + P * t + P], 0.0,
                                 lmax[p][:, 6 + t:7 + t], ALU.max, ALU.mult)
                    link(ins)
                    link(tt(xs(r, p), xs(r, p), ytmp[p][:, :].rearrange("p (t d) -> p t d", t=2), ALU.add))
                    norm_stats(r, 3, p)

                for p in range(LANES):
                    select(p)
                    if p > 0:
                        finish(p - 1)
                finish(LANES - 1)

            def sign_attention(r):
                for p in range(LANES):
                    norm_apply(r, 3, p)
                for p in range(LANES):
                    dve.wait_ge(sign_ready, nth(r, p))
                    ts(qb[p][:, :], kb[p][:, :], sgn[:, 2:3], None, ALU.mult).then_inc(qb_ready, 1)
                for p in range(LANES):
                    dve.wait_ge(tanh_done, nth(r, p))
                    stt(aw[p][:, :], th[p][:, :], 1.0, halfmask[:, :], ALU.add, ALU.mult).then_inc(aw_ready, 1)
                for p in range(LANES):
                    dve.wait_ge(y_psum, y_no(r, 3, p))
                    link(tt(ytmp[p][:, :].rearrange("p (t d) -> p t d", t=2),
                            work_ps[p][:, S:2 * S].rearrange("p (t d) -> p t d", t=2),
                            svb[:, :].unsqueeze(1).to_broadcast([P, 2, P]), ALU.mult))
                    link(tt(xs(r, p), xs(r, p), ytmp[p][:, :].rearrange("p (t d) -> p t d", t=2), ALU.add))
                    norm_stats(r, 4, p)

            dve.wait_ge(rows_ld, 48)

            def body(r):
                for p in range(LANES if r > 0 else 0):
                    norm_stats(r, 0, p)
                def scan(p):
                    dve.wait_ge(w_psum, nth(r, p))
                    tt(wa[p][:, 0, :], work_ps[p][:, S:2 * S], er[:, :], ALU.mult)
                    link(tt(wa[p][:, 1, :], work_ps[p][:, S:2 * S], esin[:, :], ALU.mult))
                    for i in range(2):
                        ins = dve.tensor_tensor_scan(ga[p][:, i, :], rdec[:, :], wa[p][:, i, :], 0.0, ALU.mult, ALU.add)
                    ins.then_inc(scan_done, 1)
                    dve.wait_ge(scan_done, nth(r, p))
                    tt(ha[p][:, 0, :], ga[p][:, 0, :], t1[:, :], ALU.mult)
                    link(tt(ha[p][:, 1, :], ga[p][:, 1, :], t2[:, :], ALU.mult))
                    tt(ha[p][:, 0, :], ha[p][:, 0, :], ha[p][:, 1, :], ALU.add).then_inc(h_ready, 1)

                def finish_ssm(p):
                    residual(r, 0, p, work_ps[p])
                    norm_stats(r, 1, p)

                for p in range(LANES - 1):
                    scan(p)
                finish_ssm(0)
                scan(LANES - 1)
                for p in range(1, LANES):
                    finish_ssm(p)
                attention(r, 0)
                hashed_ffn(r)
                sign_attention(r)
                attention(r, 1)

            dve.wait_ge(ld_x, 16)
            for p in range(LANES):
                norm_stats(0, 0, p)
            dve.wait_ge(tab_pow, 1)
            link(tt(v[T0], v[RS], v[RS], ALU.mult))
            link(tt(v[T0], v[T0], v[M2], ALU.mult))
            link(ts(v[T0], v[T0], -0.5, 1.5, ALU.mult, ALU.add))
            link(tt(v[RS], v[RS], v[T0], ALU.mult))
            link(stt(v[UR], v[AR], v[RS], v[Z0], ALU.mult, ALU.add))
            link(tt(v[UI], v[AI], v[RS], ALU.mult))
            link(tt(v[T0], v[AI], v[UI], ALU.mult))
            link(stt(v[R], v[AR], v[UR], v[T0], ALU.mult, ALU.add))
            link(ts(rdec[:, :], rdec[:, :], v[R], None, ALU.mult))
            dve.memset(er[:, 0:1], 1.0)
            link(dve.memset(ei[:, 0:1], 0.0))
            w, (ur, ui), (ur2, ui2) = 1, (v[UR], v[UI]), (v[UR2], v[UI2])
            while w < S:
                ts(stmp[:, 0:w], ei[:, 0:w], ui, None, ALU.mult)
                if 2 * w < S:
                    tt(v[T0], ui, ui, ALU.mult)
                    stt(ui2, ur, 2.0, ui, ALU.mult, ALU.mult)
                link(ts(stmp[:, P:P + w], er[:, 0:w], ui, None, ALU.mult))
                if 2 * w < S:
                    stt(ur2, ur, ur, v[T0], ALU.mult, ALU.subtract)
                stt(er[:, w:2 * w], er[:, 0:w], ur, stmp[:, 0:w], ALU.mult, ALU.subtract)
                link(stt(ei[:, w:2 * w], ei[:, 0:w], ur, stmp[:, P:P + w], ALU.mult, ALU.add))
                w, (ur, ui), (ur2, ui2) = 2 * w, (ur2, ui2), (ur, ui)
            ts(stmp, ei[:, :], v[CI], None, ALU.mult)
            link(ts(t2[:, :], er[:, :], v[CI], -1.0, ALU.mult, ALU.mult))
            ts(esin[:, :], ei[:, :], -1.0, None, ALU.mult)
            link(stt(t1[:, :], er[:, :], v[CR], stmp, ALU.mult, ALU.subtract))
            link(stt(t2[:, :], esin[:, :], v[CR], t2[:, :], ALU.mult, ALU.add))

            rounds(dve, body)

            for k, (b, _) in enumerate(DIGITS):
                ts(shifted[:, k, :], digits[:, :], b, None, ALU.logical_shift_left)
            dve.wait_ge(gate_psum, 1)
            link(dve.tensor_copy(sc[:, :], o_ps[:, 0:P]))
            dve.tensor_reduce(g[:, 0:1], sc[:, :], AX.X, ALU.max).then_inc(cmax_ready, 1)
            dve.wait_ge(cmaxT_psum, 1)
            link(dve.tensor_reduce(m8[0:1, 0:E], t_ps[0:1, 0:P].rearrange("p (c e) -> p e c", e=E), AX.X, ALU.max))
            ts(m8[0:1, P:2 * P].rearrange("p (c e) -> p c e", e=E), m8[0:1, 0:E].unsqueeze(1).to_broadcast([1, NT, E]),
               -1.0, None, ALU.mult).then_inc(m8_ready, 1)
            dve.wait_ge(mbc_psum, 1)
            dve.tensor_copy(nm8[:, :], t_ps[:, 136:136 + E])
            dve.tensor_copy(g[:, 2:3], t_ps[:, 128:129]).then_inc(nm_ready, 1)
            room = float(CAP) - 0.5
            ts(eq[:, :], sc[:, :], 0.0, None, ALU.is_ge, ALU.add, accum_out=cntb[:, 0:1]).then_inc(cnt_ready, 1)
            dve.wait_ge(tot_psum, 1)
            link(ts(V, o_ps[:, 256:257], room, -1.0, ALU.is_lt, ALU.mult))
            width = 2 ** DIGITS[0][1] - 1
            link(tt(F[:, 0:width], shifted[:, 0, 0:width], V.to_broadcast([P, width]), ALU.bitwise_xor))
            for k, (b, bits) in enumerate(DIGITS):
                width = 2 ** bits - 1
                for j in range(width):
                    ins = ts(cand[j], sc[:, :], F[:, j:j + 1].bitcast(F32), None, ALU.is_ge, ALU.add,
                             accum_out=cntb[:, j:j + 1])
                ins.then_inc(cnt_ready, 1)
                if k + 1 < len(DIGITS):
                    after = 2 ** DIGITS[k + 1][1] - 1
                    tt(NF[:, 0:after], shifted[:, k + 1, 0:after], V.to_broadcast([P, after]), ALU.bitwise_xor)
                dve.wait_ge(tot_psum, k + 2)
                link(ts(g[:, 44:44 + width], o_ps[:, 256:256 + width], room, None, ALU.is_ge, ALU.add, accum_out=g[:, 47:48]))
                link(ts(DB, g[:, 47:48], float(2 ** b), None, ALU.mult))
                if k + 1 < len(DIGITS):
                    tt(V, V, DB, ALU.bitwise_xor)
                    link(tt(F[:, 0:after], NF[:, 0:after], DB.to_broadcast([P, after]), ALU.bitwise_xor))
                else:
                    link(tt(V, V, DB, ALU.bitwise_xor))
            thr = V.bitcast(F32)
            ts(sel[:, :], sc[:, :], thr, None, ALU.is_gt, ALU.add, accum_out=g[:, 20:21])
            link(ts(eq[:, :], sc[:, :], thr, None, ALU.is_equal))
            dve.tensor_tensor_scan(cum[:, :], ones[:, :], eq[:, :], 0.0, ALU.mult, ALU.add).then_inc(ties_ready, 1)
            dve.wait_ge(ties_psum, 1)
            ts(g[:, 4:5], t_ps[:, 144:145], -1.0, float(CAP), ALU.mult, ALU.add)
            link(dve.tensor_copy(g[:, 5:6], t_ps[:, 148:149]))
            link(ts(cum[:, :], cum[:, :], g[:, 5:6], g[:, 4:5], ALU.add, ALU.is_le))
            link(tt(eq[:, :], eq[:, :], cum[:, :], ALU.mult))
            link(tt(sel[:, :], sel[:, :], eq[:, :], ALU.add))
            dve.wait_ge(gate_exp, 1)
            dve.tensor_tensor_scan(cum[:, :], ones[:, :], sel[:, :], 0.0, ALU.mult, ALU.add)
            link(dve.tensor_tensor_reduce(eq[:, :], ex[:, :], sel[:, :], 1.0, 0.0, ALU.mult, ALU.add, g[:, 22:23]))
            ts(g[:, 24:24 + E], emask[:, :], g[:, 22:23], None, ALU.mult).then_inc(sel_ready, 1)
            dve.wait_ge(sel_psum, 1)
            dve.reciprocal(rs8[:, :], t_ps[:, 160:160 + E])
            link(dve.tensor_copy(g[:, 6:7], t_ps[:, 152:153]))
            link(stt(pos[:, :], cum[:, :], g[:, 6:7], sel[:, :], ALU.add, ALU.mult))
            ts(pos[:, :], pos[:, :], -1.0, None, ALU.add).then_inc(pos_ready, 1)
            dve.wait_ge(pos_psum, 1)
            link(dve.tensor_copy(slot_i[:, :], t_ps[:, 256:384]))
            ts(high_i[:, :], slot_i[:, :], 4, None, ALU.arith_shift_right)
            link(ts(slot_i[:, :], slot_i[:, :], 15, None, ALU.bitwise_and))
            dve.tensor_copy(high_f, high_i[:, :])
            link(dve.tensor_copy(low_f, slot_i[:, :]))
            every = iota16[:, :].unsqueeze(1).to_broadcast([P, P, 16])
            tt(hot_low, low_f.unsqueeze(2).to_broadcast([P, P, 16]), every, ALU.is_equal).then_inc(hot_low_ready, 1)
            tt(hot_high, high_f.unsqueeze(2).to_broadcast([P, P, 16]), every, ALU.is_equal)
            dve.wait_ge(hot_low_ready, 1)
            ts(place[:, 0, :, :], hot_low, tokp[:, 0:1], None, ALU.mult).then_inc(hot_tiles, 1)
            dve.wait_ge(id_psum, 1)
            link(dve.tensor_copy(idpair[:, :], st_ps[0][0:16, 0:32 * E]))
            pair = idpair[:, :].rearrange("p (e v k) -> p e v k", v=2, k=16)
            stt(idrows[:, :, :], pair[:, :, 1, :], float(P), pair[:, :, 0, :], ALU.mult, ALU.add).then_inc(idrows_ready, 1)

            def weigh(e):
                dve.wait_ge(down_psum, e + 1)
                dve.wait_ge(wslot_ready, e + 1)
                if e >= 2:
                    dve.wait_ge(scattered[0], 16 * (e - 1))
                    dve.wait_ge(scattered[1], 16 * (e - 1))
                for i in range(2):
                    ins = ts(ysc[e % 2][:, i, :], quad_ps[e % 2][:, P * i:P * i + P],
                             wslot[:, 2 * e + i:2 * e + i + 1], rs8[:, e:e + 1], ALU.mult, ALU.mult)
                ins.then_inc(y_ready, 1)

            for e in range(E):
                dve.wait_ge(ws_psum, e + 1)
                ts(wlog[:, 2 * e:2 * e + 2], lane_ps[e % 2][:, S:S + 2], nm8[:, e:e + 1], None, ALU.add).then_inc(ws_added, 1)
                dve.wait_ge(tanh1_done, e + 1)
                if e >= 2:
                    dve.wait_ge(down_psum, e - 1)
                link(stt(act1[e % 2], act1[e % 2], 1.0, score_ps[e % 2][:, :].rearrange("p (t c) -> p t c", t=2),
                         ALU.add, ALU.mult))
                stt(hT[e % 2], act1[e % 2], 0.5, st_ps[e % 2][:, :].rearrange("p (t c) -> p t c", t=2),
                    ALU.mult, ALU.mult).then_inc(hT_ready, 1)
                if e >= 1:
                    weigh(e - 1)
            weigh(E - 1)


_INS = ["x", "ctx_1024", "mask_SxS2_ik0", "L0_attn_A_real", "L0_attn_A_imag", "L0_attn_B", "L0_attn_C",
        "L0_xattn_Wq", "L0_xattn_bq", "L0_xattn_Wk", "L0_xattn_bk", "L0_xattn_Wv", "L0_xattn_bv", "L0_xattn_Wo",
        "L0_xattn_bo", "L0_ffn_Wg", "L0_ffn_bg", "L0_ffn_We", "L0_ffn_be", "L1_attn_bv_q", "L1_attn_bv_k",
        "L1_attn_bv_v", "L1_xattn_Wq", "L1_xattn_bq", "L1_xattn_Wk", "L1_xattn_bk", "L1_xattn_Wv", "L1_xattn_bv",
        "L1_xattn_Wo", "L1_xattn_bo", "L1_ffn_Wg", "L1_ffn_W1", "L1_ffn_W2", "L1_ffn_W3"]


def kernel(**inputs):
    import numpy as _np
    import concourse.bacc as _bacc
    from concourse import mybir as _mybir
    from concourse.bass_utils import run_bass_kernel_spmd as _run

    nc = _bacc.Bacc("TRN2", target_bir_lowering=False, num_devices=1)
    arrays, aps = {}, {}
    for name in _INS:
        arr = _np.ascontiguousarray(inputs[name])
        arrays[f"in_{name}"] = arr
        aps[name] = nc.dram_tensor(f"in_{name}", arr.shape, _mybir.dt.from_np(arr.dtype), kind="ExternalInput").ap()
    out = nc.dram_tensor("out", (B, S, D), F32, kind="ExternalOutput").ap()
    decoder(nc, aps, out)
    r = _run(nc, [arrays], core_ids=[0])
    return r.results[0]["out"]
```
